# Optimizing a Trainium2 kernel written in Bass

```python
import numpy as np
import jax
import jax.numpy as jnp

def _softmax(x, axis=-1):
    return jax.nn.softmax(x, axis=axis)

def _gelu(x):
    return jax.nn.gelu(x, approximate=True)

def _silu(x):
    return jax.nn.silu(x)

def _sigmoid(x):
    return jax.nn.sigmoid(x)

def _layernorm(x, axis=-1, eps=1e-05):
    m = jnp.mean(x, axis=axis, keepdims=True)
    v = jnp.var(x, axis=axis, keepdims=True)
    return (x - m) / jnp.sqrt(v + eps)

def _scatter_add(tgt, idx, src, axis=0):
    return tgt.at[idx].add(src)

def _segment_sum(src, seg, n):
    return jax.ops.segment_sum(src, seg, n)
kernel_name = 'mk_adaln_d1_jaxref_r8_4649f5'

def setup_inputs(seed: int=0):
    np.random.seed(seed)
    _w = jnp.asarray

    def _L0_attn_setup():
        import math
        import jax, jax.numpy as jnp
        import numpy as np
        HIDDEN = 256
        NUM_HEADS = 32
        HEAD_DIM = HIDDEN // NUM_HEADS
        NUM_BLOCKS = 4
        INTER = 2 * HIDDEN
        EPS = 1e-05
        ROPE_THETA = 10000.0

        def _rmsnorm(x, w):
            var = jnp.mean(x * x, axis=-1, keepdims=True)
            return x * jax.lax.rsqrt(var + EPS) * w

        def _rope_cache(seq_len, dim, theta, scale):
            inv_freq = 1.0 / theta ** (jnp.arange(0, dim, 2, dtype=jnp.float32) / dim)
            t = jnp.arange(seq_len, dtype=jnp.float32) / scale
            freqs = jnp.outer(t, inv_freq)
            emb = jnp.concatenate([freqs, freqs], axis=-1)
            return (jnp.cos(emb), jnp.sin(emb))

        def _apply_rope(x, cos, sin):
            d2 = x.shape[-1] // 2
            x1, x2 = (x[..., :d2], x[..., d2:])
            rot = jnp.concatenate([-x2, x1], axis=-1)
            return x * cos[None, None] + rot * sin[None, None]
        key = jax.random.key(seed)
        ks = jax.random.split(key, 6)
        B, S = (2, 256)
        sc = 0.02
        return {'x': jax.random.normal(ks[0], (B, S, HIDDEN), jnp.float32), 'attn_norm_w': jnp.ones((HIDDEN,), jnp.float32), 'ffn_norm_w': jnp.ones((HIDDEN,), jnp.float32), 'w_qkv': jax.random.normal(ks[1], (3 * HIDDEN, HIDDEN), jnp.float32) * sc, 'w_o': jax.random.normal(ks[2], (HIDDEN, HIDDEN), jnp.float32) * sc, 'w_up': jax.random.normal(ks[3], (2 * INTER, HIDDEN), jnp.float32) * sc, 'w_down': jax.random.normal(ks[4], (HIDDEN, INTER), jnp.float32) * sc}
    _L0_attn_in = _L0_attn_setup()

    def _L0_ffn_setup():
        import jax, jax.numpy as jnp
        import numpy as np
        B, S, D = (4, 256, 256)
        DFF = 704
        E, K, R = (8, 2, 16)
        SCALING = 32.0 / 16.0
        key = jax.random.key(seed)
        ks = jax.random.split(key, 12)
        s = lambda k, shape, scale: jax.random.normal(k, shape, dtype=jnp.float32) * scale
        return {'x': s(ks[0], (B, S, D), 1.0), 'Wg': s(ks[1], (DFF, D), 0.02), 'Wu': s(ks[2], (DFF, D), 0.02), 'Wd': s(ks[3], (D, DFF), 0.02), 'Wr': s(ks[4], (E, D), 0.02), 'Ag': s(ks[5], (E, R, D), 0.02), 'Bg': s(ks[6], (E, DFF, R), 0.02), 'Au': s(ks[7], (E, R, D), 0.02), 'Bu': s(ks[8], (E, DFF, R), 0.02), 'Ad': s(ks[9], (E, R, DFF), 0.02), 'Bd': s(ks[10], (E, D, R), 0.02)}
    _L0_ffn_in = _L0_ffn_setup()
    _L0_c = _w((lambda *s: np.random.randn(*s).astype(np.float32) * 0.05)(4, 256))
    _L0_wmod = _w((lambda *s: np.random.randn(*s).astype(np.float32) * 0.05)(256, 6 * 256) * 256 ** (-0.5))
    _d = {'L0_attn_x': _L0_attn_in['x'], 'L0_attn_attn_norm_w': _L0_attn_in['attn_norm_w'], 'L0_attn_ffn_norm_w': _L0_attn_in['ffn_norm_w'], 'L0_attn_w_qkv': _L0_attn_in['w_qkv'], 'L0_attn_w_o': _L0_attn_in['w_o'], 'L0_attn_w_up': _L0_attn_in['w_up'], 'L0_attn_w_down': _L0_attn_in['w_down'], 'L0_ffn_Wg': _L0_ffn_in['Wg'], 'L0_ffn_Wu': _L0_ffn_in['Wu'], 'L0_ffn_Wd': _L0_ffn_in['Wd'], 'L0_ffn_Wr': _L0_ffn_in['Wr'], 'L0_ffn_Ag': _L0_ffn_in['Ag'], 'L0_ffn_Bg': _L0_ffn_in['Bg'], 'L0_ffn_Au': _L0_ffn_in['Au'], 'L0_ffn_Bu': _L0_ffn_in['Bu'], 'L0_ffn_Ad': _L0_ffn_in['Ad'], 'L0_ffn_Bd': _L0_ffn_in['Bd'], 'L0_c': _L0_c, 'L0_wmod': _L0_wmod}
    _x0 = _d['L0_attn_x']
    _d['L0_attn_x'] = jax.random.normal(jax.random.fold_in(jax.random.key(seed), 1), (4, 512, 256), dtype=_x0.dtype)
    del _x0
    return _d

def reference(L0_attn_x, L0_attn_attn_norm_w, L0_attn_ffn_norm_w, L0_attn_w_qkv, L0_attn_w_o, L0_attn_w_up, L0_attn_w_down, L0_ffn_Wg, L0_ffn_Wu, L0_ffn_Wd, L0_ffn_Wr, L0_ffn_Ag, L0_ffn_Bg, L0_ffn_Au, L0_ffn_Bu, L0_ffn_Ad, L0_ffn_Bd, L0_c, L0_wmod):

    def _L0_attn_ref(x, attn_norm_w, ffn_norm_w, w_qkv, w_o, w_up, w_down):
        import math
        import jax, jax.numpy as jnp
        import numpy as np
        HIDDEN = 256
        NUM_HEADS = 32
        HEAD_DIM = HIDDEN // NUM_HEADS
        NUM_BLOCKS = 4
        INTER = 2 * HIDDEN
        EPS = 1e-05
        ROPE_THETA = 10000.0

        def _rmsnorm(x, w):
            var = jnp.mean(x * x, axis=-1, keepdims=True)
            return x * jax.lax.rsqrt(var + EPS) * w

        def _rope_cache(seq_len, dim, theta, scale):
            inv_freq = 1.0 / theta ** (jnp.arange(0, dim, 2, dtype=jnp.float32) / dim)
            t = jnp.arange(seq_len, dtype=jnp.float32) / scale
            freqs = jnp.outer(t, inv_freq)
            emb = jnp.concatenate([freqs, freqs], axis=-1)
            return (jnp.cos(emb), jnp.sin(emb))

        def _apply_rope(x, cos, sin):
            d2 = x.shape[-1] // 2
            x1, x2 = (x[..., :d2], x[..., d2:])
            rot = jnp.concatenate([-x2, x1], axis=-1)
            return x * cos[None, None] + rot * sin[None, None]
        B, S, _ = x.shape
        residual = x
        h = _rmsnorm(x, attn_norm_w)
        qkv = jnp.einsum('bsh,oh->bso', h, w_qkv)
        qkv = qkv.reshape(B, S, 3, NUM_HEADS, HEAD_DIM)
        q, k, v = (qkv[:, :, 0], qkv[:, :, 1], qkv[:, :, 2])
        q = q.transpose(0, 2, 1, 3)
        k = k.transpose(0, 2, 1, 3)
        v = v.transpose(0, 2, 1, 3)
        cos, sin = _rope_cache(S, HEAD_DIM, ROPE_THETA, 1.0)
        q = _apply_rope(q, cos, sin)
        k = _apply_rope(k, cos, sin)
        scale = 1.0 / math.sqrt(HEAD_DIM)
        attn = jnp.einsum('bhqd,bhkd->bhqk', q, k) * scale
        num_blocks = max(1, min(NUM_BLOCKS, S))
        blk = math.ceil(S / num_blocks)
        pos = jnp.arange(S)
        block_ids = pos // blk
        block_mask = block_ids[:, None] != block_ids[None, :]
        causal_mask = pos[:, None] < pos[None, :]
        invalid = causal_mask | block_mask
        mask_floor = jnp.finfo(attn.dtype).min
        attn = jnp.where(invalid[None, None], mask_floor, attn)
        attn = jax.nn.softmax(attn, axis=-1)
        context = jnp.einsum('bhqk,bhkd->bhqd', attn, v)
        context = context.transpose(0, 2, 1, 3).reshape(B, S, HIDDEN)
        x = residual + jnp.einsum('bsh,oh->bso', context, w_o)
        residual = x
        h = _rmsnorm(x, ffn_norm_w)
        up = jnp.einsum('bsh,oh->bso', h, w_up)
        gate, value = (up[..., :INTER], up[..., INTER:])
        down = jnp.einsum('bsi,oi->bso', jax.nn.silu(gate) * value, w_down)
        return residual + down

    def _L0_ffn_ref(x, Wg, Wu, Wd, Wr, Ag, Bg, Au, Bu, Ad, Bd):
        import jax, jax.numpy as jnp
        import numpy as np
        B, S, D = (4, 256, 256)
        DFF = 704
        E, K, R = (8, 2, 16)
        SCALING = 32.0 / 16.0
        b, s, d = x.shape
        xf = x.reshape(-1, d)
        gate_base = xf @ Wg.T
        up_base = xf @ Wu.T
        base_out = jax.nn.silu(gate_base) * up_base @ Wd.T
        router_logits = xf @ Wr.T
        probs = jax.nn.softmax(router_logits.astype(jnp.float32), axis=-1)
        topw, topi = jax.lax.top_k(probs, K)
        topw = topw.astype(x.dtype)
        expert_w = jnp.sum(jax.nn.one_hot(topi, E, dtype=x.dtype) * topw[..., None], axis=1)

        def expert_step(acc, params):
            Ag_e, Bg_e, Au_e, Bu_e, Ad_e, Bd_e, we = params
            g_lora = xf @ Ag_e.T @ Bg_e.T * SCALING
            u_lora = xf @ Au_e.T @ Bu_e.T * SCALING
            h = jax.nn.silu(gate_base + g_lora) * (up_base + u_lora)
            d_delta = h @ Ad_e.T @ Bd_e.T * SCALING
            return (acc + d_delta * we[:, None], None)
        acc0 = jnp.zeros_like(base_out)
        acc, _ = jax.lax.scan(expert_step, acc0, (Ag, Bg, Au, Bu, Ad, Bd, expert_w.T))
        return (base_out + acc).reshape(b, s, d)
    x = L0_attn_x
    mod = (_silu(L0_c) @ L0_wmod).reshape(L0_c.shape[0], 6, 1, -1)
    sa, ca, ga, sb, cb, gb = (mod[:, 0], mod[:, 1], mod[:, 2], mod[:, 3], mod[:, 4], mod[:, 5])
    ga = (2 * (ga >= 0) - 1) * jnp.maximum(jnp.abs(ga), 0.25)
    gb = (2 * (gb >= 0) - 1) * jnp.maximum(jnp.abs(gb), 0.25)
    h = _layernorm(x, axis=-1) * (1 + ca) + sa
    x = x + ga * _L0_attn_ref(h, L0_attn_attn_norm_w, L0_attn_ffn_norm_w, L0_attn_w_qkv, L0_attn_w_o, L0_attn_w_up, L0_attn_w_down)
    h = _layernorm(x, axis=-1) * (1 + cb) + sb
    x = x + gb * _L0_ffn_ref(h, L0_ffn_Wg, L0_ffn_Wu, L0_ffn_Wd, L0_ffn_Wr, L0_ffn_Ag, L0_ffn_Bg, L0_ffn_Au, L0_ffn_Bu, L0_ffn_Ad, L0_ffn_Bd)
    return x

_drawn_inputs = setup_inputs


def setup_inputs(seed=0):
    import zlib

    import numpy as np

    out = dict(_drawn_inputs(seed))
    spreads = {'L0_attn_attn_norm_w': (1.0, 0.6), 'L0_attn_ffn_norm_w': (1.0, 0.6)}
    factors = {'L0_attn_w_qkv': 8.0,
     'L0_attn_w_o': 8.0,
     'L0_attn_w_up': 8.0,
     'L0_attn_w_down': 8.0,
     'L0_ffn_Wg': 7.598,
     'L0_ffn_Wu': 7.061,
     'L0_ffn_Wd': 6.935,
     'L0_ffn_Wr': 8.0,
     'L0_ffn_Ag': 8.0,
     'L0_ffn_Bg': 8.0,
     'L0_ffn_Au': 8.0,
     'L0_ffn_Bu': 8.0,
     'L0_ffn_Ad': 8.0,
     'L0_ffn_Bd': 8.0}
    for name, (base, spread) in spreads.items():
        noise = np.random.default_rng([zlib.crc32(name.encode()), seed]).standard_normal(out[name].shape)
        drawn = base * np.exp(spread * noise) if base else spread * noise
        out[name] = jnp.asarray(drawn.astype(out[name].dtype))
    for name, factor in factors.items():
        out[name] = (out[name] * factor).astype(out[name].dtype)
    return out
```

```python
from contextlib import ExitStack

import numpy as np

import concourse.bass as bass
from concourse import mybir

ALU = mybir.AluOpType
ACT = mybir.ActivationFunctionType
F32 = mybir.dt.float32
F32R = mybir.dt.float32r
BF16 = mybir.dt.bfloat16
AX_X = mybir.AxisListType.X

P = 128
B, S, D = 4, 512, 256
KT = D // P
HEADS, HD = 32, 8
BLOCK = S // 4
INTER = 512
MT = INTER // P
DFF = 704
E, R = 8, 16
EPS = 1e-5
SCALE = float(HD) ** -0.5
LORA_SCALE = 2.0
MASKED = -1e30

GH = 4
HALF = HEADS // 2
GQ = HALF // GH
UNITS = 2 * (S // BLOCK)
PARTS = 3
MROW = PARTS * 32
KS = MROW + GH
FF_TILES = [(m * P, min(P, DFF - m * P)) for m in range(-(-DFF // P))]
FT = len(FF_TILES)
VARIANTS = 3

SPLIT_WIDTHS = [("qk", KT * 2 * D), ("v", KT * D), ("up", KT * 2 * INTER), ("ag", KT * E * R),
                ("au", KT * E * R), ("wg", KT * DFF), ("wu", KT * DFF), ("bg", DFF), ("bu", DFF),
                ("wd", FT * D), ("ad", FT * E * R)]
PLAIN_WIDTHS = [("o", KT * D), ("down", MT * D), ("bd", D), ("r", KT * E)]
CONST_WIDTHS = [("cos", S), ("sin", S), ("ident", P), ("mean", P), ("swap", P), ("head", GH), ("before", E * E), ("one", 1)]


def layout(widths):
    places, at = {}, 0
    for name, width in widths:
        places[name] = (at, width)
        at += width
    return places, at


SPLIT, SPLIT_COLS = layout(SPLIT_WIDTHS)
PLAIN, PLAIN_COLS = layout(PLAIN_WIDTHS)
CONST, CONST_COLS = layout(CONST_WIDTHS)
STAGE = 4 * S
CHUNKS = [(c, min(STAGE, SPLIT_COLS - c)) for c in range(0, SPLIT_COLS, STAGE)]




def ff_steps():
    steps = [(0, 0)]
    for m in range(FT):
        steps += [(m, 1)] + ([(m + 1, 0)] if m + 1 < FT else []) + [(m, 2)]
    return steps


FF_STEPS = ff_steps()
FF_USED = [VARIANTS * m + v + 1 for m, v in FF_STEPS]


class Signal:

    def __init__(self, sem, per_row, before=0):
        self.sem, self.per_row, self.before = sem, per_row, before

    def count(self, row, k):
        return row * self.per_row + (self.before + k)


def adaln_kernel(nc, x, smalls, wmod, wsplit, wplain, consts, masks, out):
    with ExitStack() as ctx:
        def sb(name, shape, dt=F32):
            return ctx.enter_context(nc.sbuf_tensor(name, shape, dt))

        def signal(name, per_row, before=0):
            return Signal(ctx.enter_context(nc.semaphore(name)), per_row, before)

        w_hi = sb("w_hi", [P, SPLIT_COLS], F32R)
        w_lo = sb("w_lo", [P, SPLIT_COLS], F32R)
        w_plain = sb("w_plain", [P, PLAIN_COLS])
        const = sb("const", [P, CONST_COLS])
        mask = sb("mask", [P, 3, P], BF16)
        small = sb("small", [P, 2 * KT + KT * B])
        act_c = sb("act_c", [P, KT * B])
        mod_all = sb("mod_all", [P, 6 * KT, B])
        mod = sb("mod", [P, 6 * KT])
        gate_tmp = sb("gate_tmp", [P, 2 * KT * B])
        x_in = sb("x_in", [P, KT, S])
        h = sb("h", [P, KT, S])
        n_hi = sb("n_hi", [P, KT, S], F32R)
        n_lo = sb("n_lo", [P, KT, S], F32R)
        q_st = sb("q_st", [P, HEADS // GH, S], F32R)
        k_st = sb("k_st", [P, HEADS // GH, S], F32R)
        v_ex = sb("v_ex", [P, HALF, P])
        arena = sb("arena", [P, 10, S])
        arena_r = sb("arena_r", [P, 16, S], F32R)
        logits = sb("logits", [P, S // P, E])
        l_max = sb("l_max", [P, S // P])
        l_sum = sb("l_sum", [P, S // P])
        l_exp = sb("l_exp", [P, S // P, E])
        rank = sb("rank", [P, S // P, E])
        pick = sb("pick", [P, 2, S // P, E])
        eps_col = sb("eps_col", [P, 1])
        std = sb("std", [P, S // P])
        rstd = sb("rstd", [P, S // P])
        bank = ctx.enter_context(nc.psum_tensor("bank", [P, 8, S], F32))

        def hi_lo(name):
            at, width = SPLIT[name]
            return w_hi[:, at:at + width], w_lo[:, at:at + width]

        def plain(name):
            at, width = PLAIN[name]
            return w_plain[:, at:at + width]

        def con(name):
            at, width = CONST[name]
            return const[:, at:at + width]

        xc = arena[:, 0:2, :]
        sq = arena[:, 2:4, :]
        tile_sum = arena[:, 4, :]
        qk_sb, q_cos, q_sin = arena[:, 6:8, :], arena[:, 8, :], arena[:, 9, :]
        roped = arena[:, 2:4, :]
        prob = [arena[:, 2 * i:2 * i + 2, :].rearrange("p a s -> p (a s)") for i in range(2)]
        v_sb = arena[:, 4:6, :].rearrange("p a (b f) -> p (a b) f", b=2)
        ctx_n = arena[:, 6:8, :]
        den_inv = arena[0:P // 2, 8, 0:2 * P]
        neg_max = arena[:, 9, :].rearrange("p (g c) -> p g c", c=P)
        hidden = arena[:, 6:10, :]
        silu_out = [arena[:, 2 + i, :] for i in range(2)]
        pair_tmp = [arena[:, 5 + i, :] for i in range(2)]
        picks_t = [arena[:, i, :] for i in (7, 8, 9, 4)]
        k_ex = [arena_r[:, 4 * i:4 * i + 4, :].rearrange("p g (h s) -> p g h s", h=GH) for i in range(2)]
        rope_hl = [(arena_r[:, 8 + 2 * i, :], arena_r[:, 9 + 2 * i, :]) for i in range(2)]
        lora_hl = [(arena_r[:, 2 * i, :], arena_r[:, 2 * i + 1, :]) for i in range(4)]
        ff_hl = [(arena_r[:, 8 + 2 * i, :], arena_r[:, 9 + 2 * i, :]) for i in range(4)]

        x_loaded = signal("x_loaded", 16)
        small_loaded = signal("small_loaded", 0)
        wmod_loaded = signal("wmod_loaded", 0)
        const_loaded = signal("const_loaded", 0)
        plain_loaded = signal("plain_loaded", 0)
        chunk_loaded = [signal(f"chunk_loaded{i}", 0) for i in range(2)]
        chunk_hi = signal("chunk_hi", 0)
        chunk_lo = signal("chunk_lo", 0)
        cond_ready = signal("cond_ready", 0)
        mod_ready = signal("mod_ready", 0)
        mod_steps = signal("mod_steps", 0)
        zeroed = signal("zeroed", 0)
        mod_row = signal("mod_row", 1)
        sum_ready = signal("sum_ready", 2)
        mean_ready = signal("mean_ready", 2)
        square_mean = signal("square_mean", 4)
        sq_ready = signal("sq_ready", 4)
        std_ready = signal("std_ready", 4)
        rstd_ready = signal("rstd_ready", 4)
        rstd_spread = signal("rstd_spread", 4)
        xc_ready = signal("xc_ready", 2)
        scaled_ready = signal("scaled_ready", 2)
        h_ready = signal("h_ready", 2)
        norm_ready = signal("norm_ready", 2)
        n_hi_ready = signal("n_hi_ready", 3)
        n_lo_ready = signal("n_lo_ready", 3)
        qk_proj = signal("qk_proj", 4)
        qk_copied = signal("qk_copied", 4)
        swapped = signal("swapped", 4)
        cos_done = signal("cos_done", 4)
        sin_done = signal("sin_done", 4)
        rope_done = signal("rope_done", 4)
        rope_hi = signal("rope_hi", 4)
        rope_lo = signal("rope_lo", 4)
        stacked = [signal(f"stacked{i}", 2 * PARTS * GQ * 16) for i in range(2)]
        v_proj = signal("v_proj", 2)
        v_copied = signal("v_copied", 2)
        k_spread = signal("k_spread", UNITS)
        v_spread = signal("v_spread", UNITS)
        s1_ready = signal("s1_ready", 2 * UNITS)
        max_done = signal("max_done", 2 * UNITS)
        max_t = signal("max_t", UNITS)
        max_rows = signal("max_rows", UNITS)
        s2_ready = signal("s2_ready", 2 * UNITS)
        exp_done = signal("exp_done", 2 * UNITS)
        den_done = signal("den_done", UNITS)
        pv_done = signal("pv_done", 2 * UNITS)
        ctx_done = signal("ctx_done", UNITS)
        o_proj = signal("o_proj", 1)
        x1_ready = signal("x1_ready", 1)
        up_ready = signal("up_ready", MT)
        up_silu = signal("up_silu", MT)
        hidden_done = signal("hidden_done", MT)
        down_ready = signal("down_ready", 1)
        d_added = signal("d_added", 1)
        x2_ready = signal("x2_ready", 1)
        route_ready = signal("route_ready", 1)
        l_copied = signal("l_copied", 1)
        l_steps = signal("l_steps", 10)
        l_exp_done = signal("l_exp_done", 1)
        l_picks = signal("l_picks", 2)
        spread = signal("spread", 4)
        pick_t = signal("pick_t", 4)
        pick_copied = signal("pick_copied", 4)
        lora_a = signal("lora_a", 1)
        lora_in = signal("lora_in", 4)
        lora_hi = signal("lora_hi", 4)
        lora_lo = signal("lora_lo", 4)
        gu_ready = signal("gu_ready", FT * VARIANTS)
        ff_silu = signal("ff_silu", FT * VARIANTS)
        ff_prod = signal("ff_prod", FT * VARIANTS)
        ff_hi = signal("ff_hi", FT * VARIANTS)
        ff_lo = signal("ff_lo", FT * VARIANTS)
        ff_used = signal("ff_used", FT * VARIANTS - 1)
        z_ready = signal("z_ready", 1)
        z_steps = signal("z_steps", 3)
        y_ready = signal("y_ready", 1)
        out_ready = signal("out_ready", 1, before=1)
        stored = signal("stored", 16, before=16)

        fills = [("s1", 0), ("s1", 1), ("t", 0)]
        for u in range(UNITS):
            if u + 1 < UNITS:
                fills += [("s1", 2 * u + 2), ("s1", 2 * u + 3)]
            fills += [("s2", 2 * u), ("s2", 2 * u + 1)]
            if u + 1 < UNITS:
                fills += [("t", u + 1)]
        slot_of = {fill: n % 3 for n, fill in enumerate(fills)}
        freed_by = {"s1": max_done, "t": max_rows, "s2": exp_done}

        def slot(fill):
            return bank[:, 2 * slot_of[fill]:2 * slot_of[fill] + 2, :]

        def diagonal(flat, first):
            step = P + HD
            whole = flat[:, first:first + 7 * step + HD]
            return bass.AP(whole.tensor, whole.offset, [whole.ap[0], [step, 8], [1, HD]])

        block = ctx.enter_context(nc.Block())

        @block.sync
        def _(sp):
            sp.dma_start(small[:], smalls).then_inc(small_loaded.sem, 16)
            sp.dma_start(arena[:, 4:10, :].rearrange("p a s -> p (a s)"), wmod).then_inc(wmod_loaded.sem, 16)
            sp.dma_start(const[:], consts).then_inc(const_loaded.sem, 16)
            sp.dma_start(mask[:], masks).then_inc(const_loaded.sem, 16)
            sp.dma_start(x_in[:], x[0]).then_inc(x_loaded.sem, 16)
            for c, (at, width) in enumerate(CHUNKS):
                if c == 1:
                    sp.wait_ge(mod_ready.sem, 1)
                if c >= 2:
                    sp.wait_ge(chunk_lo.sem, c - 1)
                stage = arena[:, 4 * (c % 2):4 * (c % 2) + 4, :].rearrange("p a s -> p (a s)")
                sp.dma_start(stage[:, 0:width], wsplit[:, at:at + width]).then_inc(chunk_loaded[c % 2].sem, 16)
            sp.dma_start(w_plain[:], wplain).then_inc(plain_loaded.sem, 16)

            def row_steps(row, next_row):
                for i in range(4):
                    dt, is_k = i // 2, i % 2
                    sp.wait_ge(rope_hi.sem, rope_hi.count(row, i + 1))
                    sp.wait_ge(rope_lo.sem, rope_lo.count(row, i + 1))
                    hi, lo = rope_hl[i % 2]
                    dest = k_st if is_k else q_st
                    for part, src in enumerate((hi, lo, hi) if is_k else (hi, hi, lo)):
                        for gq in range(GQ):
                            sp.dma_start(dest[32 * part:32 * part + 32, dt * GQ + gq, :].bitcast(F32),
                                         src[32 * gq:32 * gq + 32, :].bitcast(F32)).then_inc(stacked[i % 2].sem, 16)
                if next_row is not None:
                    sp.wait_ge(x2_ready.sem, x2_ready.count(row, 1))
                    sp.dma_start(x_in[:], x[bass.ds(next_row, 1)].rearrange("b p t s -> p (b t) s"))\
                        .then_inc(x_loaded.sem, 16)
                sp.wait_ge(out_ready.sem, out_ready.count(row, 1))
                sp.dma_start(out[bass.ds(row, 1)].rearrange("b p t s -> p (b t) s"),
                             arena[:, 5:7, :]).then_inc(stored.sem, 16)

            with sp.Fori(0, B - 1) as row:
                row_steps(row, row + 1)
            row_steps(B - 1, None)
            sp.wait_ge(stored.sem, stored.count(B - 1, 16))

        @block.gpsimd
        def _(pool):
            with pool.Fori(0, B) as row:
                def tile_sums(src):
                    nc.gpsimd.tensor_tensor(tile_sum, src[:, 0, :], src[:, 1, :], ALU.add).then_inc(sum_ready.sem, 1)

                pool.wait_ge(x_loaded.sem, x_loaded.count(row, 16))
                pool.wait_ge(mod_row.sem, mod_row.count(row, 1))
                tile_sums(x_in)
                for i in range(4):
                    pool.wait_ge(qk_copied.sem, qk_copied.count(row, i + 1))
                    if i:
                        pool.wait_ge(rope_done.sem, rope_done.count(row, i))
                    nc.gpsimd.tensor_tensor(q_cos, qk_sb[:, i % 2, :], con("cos"), ALU.mult).then_inc(cos_done.sem, 1)
                pool.wait_ge(zeroed.sem, 5)
                def spread_keys(u):
                    blk, half = u // 2, u % 2
                    if u < 2:
                        for i in range(2):
                            pool.wait_ge(stacked[i].sem, stacked[i].count(row, (half + 1) * PARTS * GQ * 16))
                    if u >= 2:
                        pool.wait_ge(s2_ready.sem, s2_ready.count(row, 2 * (u - 1)))
                    src = k_st[0:KS, half * GQ:(half + 1) * GQ, blk * P:(blk + 1) * P].bitcast(F32)
                    nc.gpsimd.tensor_tensor(k_ex[u % 2][0:KS, :, 0, :], src,
                                            con("head")[0:KS, 0:1].unsqueeze(2).broadcast_to([KS, GQ, P]), ALU.mult)
                    for hh in range(1, GH):
                        last = nc.gpsimd.tensor_scalar(k_ex[u % 2][0:KS, :, hh, :], src,
                                                       con("head")[0:KS, hh:hh + 1], 1.0, ALU.mult, ALU.mult)
                    last.then_inc(k_spread.sem, 1)

                def spread_values(u):
                    blk, half = u // 2, u % 2
                    if u % 4 == 0:
                        pool.wait_ge(v_copied.sem, v_copied.count(row, u // 4 + 1))
                    if u:
                        pool.wait_ge(pv_done.sem, pv_done.count(row, 2 * u))
                    values = v_sb[:, blk, half * P:(half + 1) * P].rearrange("p (a j d) -> p a j d", a=2, d=HD)
                    for a in range(2):
                        flat = v_ex[:, 8 * a:8 * a + 8, :].rearrange("p j c -> p (j c)")
                        last = nc.gpsimd.tensor_tensor(diagonal(flat, 0), values[:, a],
                                                       con("one").unsqueeze(2).broadcast_to([P, 8, HD]), ALU.mult)
                    last.then_inc(v_spread.sem, 1)

                spread_keys(0)
                for u in range(UNITS):
                    if u + 1 < UNITS:
                        spread_keys(u + 1)
                    spread_values(u)
                pool.wait_ge(x2_ready.sem, x2_ready.count(row, 1))
                tile_sums(h)

        @block.scalar
        def _(act):
            act.wait_ge(small_loaded.sem, 16)
            nc.scalar.activation(act_c[:], small[:, 2 * KT:], ACT.Silu).then_inc(cond_ready.sem, 1)
            for c, (at, width) in enumerate(CHUNKS):
                act.wait_ge(chunk_loaded[c % 2].sem, 16 * (c // 2 + 1))
                stage = arena[:, 4 * (c % 2):4 * (c % 2) + 4, :].rearrange("p a s -> p (a s)")
                nc.scalar.copy(w_hi[:, at:at + width], stage[:, 0:width]).then_inc(chunk_hi.sem, 1)
            with act.Fori(0, B) as row:
                def squares(n, src):
                    for t in range(KT):
                        last = nc.scalar.activation(sq[:, t, :], src[:, t, :], ACT.Square)
                    last.then_inc(sq_ready.sem, 1)

                def deviation(n, where):
                    act.wait_ge(square_mean.sem, square_mean.count(row, n + 1))
                    nc.scalar.activation(std[:], bank[:, where, 0:S // P], ACT.Sqrt, bias=eps_col[:])\
                        .then_inc(std_ready.sem, 1)

                act.wait_ge(xc_ready.sem, xc_ready.count(row, 1))
                squares(0, xc)
                deviation(0, 1)
                act.wait_ge(scaled_ready.sem, scaled_ready.count(row, 1))
                for t in range(KT):
                    last = nc.scalar.activation(h[:, t, :], xc[:, t, :], ACT.Identity, bias=mod[:, t:t + 1])
                last.then_inc(h_ready.sem, 1)
                act.wait_ge(h_ready.sem, h_ready.count(row, 1))
                squares(1, h)
                deviation(1, 2)
                act.wait_ge(norm_ready.sem, norm_ready.count(row, 1))
                nc.scalar.copy(n_hi[:], xc[:]).then_inc(n_hi_ready.sem, 1)
                for i in range(5):
                    if i < 4:
                        act.wait_ge(qk_proj.sem, qk_proj.count(row, i + 1))
                        if i == 0:
                            act.wait_ge(stored.sem, stored.count(row, 0))
                        if i >= 2:
                            act.wait_ge(swapped.sem, swapped.count(row, i - 1))
                            act.wait_ge(cos_done.sem, cos_done.count(row, i - 1))
                        nc.scalar.copy(qk_sb[:, i % 2, :], bank[:, 3 + i % 2, :]).then_inc(qk_copied.sem, 1)
                    if i:
                        j = i - 1
                        act.wait_ge(rope_done.sem, rope_done.count(row, j + 1))
                        if j >= 2:
                            act.wait_ge(stacked[j % 2].sem, stacked[j % 2].count(row, PARTS * GQ * 16))
                        nc.scalar.copy(rope_hl[j % 2][0], roped[:, j % 2, :]).then_inc(rope_hi.sem, 1)
                for i in range(2):
                    act.wait_ge(v_proj.sem, v_proj.count(row, i + 1))
                    nc.scalar.copy(arena[:, 4 + i, :], bank[:, 7 if i == 0 else 2, :]).then_inc(v_copied.sem, 1)

                def max_to_rows(u):
                    blk, half = u // 2, u % 2
                    act.wait_ge(max_t.sem, max_t.count(row, u + 1))
                    src = slot(("t", u))[MROW:KS, 0, :].rearrange("p (g s) -> p g s", s=P)
                    nc.scalar.copy(q_st[MROW:KS, half * GQ:(half + 1) * GQ, blk * P:(blk + 1) * P], src)\
                        .then_inc(max_rows.sem, 1)

                max_to_rows(0)
                for u in range(UNITS):
                    for a in range(2):
                        n = 2 * u + a
                        act.wait_ge(s2_ready.sem, s2_ready.count(row, n + 1))
                        if n >= 2:
                            act.wait_ge(pv_done.sem, pv_done.count(row, n - 1))
                        nc.scalar.activation(prob[a], slot(("s2", n)).rearrange("p a s -> p (a s)"),
                                             ACT.Exp, scale=SCALE).then_inc(exp_done.sem, 1)
                    if u + 1 < UNITS:
                        max_to_rows(u + 1)
                act.wait_ge(x1_ready.sem, x1_ready.count(row, 1))
                squares(2, h)
                deviation(2, 2)
                act.wait_ge(norm_ready.sem, norm_ready.count(row, 2))
                nc.scalar.copy(n_hi[:], xc[:]).then_inc(n_hi_ready.sem, 1)
                for m in range(MT):
                    act.wait_ge(up_ready.sem, up_ready.count(row, m + 1))
                    if m >= 2:
                        act.wait_ge(hidden_done.sem, hidden_done.count(row, m - 1))
                    nc.scalar.activation(silu_out[m % 2], bank[:, 3 + 2 * (m % 2), :], ACT.Silu).then_inc(up_silu.sem, 1)
                act.wait_ge(xc_ready.sem, xc_ready.count(row, 2))
                squares(3, xc)
                deviation(3, 7)
                act.wait_ge(scaled_ready.sem, scaled_ready.count(row, 2))
                for t in range(KT):
                    last = nc.scalar.activation(xc[:, t, :], xc[:, t, :], ACT.Identity,
                                                bias=mod[:, 3 * KT + t:3 * KT + t + 1])
                last.then_inc(h_ready.sem, 1)
                act.wait_ge(h_ready.sem, h_ready.count(row, 2))
                nc.scalar.copy(n_hi[:], xc[:]).then_inc(n_hi_ready.sem, 1)
                act.wait_ge(l_steps.sem, l_steps.count(row, 2))
                nc.scalar.activation(l_exp[:], l_exp[:], ACT.Exp).then_inc(l_exp_done.sem, 1)
                for kind in range(4):
                    act.wait_ge(pick_t.sem, pick_t.count(row, kind + 1))
                    nc.scalar.copy(picks_t[kind], bank[:, 4 + kind, :]).then_inc(pick_copied.sem, 1)
                for i in range(4):
                    act.wait_ge(lora_in.sem, lora_in.count(row, i + 1))
                    nc.scalar.copy(lora_hl[i][0], pair_tmp[i % 2]).then_inc(lora_hi.sem, 1)
                for n in range(len(FF_STEPS) + 1):
                    if n < len(FF_STEPS):
                        m, v = FF_STEPS[n]
                        width = FF_TILES[m][1]
                        act.wait_ge(gu_ready.sem, gu_ready.count(row, n + 1))
                        if n >= 2:
                            act.wait_ge(ff_prod.sem, ff_prod.count(row, n - 1))
                        nc.scalar.activation(silu_out[n % 2][0:width], bank[0:width, 2 + 2 * (m % 2), :], ACT.Silu)\
                            .then_inc(ff_silu.sem, 1)
                    if n:
                        j = n - 1
                        width = FF_TILES[FF_STEPS[j][0]][1]
                        act.wait_ge(ff_prod.sem, ff_prod.count(row, j + 1))
                        if j >= 4:
                            act.wait_ge(ff_used.sem, ff_used.count(row, FF_USED[j - 4]))
                        nc.scalar.copy(ff_hl[j % 4][0][0:width], pair_tmp[j % 2][0:width]).then_inc(ff_hi.sem, 1)

        @block.vector
        def _(dve):
            nc.vector.memset(k_st[MROW:P, :, :].bitcast(F32), 1.0).then_inc(zeroed.sem, 1)
            nc.vector.memset(eps_col[:], EPS).then_inc(zeroed.sem, 1)
            nc.vector.memset(v_ex[:], 0.0).then_inc(zeroed.sem, 1)
            dve.wait_ge(zeroed.sem, 3)
            for a in range(2):
                flat = v_ex[:, 8 * a:8 * a + 8, :].rearrange("p j c -> p (j c)")
                nc.vector.memset(diagonal(flat, P // 2), 1.0).then_inc(zeroed.sem, 1)
            nc.vector.memset(l_max[:], 0.0).then_inc(stored.sem, 16)
            nc.vector.memset(mod[:], 0.0).then_inc(out_ready.sem, 1)
            dve.wait_ge(mod_ready.sem, 1)
            mod_ps = bank[:, 0, 0:6 * KT * B].rearrange("p (c b) -> p c b", b=B)
            nc.vector.tensor_copy(mod_all[:], mod_ps).then_inc(mod_steps.sem, 1)
            dve.wait_ge(mod_steps.sem, 1)
            for n, c in enumerate((1, 4)):
                part = mod_all[:, c * KT:(c + 1) * KT, :]
                nc.vector.tensor_scalar(part, part, 1.0, None, ALU.add).then_inc(mod_steps.sem, 1)
            for n, c in enumerate((2, 5)):
                part = mod_all[:, c * KT:(c + 1) * KT, :]
                sign = gate_tmp[:, n * KT * B:(n + 1) * KT * B].rearrange("p (t b) -> p t b", b=B)
                nc.vector.tensor_scalar(sign, part, 0.0, 2.0, ALU.is_ge, ALU.mult).then_inc(mod_steps.sem, 1)
                dve.wait_ge(mod_steps.sem, 4 + 4 * n)
                nc.vector.scalar_tensor_tensor(part, part, -1.0, part, ALU.mult, ALU.max).then_inc(mod_steps.sem, 1)
                dve.wait_ge(mod_steps.sem, 5 + 4 * n)
                nc.vector.tensor_scalar(part, part, 0.25, None, ALU.max).then_inc(mod_steps.sem, 1)
                dve.wait_ge(mod_steps.sem, 6 + 4 * n)
                nc.vector.scalar_tensor_tensor(part, sign, -1.0, part, ALU.add, ALU.mult).then_inc(mod_steps.sem, 1)
            dve.wait_ge(mod_steps.sem, 11)
            for c, (at, width) in enumerate(CHUNKS):
                dve.wait_ge(chunk_hi.sem, c + 1)
                stage = arena[:, 4 * (c % 2):4 * (c % 2) + 4, :].rearrange("p a s -> p (a s)")
                nc.vector.tensor_tensor(w_lo[:, at:at + width], stage[:, 0:width],
                                        w_hi[:, at:at + width].bitcast(F32), ALU.subtract).then_inc(chunk_lo.sem, 1)
            dve.wait_ge(chunk_lo.sem, len(CHUNKS))
            with dve.Fori(0, B) as row:
                def centred(n, src, where):
                    dve.wait_ge(mean_ready.sem, mean_ready.count(row, n + 1))
                    for t in range(KT):
                        last = nc.vector.tensor_tensor(xc[:, t, :], src[:, t, :], bank[:, where, :], ALU.subtract)
                    last.then_inc(xc_ready.sem, 1)

                def inverse(n):
                    dve.wait_ge(std_ready.sem, std_ready.count(row, n + 1))
                    nc.vector.reciprocal(rstd[:], std[:]).then_inc(rstd_ready.sem, 1)

                def scaled(n, src, columns, where, out_signal):
                    dve.wait_ge(rstd_spread.sem, rstd_spread.count(row, n + 1))
                    for t in range(KT):
                        last = nc.vector.scalar_tensor_tensor(xc[:, t, :], src[:, t, :], columns[:, t:t + 1],
                                                              bank[:, where, :], ALU.mult, ALU.mult)
                    last.then_inc(out_signal.sem, 1)

                def n_lows(n):
                    dve.wait_ge(n_hi_ready.sem, n_hi_ready.count(row, n + 1))
                    nc.vector.tensor_tensor(n_lo[:], xc[:], n_hi[:].bitcast(F32), ALU.subtract)\
                        .then_inc(n_lo_ready.sem, 1)

                dve.wait_ge(out_ready.sem, out_ready.count(row, 0))
                nc.vector.tensor_copy(mod[:], mod_all[:, :, bass.ds(row, 1)].rearrange("p c b -> p (c b)"))\
                    .then_inc(mod_row.sem, 1)
                dve.wait_ge(mod_row.sem, mod_row.count(row, 1))
                dve.wait_ge(x_loaded.sem, x_loaded.count(row, 16))
                centred(0, x_in, 0)
                inverse(0)
                scaled(0, xc, mod[:, KT:2 * KT], 1, scaled_ready)
                inverse(1)
                scaled(1, h, small[:, 0:KT], 2, norm_ready)
                dve.wait_ge(norm_ready.sem, norm_ready.count(row, 1))
                n_lows(0)

                def rope_low(i):
                    dve.wait_ge(rope_hi.sem, rope_hi.count(row, i + 1))
                    nc.vector.tensor_tensor(rope_hl[i % 2][1], roped[:, i % 2, :], rope_hl[i % 2][0].bitcast(F32),
                                            ALU.subtract).then_inc(rope_lo.sem, 1)

                for i in range(4):
                    dve.wait_ge(swapped.sem, swapped.count(row, i + 1))
                    if i:
                        dve.wait_ge(rope_done.sem, rope_done.count(row, i))
                    nc.vector.tensor_tensor(q_sin, bank[:, 5 + i % 2, :], con("sin"), ALU.mult).then_inc(sin_done.sem, 1)
                    if i:
                        rope_low(i - 1)
                    dve.wait_ge(cos_done.sem, cos_done.count(row, i + 1))
                    dve.wait_ge(sin_done.sem, sin_done.count(row, i + 1))
                    nc.vector.tensor_tensor(roped[:, i % 2, :], q_cos, q_sin, ALU.add).then_inc(rope_done.sem, 1)
                dve.wait_ge(rope_done.sem, rope_done.count(row, 4))
                rope_low(3)

                def unit_max(u):
                    if u:
                        dve.wait_ge(max_t.sem, max_t.count(row, u))
                    for a in range(2):
                        n = 2 * u + a
                        dve.wait_ge(s1_ready.sem, s1_ready.count(row, n + 1))
                        nc.vector.tensor_reduce(neg_max[:, 2 * a:2 * a + 2, MROW:KS],
                                                slot(("s1", n)).rearrange("p a (h s) -> p a h s", s=P),
                                                AX_X, ALU.max, negate=True).then_inc(max_done.sem, 1)

                def normalise(u):
                    blk, half = u // 2, u % 2
                    acc = bank[:, 6 + u % 2, 0:2 * P]
                    dve.wait_ge(pv_done.sem, pv_done.count(row, 2 * u + 2))
                    if u:
                        dve.wait_ge(ctx_done.sem, ctx_done.count(row, u))
                    nc.vector.reciprocal(den_inv, acc[P // 2:P, :]).then_inc(den_done.sem, 1)
                    dve.wait_ge(den_done.sem, den_done.count(row, u + 1))
                    for a in range(2):
                        last = nc.vector.tensor_tensor(ctx_n[64 * a:64 * a + 64, half, blk * P:(blk + 1) * P],
                                                       acc[0:64, a * P:(a + 1) * P], den_inv[:, a * P:(a + 1) * P],
                                                       ALU.mult)
                    last.then_inc(ctx_done.sem, 1)

                unit_max(0)
                for u in range(UNITS):
                    if u + 1 < UNITS:
                        unit_max(u + 1)
                    normalise(u)
                dve.wait_ge(o_proj.sem, o_proj.count(row, 1))
                nc.vector.tensor_tensor(h[:], h[:], bank[:, 0:2, :], ALU.add).then_inc(x1_ready.sem, 1)
                dve.wait_ge(x1_ready.sem, x1_ready.count(row, 1))
                inverse(2)
                scaled(2, h, small[:, KT:2 * KT], 2, norm_ready)
                dve.wait_ge(norm_ready.sem, norm_ready.count(row, 2))
                n_lows(1)
                for m in range(MT):
                    dve.wait_ge(up_silu.sem, up_silu.count(row, m + 1))
                    nc.vector.tensor_tensor(hidden[:, m, :], silu_out[m % 2], bank[:, 4 + 2 * (m % 2), :], ALU.mult)\
                        .then_inc(hidden_done.sem, 1)
                dve.wait_ge(down_ready.sem, down_ready.count(row, 1))
                nc.vector.tensor_tensor(h[:], h[:], bank[:, 0:2, :], ALU.add).then_inc(d_added.sem, 1)
                dve.wait_ge(d_added.sem, d_added.count(row, 1))
                for t in range(KT):
                    last = nc.vector.scalar_tensor_tensor(h[:, t, :], h[:, t, :], mod[:, 2 * KT + t:2 * KT + t + 1],
                                                          x_in[:, t, :], ALU.mult, ALU.add)
                last.then_inc(x2_ready.sem, 1)
                dve.wait_ge(x2_ready.sem, x2_ready.count(row, 1))
                centred(1, h, 2)
                inverse(3)
                scaled(3, xc, mod[:, 4 * KT:5 * KT], 7, scaled_ready)
                n_lows(2)

                steps = [0]

                def step(ins):
                    steps[0] += 1
                    ins.then_inc(l_steps.sem, 1)
                    return steps[0]

                def after(n):
                    dve.wait_ge(l_steps.sem, l_steps.count(row, n))

                dve.wait_ge(route_ready.sem, route_ready.count(row, 1))
                nc.vector.tensor_copy(logits[:], bank[:, 3, 0:S // P * E].rearrange("p (j e) -> p j e", e=E))\
                    .then_inc(l_copied.sem, 1)
                dve.wait_ge(l_copied.sem, l_copied.count(row, 1))
                after(step(nc.vector.tensor_reduce(l_max[:], logits[:], AX_X, ALU.max)))
                step(nc.vector.tensor_tensor(l_exp[:], logits[:], l_max[:].unsqueeze(2).broadcast_to([P, S // P, E]),
                                             ALU.subtract))
                wide = [t.rearrange("p (j e f) -> p j e f", j=8, e=8)[:, 0:S // P] for t in pair_tmp]
                other = logits[:].unsqueeze(2).broadcast_to([P, S // P, E, E])
                own = logits[:].unsqueeze(3).broadcast_to([P, S // P, E, E])
                before = con("before").rearrange("p (e f) -> p e f", f=E).unsqueeze(1).broadcast_to([P, S // P, E, E])
                step(nc.vector.tensor_tensor(wide[0], other, own, ALU.is_gt))
                after(step(nc.vector.tensor_tensor(wide[1], other, own, ALU.is_equal)))
                after(step(nc.vector.tensor_tensor(wide[1], wide[1], before, ALU.mult)))
                after(step(nc.vector.tensor_tensor(wide[0], wide[0], wide[1], ALU.add)))
                after(step(nc.vector.tensor_reduce(rank[:], wide[0], AX_X, ALU.add)))
                dve.wait_ge(l_exp_done.sem, l_exp_done.count(row, 1))
                after(step(nc.vector.tensor_reduce(l_sum[:], l_exp[:], AX_X, ALU.add)))
                after(step(nc.vector.reciprocal(l_max[:], l_sum[:])))
                step(nc.vector.tensor_tensor(l_exp[:], l_exp[:], l_max[:].unsqueeze(2).broadcast_to([P, S // P, E]),
                                             ALU.mult))
                def spread_to(kind):
                    return pair_tmp[kind % 2].rearrange("p (j e r) -> p j e r", j=S // P, r=R)

                def over_ranks(t):
                    return t.unsqueeze(3).broadcast_to([P, S // P, E, R])

                after(steps[0])
                nc.vector.tensor_scalar(pick[:, 0], rank[:], 0.0, LORA_SCALE, ALU.is_equal, ALU.mult)\
                    .then_inc(l_picks.sem, 1)
                nc.vector.tensor_scalar(pick[:, 1], rank[:], 1.0, LORA_SCALE, ALU.is_equal, ALU.mult)\
                    .then_inc(l_picks.sem, 1)
                dve.wait_ge(l_picks.sem, l_picks.count(row, 2))
                nc.vector.tensor_copy(spread_to(0), over_ranks(pick[:, 0])).then_inc(spread.sem, 1)
                nc.vector.tensor_tensor(spread_to(1), over_ranks(pick[:, 1]), over_ranks(pick[:, 0]), ALU.subtract)\
                    .then_inc(spread.sem, 1)
                for k in range(2):
                    dve.wait_ge(pick_t.sem, pick_t.count(row, k + 1))
                    nc.vector.tensor_tensor(spread_to(k), over_ranks(pick[:, k]), over_ranks(l_exp[:]), ALU.mult)\
                        .then_inc(spread.sem, 1)
                dve.wait_ge(lora_a.sem, lora_a.count(row, 1))
                dve.wait_ge(pick_t.sem, pick_t.count(row, 4))

                def lora_low(i):
                    dve.wait_ge(lora_hi.sem, lora_hi.count(row, i + 1))
                    nc.vector.tensor_tensor(lora_hl[i][1], pair_tmp[i % 2], lora_hl[i][0].bitcast(F32), ALU.subtract)\
                        .then_inc(lora_lo.sem, 1)

                for i in range(4):
                    gate_up, kind = i % 2, i // 2
                    dve.wait_ge(pick_copied.sem, pick_copied.count(row, kind + 1))
                    if i >= 2:
                        lora_low(i - 2)
                        dve.wait_ge(lora_lo.sem, lora_lo.count(row, i - 1))
                    nc.vector.tensor_tensor(pair_tmp[i % 2], picks_t[kind], bank[:, gate_up, :], ALU.mult)\
                        .then_inc(lora_in.sem, 1)
                lora_low(2)
                lora_low(3)

                def ff_low(j):
                    width = FF_TILES[FF_STEPS[j][0]][1]
                    dve.wait_ge(ff_hi.sem, ff_hi.count(row, j + 1))
                    nc.vector.tensor_tensor(ff_hl[j % 4][1][0:width], pair_tmp[j % 2][0:width],
                                            ff_hl[j % 4][0][0:width].bitcast(F32), ALU.subtract)\
                        .then_inc(ff_lo.sem, 1)

                for n, (m, v) in enumerate(FF_STEPS):
                    width = FF_TILES[m][1]
                    if n >= 2:
                        ff_low(n - 2)
                    dve.wait_ge(ff_silu.sem, ff_silu.count(row, n + 1))
                    if n >= 2:
                        dve.wait_ge(ff_lo.sem, ff_lo.count(row, n - 1))
                    else:
                        dve.wait_ge(lora_lo.sem, lora_lo.count(row, n + 3))
                    nc.vector.tensor_tensor(pair_tmp[n % 2][0:width], silu_out[n % 2][0:width],
                                            bank[0:width, 3 + 2 * (m % 2), :], ALU.mult).then_inc(ff_prod.sem, 1)
                ff_low(len(FF_STEPS) - 2)
                ff_low(len(FF_STEPS) - 1)
                dve.wait_ge(z_ready.sem, z_ready.count(row, 1))
                for k in range(2):
                    nc.vector.tensor_tensor(silu_out[k], picks_t[2 + k], bank[:, k, :], ALU.mult)\
                        .then_inc(z_steps.sem, 1)
                dve.wait_ge(z_steps.sem, z_steps.count(row, 2))
                nc.vector.tensor_tensor(silu_out[0], silu_out[0], silu_out[1], ALU.add).then_inc(z_steps.sem, 1)
                dve.wait_ge(y_ready.sem, y_ready.count(row, 1))
                for t in range(KT):
                    last = nc.vector.scalar_tensor_tensor(pair_tmp[t], bank[:, 6 + t, :],
                                                          mod[:, 5 * KT + t:5 * KT + t + 1], h[:, t, :],
                                                          ALU.mult, ALU.add)
                last.then_inc(out_ready.sem, 1)

        @block.tensor
        def _(pe):
            def product(to, w, w_cols, acts, rows, start, stop):
                (wh, wl), (ah, al) = w, acts
                nc.tensor.matmul(to, wl[rows, w_cols], ah[rows], start=start, stop=False)
                nc.tensor.matmul(to, wh[rows, w_cols], al[rows], start=False, stop=False)
                return nc.tensor.matmul(to, wh[rows, w_cols], ah[rows], start=False, stop=stop)

            def normed(w, width, cols, to):
                for kt in range(KT):
                    last = product(to, w, slice(kt * width + cols.start, kt * width + cols.stop),
                                   (n_hi[:, kt, :], n_lo[:, kt, :]), slice(0, P), kt == 0, kt == KT - 1)
                return last

            pe.wait_ge(cond_ready.sem, 1)
            pe.wait_ge(wmod_loaded.sem, 16)
            pe.wait_ge(const_loaded.sem, 32)
            wm = arena[:, 4:10, :].rearrange("p a s -> p (a s)")
            for c in range(6 * KT):
                for kt in range(KT):
                    last = nc.tensor.matmul(bank[:, 0, c * B:(c + 1) * B],
                                            wm[:, kt * 6 * D + c * P:kt * 6 * D + (c + 1) * P],
                                            act_c[:, kt * B:(kt + 1) * B], start=kt == 0, stop=kt == KT - 1)
            last.then_inc(mod_ready.sem, 1)
            pe.wait_ge(plain_loaded.sem, 16)
            pe.wait_ge(chunk_lo.sem, len(CHUNKS))
            pe.wait_ge(zeroed.sem, 5)
            pe.wait_ge(mod_steps.sem, 1)
            with pe.Fori(0, B) as row:
                def mean(n, where):
                    pe.wait_ge(sum_ready.sem, sum_ready.count(row, n + 1))
                    nc.tensor.matmul(bank[:, where, :], con("mean"), tile_sum, start=True, stop=True)\
                        .then_inc(mean_ready.sem, 1)

                def inverse_deviation(n, where):
                    pe.wait_ge(sq_ready.sem, sq_ready.count(row, n + 1))
                    for j in range(S // P):
                        for t in range(KT):
                            last = nc.tensor.matmul(bank[:, where, j:j + 1], sq[:, t, j * P:(j + 1) * P],
                                                    con("mean")[:, 0:1], start=t == 0, stop=t == KT - 1)
                    last.then_inc(square_mean.sem, 1)
                    pe.wait_ge(rstd_ready.sem, rstd_ready.count(row, n + 1))
                    for j in range(S // P):
                        last = nc.tensor.matmul(bank[:, where, j * P:(j + 1) * P], rstd[:, j:j + 1].broadcast_to([P, P]),
                                                con("ident"), start=True, stop=True)
                    last.then_inc(rstd_spread.sem, 1)

                mean(0, 0)
                inverse_deviation(0, 1)
                inverse_deviation(1, 2)
                pe.wait_ge(n_lo_ready.sem, n_lo_ready.count(row, 1))

                def swap(i):
                    pe.wait_ge(qk_copied.sem, qk_copied.count(row, i + 1))
                    if i >= 2:
                        pe.wait_ge(sin_done.sem, sin_done.count(row, i - 1))
                    nc.tensor.matmul(bank[:, 5 + i % 2, :], con("swap"), qk_sb[:, i % 2, :], start=True, stop=True)\
                        .then_inc(swapped.sem, 1)

                for i in range(4):
                    first = (i // 2) * P + (i % 2) * D
                    if i >= 2:
                        pe.wait_ge(qk_copied.sem, qk_copied.count(row, i - 1))
                    normed(hi_lo("qk"), 2 * D, slice(first, first + P), bank[:, 3 + i % 2, :])\
                        .then_inc(qk_proj.sem, 1)
                    if i:
                        swap(i - 1)
                wv = hi_lo("v")
                for blk in range(S // P):
                    to = bank[:, 7 if blk < 2 else 2, (blk % 2) * D:(blk % 2 + 1) * D]
                    for kt in range(KT):
                        rows = slice(kt * S + blk * P, kt * S + (blk + 1) * P)
                        feats = slice(kt * D, (kt + 1) * D)
                        nh = n_hi[:].rearrange("p t s -> p (t s)")[:, rows]
                        nl = n_lo[:].rearrange("p t s -> p (t s)")[:, rows]
                        nc.tensor.matmul(to, nl, wv[0][:, feats], start=kt == 0, stop=False)
                        nc.tensor.matmul(to, nh, wv[1][:, feats], start=False, stop=False)
                        last = nc.tensor.matmul(to, nh, wv[0][:, feats], start=False, stop=kt == KT - 1)
                    if blk % 2:
                        last.then_inc(v_proj.sem, 1)
                    if blk == 0:
                        swap(3)

                def fill(kind, n):
                    at = fills.index((kind, n))
                    if at >= 3:
                        what, k = fills[at - 3]
                        pe.wait_ge(freed_by[what].sem, freed_by[what].count(row, k + 1))
                    return slot((kind, n))

                def masked(to, which):
                    nc.tensor.matmul(to, mask[:, 0, :], mask[:, which:which + 1, :].broadcast_to([P, GH, P]),
                                     start=True, stop=which == 2)

                def scores_for_max(n):
                    u, a = n // 2, n % 2
                    blk, half = u // 2, u % 2
                    if a == 0:
                        pe.wait_ge(k_spread.sem, k_spread.count(row, u + 1))
                    to = fill("s1", n)
                    for g in range(2):
                        masked(to[:, g, :], 1)
                    for g in range(2):
                        gq = 2 * a + g
                        last = nc.tensor.matmul(to[:, g, :],
                                                q_st[0:MROW, half * GQ + gq, blk * P:(blk + 1) * P],
                                                k_ex[u % 2][0:MROW, gq, :, :], start=False, stop=True)
                    last.then_inc(s1_ready.sem, 1)

                def max_transposed(u):
                    pe.wait_ge(max_done.sem, max_done.count(row, 2 * u + 2))
                    to = fill("t", u)
                    for gq in range(GQ):
                        last = nc.tensor.transpose(to[0:KS, 0, gq * P:(gq + 1) * P], neg_max[:, gq, 0:KS], con("ident"))
                    last.then_inc(max_t.sem, 1)

                def shifted_scores(n):
                    u, a = n // 2, n % 2
                    blk, half = u // 2, u % 2
                    if a == 0:
                        pe.wait_ge(max_rows.sem, max_rows.count(row, u + 1))
                    to = fill("s2", n)
                    for g in range(2):
                        masked(to[:, g, :], 2)
                    for g in range(2):
                        gq = 2 * a + g
                        for hh in range(GH):
                            last = nc.tensor.matmul(to[:, g, hh * P:(hh + 1) * P], k_ex[u % 2][0:KS, gq, hh, :],
                                                    q_st[0:KS, half * GQ + gq, blk * P:(blk + 1) * P],
                                                    start=False, stop=True, skip_group_check=True)
                    last.then_inc(s2_ready.sem, 1)

                def contexts(n):
                    u, a = n // 2, n % 2
                    if a == 0:
                        pe.wait_ge(v_spread.sem, v_spread.count(row, u + 1))
                        if u >= 2:
                            pe.wait_ge(ctx_done.sem, ctx_done.count(row, u - 1))
                    pe.wait_ge(exp_done.sem, exp_done.count(row, n + 1))
                    for j in range(8):
                        last = nc.tensor.matmul(bank[:, 6 + u % 2, a * P:(a + 1) * P], v_ex[:, 8 * a + j, :],
                                                prob[a][:, j * P:(j + 1) * P], start=j == 0, stop=j == 7)
                    last.then_inc(pv_done.sem, 1)

                for i in range(2):
                    pe.wait_ge(stacked[i].sem, stacked[i].count(row, 2 * PARTS * GQ * 16))
                pe.wait_ge(v_copied.sem, v_copied.count(row, 2))
                scores_for_max(0)
                scores_for_max(1)
                max_transposed(0)
                for u in range(UNITS):
                    if u + 1 < UNITS:
                        scores_for_max(2 * u + 2)
                        scores_for_max(2 * u + 3)
                    shifted_scores(2 * u)
                    shifted_scores(2 * u + 1)
                    contexts(2 * u)
                    if u + 1 < UNITS:
                        max_transposed(u + 1)
                    contexts(2 * u + 1)
                pe.wait_ge(ctx_done.sem, ctx_done.count(row, UNITS))
                for t in range(KT):
                    for kt in range(KT):
                        last = nc.tensor.matmul(bank[:, t, :], plain("o")[:, kt * D + t * P:kt * D + (t + 1) * P],
                                                ctx_n[:, kt, :], start=kt == 0, stop=kt == KT - 1)
                last.then_inc(o_proj.sem, 1)
                inverse_deviation(2, 2)
                pe.wait_ge(n_lo_ready.sem, n_lo_ready.count(row, 2))
                for m in range(MT):
                    if m >= 2:
                        pe.wait_ge(hidden_done.sem, hidden_done.count(row, m - 1))
                    for part in range(2):
                        last = normed(hi_lo("up"), 2 * INTER, slice(part * INTER + m * P, part * INTER + (m + 1) * P),
                                      bank[:, 3 + 2 * (m % 2) + part, :])
                    last.then_inc(up_ready.sem, 1)
                pe.wait_ge(x1_ready.sem, x1_ready.count(row, 1))
                for t in range(KT):
                    for m in range(MT):
                        if t == 0:
                            pe.wait_ge(hidden_done.sem, hidden_done.count(row, m + 1))
                        last = nc.tensor.matmul(bank[:, t, :], plain("down")[:, m * D + t * P:m * D + (t + 1) * P],
                                                hidden[:, m, :], start=m == 0, stop=m == MT - 1)
                last.then_inc(down_ready.sem, 1)
                mean(1, 2)
                inverse_deviation(3, 7)
                pe.wait_ge(h_ready.sem, h_ready.count(row, 2))
                for j in range(S // P):
                    for kt in range(KT):
                        last = nc.tensor.matmul(bank[:, 3, j * E:(j + 1) * E], xc[:, kt, j * P:(j + 1) * P],
                                                plain("r")[:, kt * E:(kt + 1) * E], start=kt == 0, stop=kt == KT - 1)
                last.then_inc(route_ready.sem, 1)
                pe.wait_ge(n_lo_ready.sem, n_lo_ready.count(row, 3))
                normed(hi_lo("ag"), E * R, slice(0, E * R), bank[:, 0, :])
                normed(hi_lo("au"), E * R, slice(0, E * R), bank[:, 1, :]).then_inc(lora_a.sem, 1)

                gate_banks = [(2, 3), (4, 5)]

                def base(m):
                    at, width = FF_TILES[m]
                    if m >= 2:
                        pe.wait_ge(ff_prod.sem, ff_prod.count(row, FF_STEPS.index((m - 2, 2)) + 1))
                    for name, where in zip(("wg", "wu"), gate_banks[m % 2]):
                        last = normed(hi_lo(name), DFF, slice(at, at + width), bank[0:width, where, :])
                    last.then_inc(gu_ready.sem, 1)

                pe.wait_ge(l_copied.sem, l_copied.count(row, 1))
                base(0)
                for kind in range(4):
                    pe.wait_ge(spread.sem, spread.count(row, kind + 1))
                    for j in range(S // P):
                        last = nc.tensor.transpose(bank[:, 4 + kind, j * P:(j + 1) * P],
                                                   pair_tmp[kind % 2][:, j * P:(j + 1) * P], con("ident"))
                    last.then_inc(pick_t.sem, 1)

                def lora(m, v):
                    at, width = FF_TILES[m]
                    before = FF_STEPS.index((m, v - 1)) + 1
                    pe.wait_ge(ff_prod.sem, ff_prod.count(row, before))
                    if m == 0:
                        pe.wait_ge(lora_lo.sem, lora_lo.count(row, 2 * v))
                    for i, (name, where) in enumerate(zip(("bg", "bu"), gate_banks[m % 2])):
                        wh, wl = hi_lo(name)
                        ah, al = lora_hl[2 * (v - 1) + i]
                        to = bank[0:width, where, :]
                        cols = slice(at, at + width)
                        nc.tensor.matmul(to, wl[:, cols], ah, start=False, stop=False, skip_group_check=True)
                        nc.tensor.matmul(to, wh[:, cols], al, start=False, stop=False, skip_group_check=True)
                        last = nc.tensor.matmul(to, wh[:, cols], ah, start=False, stop=True, skip_group_check=True)
                    last.then_inc(gu_ready.sem, 1)

                def down(m, v):
                    n = FF_STEPS.index((m, v))
                    rows = slice(0, FF_TILES[m][1])
                    pe.wait_ge(ff_lo.sem, ff_lo.count(row, n + 1))
                    if v == 0:
                        for t in range(KT):
                            last = product(bank[:, 6 + t, :], hi_lo("wd"), slice(m * D + t * P, m * D + (t + 1) * P),
                                           ff_hl[n % 4], rows, m == 0, m == FT - 1)
                    else:
                        last = product(bank[:, v - 1, :], hi_lo("ad"), slice(m * P, (m + 1) * P),
                                       ff_hl[n % 4], rows, m == 0, m == FT - 1)
                        if m == FT - 1 and v == 2:
                            last.then_inc(z_ready.sem, 1)
                            return
                    last.then_inc(ff_used.sem, 1)

                for m in range(FT):
                    lora(m, 1)
                    if m == 0:
                        pe.wait_ge(pick_copied.sem, pick_copied.count(row, 4))
                    if m + 1 < FT:
                        base(m + 1)
                    if m:
                        down(m - 1, 2)
                    lora(m, 2)
                    down(m, 0)
                    if m == 0:
                        pe.wait_ge(lora_in.sem, lora_in.count(row, 4))
                    down(m, 1)
                down(FT - 1, 2)
                pe.wait_ge(z_steps.sem, z_steps.count(row, 3))
                for t in range(KT):
                    last = nc.tensor.matmul(bank[:, 6 + t, :], plain("bd")[:, t * P:(t + 1) * P], silu_out[0],
                                            start=False, stop=True, skip_group_check=True)
                last.then_inc(y_ready.sem, 1)


def _tiles(w):
    n_out, n_in = w.shape
    tiles = -(-n_in // P)
    t = np.zeros((tiles * P, n_out), w.dtype)
    t[:n_in] = w.T
    return t.reshape(tiles, P, n_out).transpose(1, 0, 2).reshape(P, tiles * n_out)


def _columns(v):
    v = v.reshape(-1, KT, P)
    return v.transpose(2, 1, 0).reshape(P, -1)


def _constants():
    inv_freq = (1.0 / np.float32(10000.0) ** (np.arange(0, HD, 2, dtype=np.float32) / np.float32(HD))).astype(np.float32)
    freqs = np.outer(np.arange(S, dtype=np.float32), inv_freq).astype(np.float32)
    angle = np.concatenate([freqs, freqs], -1).astype(np.float64).T
    sign = np.where(np.arange(HD) < HD // 2, -1.0, 1.0)[:, None]
    rows = np.arange(P)
    partner = rows // HD * HD + (rows % HD + HD // 2) % HD
    swap = np.zeros((P, P))
    swap[partner, rows] = 1
    head = np.zeros((P, GH))
    for part in range(PARTS):
        for r in range(32):
            head[32 * part + r, r // HD] = 1
    for i in range(GH):
        head[MROW + i, i] = 1
    before = np.tile((np.arange(E)[None, :] < np.arange(E)[:, None]).reshape(1, -1), (P, 1))
    parts = {"cos": np.tile(np.cos(angle), (P // HD, 1)), "sin": np.tile(np.sin(angle) * sign, (P // HD, 1)),
             "ident": np.eye(P), "mean": np.full((P, P), 1.0 / D), "swap": swap, "head": head, "before": before,
             "one": np.ones((P, 1))}
    return np.concatenate([parts[n] for n, _ in CONST_WIDTHS], 1).astype(np.float32)


def kernel(**inputs):
    import concourse.bacc as bacc
    from concourse.bass_utils import run_bass_kernel_spmd
    import ml_dtypes

    a = {k[3:]: np.asarray(v) for k, v in inputs.items()}
    x = a["attn_x"].transpose(0, 2, 1).reshape(B, KT, P, S).transpose(0, 2, 1, 3)
    qkv = a["attn_w_qkv"]
    split = {"qk": _tiles(qkv[:2 * D]), "v": _tiles(qkv[2 * D:]), "up": _tiles(a["attn_w_up"]),
             "ag": _tiles(a["ffn_Ag"].reshape(E * R, D)), "au": _tiles(a["ffn_Au"].reshape(E * R, D)),
             "wg": _tiles(a["ffn_Wg"]), "wu": _tiles(a["ffn_Wu"]),
             "bg": a["ffn_Bg"].transpose(0, 2, 1).reshape(E * R, DFF),
             "bu": a["ffn_Bu"].transpose(0, 2, 1).reshape(E * R, DFF),
             "wd": _tiles(a["ffn_Wd"]), "ad": _tiles(a["ffn_Ad"].reshape(E * R, DFF))}
    plain = {"o": _tiles(a["attn_w_o"]), "down": _tiles(a["attn_w_down"]),
             "bd": a["ffn_Bd"].transpose(0, 2, 1).reshape(E * R, D), "r": _tiles(a["ffn_Wr"])}
    query, key = np.arange(P)[:, None], np.arange(P)[None, :]
    masks = np.stack([np.eye(P), np.where(key > query, MASKED, 0), np.where(key > query, MASKED, 0).T], 1)
    arrays = {
        "x": x,
        "smalls": np.concatenate([_columns(a["attn_attn_norm_w"]), _columns(a["attn_ffn_norm_w"]),
                                  _columns(a["c"])], 1),
        "wmod": _tiles(a["wmod"].T),
        "wsplit": np.concatenate([split[n] for n, _ in SPLIT_WIDTHS], 1),
        "wplain": np.concatenate([plain[n] for n, _ in PLAIN_WIDTHS], 1),
        "consts": _constants(),
        "masks": masks.astype(ml_dtypes.bfloat16),
    }
    arrays = {k: np.ascontiguousarray(v) for k, v in arrays.items()}
    nc = bacc.Bacc("TRN2", target_bir_lowering=False, num_devices=1)
    args = [nc.dram_tensor(f"in_{k}", v.shape, mybir.dt.from_np(v.dtype), kind="ExternalInput").ap()
            for k, v in arrays.items()]
    out = nc.dram_tensor("out_0", (B, P, KT, S), F32, kind="ExternalOutput").ap()
    adaln_kernel(nc, *args, out)
    r = run_bass_kernel_spmd(nc, [{f"in_{k}": v for k, v in arrays.items()}], core_ids=[0])
    got = r.results[0]["out_0"]
    return got.transpose(0, 2, 1, 3).reshape(B, D, S).transpose(0, 2, 1)
```

```python
from contextlib import ExitStack

import numpy as np

import concourse.bass as bass
from concourse import mybir

ALU = mybir.AluOpType
ACT = mybir.ActivationFunctionType
F32 = mybir.dt.float32
F32R = mybir.dt.float32r
BF16 = mybir.dt.bfloat16
AX_X = mybir.AxisListType.X

P = 128
B, S, D = 4, 512, 256
KT = D // P
HEADS, HD = 32, 8
BLOCK = S // 4
INTER = 512
MT = INTER // P
DFF = 704
E, R = 8, 16
EPS = 1e-5
SCALE = float(HD) ** -0.5
LORA_SCALE = 2.0
MASKED = -1e30

GH = 4
HALF = HEADS // 2
GQ = HALF // GH
STACK_DMAS = 2 * 3 * GQ
BLOCKS = S // BLOCK
UNITS = 2 * BLOCKS
PARTS = 3
MROW = PARTS * 32
KS = MROW + GH
FF_TILES = [(m * P, min(P, DFF - m * P)) for m in range(-(-DFF // P))]
FT = len(FF_TILES)
VARIANTS = 3

SPLIT_WIDTHS = [("qk", KT * 2 * D), ("v", KT * D), ("up", KT * 2 * INTER), ("ag", KT * E * R),
                ("au", KT * E * R), ("wg", KT * DFF), ("wu", KT * DFF), ("bg", DFF), ("bu", DFF),
                ("wd", FT * D), ("ad", FT * E * R)]
PLAIN_WIDTHS = [("o", KT * D), ("down", MT * D), ("bd", D), ("r", KT * E)]
CONST_WIDTHS = [("cos", S), ("sin", S), ("ident", P), ("mean", P), ("swap", P), ("head", GH), ("before", E * E), ("one", 1)]


def layout(widths):
    places, at = {}, 0
    for name, width in widths:
        places[name] = (at, width)
        at += width
    return places, at


SPLIT, SPLIT_COLS = layout(SPLIT_WIDTHS)
PLAIN, PLAIN_COLS = layout(PLAIN_WIDTHS)
CONST, CONST_COLS = layout(CONST_WIDTHS)
CHUNK_WIDTHS = [KT * 3 * D] + 4 * [4 * S]
CHUNK_WIDTHS += [SPLIT_COLS - sum(CHUNK_WIDTHS)]
CHUNKS = [(sum(CHUNK_WIDTHS[:c]), width) for c, width in enumerate(CHUNK_WIDTHS)]
EARLY_CHUNKS = 3




def ff_steps():
    steps = [(0, 0), (1, 0), (0, 1), (0, 2)]
    for m in range(1, FT):
        steps += [(m, 1)] + ([(m + 1, 0)] if m + 1 < FT else []) + [(m, 2)]
    return steps


FF_STEPS = ff_steps()
FF_USED = [VARIANTS * m + v + 1 for m, v in FF_STEPS]


class Signal:

    def __init__(self, sem, per_row, before=0):
        self.sem, self.per_row, self.before = sem, per_row, before

    def count(self, row, k, ahead=0):
        return row * self.per_row + (self.before + k + ahead * self.per_row)


class Norm:

    def __init__(self, signals, std, rstd, where):
        (self.sum_ready, self.mean_ready, self.centred, self.sq_ready, self.square_mean, self.std_ready,
         self.rstd_ready, self.rstd_spread, self.scaled, self.shifted, self.rms_normed, self.n_hi_ready,
         self.n_lo_ready) = signals
        self.std, self.rstd, self.where = std, rstd, where


def adaln_kernel(nc, x, smalls, wmod, wsplit, wplain, consts, masks, out):
    with ExitStack() as ctx:
        def sb(name, shape, dt=F32):
            return ctx.enter_context(nc.sbuf_tensor(name, shape, dt))

        def signal(name, per_row, before=0):
            return Signal(ctx.enter_context(nc.semaphore(name)), per_row, before)

        w_hi = sb("w_hi", [P, SPLIT_COLS], F32R)
        w_lo = sb("w_lo", [P, SPLIT_COLS], F32R)
        w_plain = sb("w_plain", [P, PLAIN_COLS])
        const = sb("const", [P, CONST_COLS])
        mask = sb("mask", [P, 3, P], BF16)
        small = sb("small", [P, 2 * KT + KT * B])
        act_c = sb("act_c", [P, KT * B])
        mod_all = sb("mod_all", [P, 6 * KT, B])
        mod = sb("mod", [P, 6 * KT])
        front_mod = sb("front_mod", [P, 2 * KT])
        gate_tmp = sb("gate_tmp", [P, 2 * KT * B])
        h_next = sb("h_next", [P, KT, S])
        h = sb("h", [P, KT, S])
        n_hi = sb("n_hi", [P, KT, S], F32R)
        n_lo = sb("n_lo", [P, KT, S], F32R)
        q_st = sb("q_st", [P, HEADS // GH, S], F32R)
        k_st = sb("k_st", [P, HEADS // GH, S], F32R)
        v_ex = sb("v_ex", [P, HALF, P])
        arena = sb("arena", [P, 10, S])
        with nc.sbuf_tensor("tile_f", [P, 16, S], F32) as tile_f:
            pass
        arena_r = sb("arena_r", [P, 16, S], F32R)
        logits = sb("logits", [P, S // P, E])
        l_max = sb("l_max", [P, S // P])
        l_sum = sb("l_sum", [P, S // P])
        l_exp = sb("l_exp", [P, S // P, E])
        rank = sb("rank", [P, S // P, E])
        pick = sb("pick", [P, 2, S // P, E])
        eps_col = sb("eps_col", [P, 1])
        bank = ctx.enter_context(nc.psum_tensor("bank", [P, 8, S], F32))

        def hi_lo(name):
            at, width = SPLIT[name]
            return w_hi[:, at:at + width], w_lo[:, at:at + width]

        def plain(name):
            at, width = PLAIN[name]
            return w_plain[:, at:at + width]

        def con(name):
            at, width = CONST[name]
            return const[:, at:at + width]

        xc = arena[:, 0:2, :]
        sq = arena[:, 2:4, :]
        tile_sum = arena[:, 2, :]
        v_sb = arena[:, 4:6, :].rearrange("p a (b f) -> p (a b) f", b=2)
        ctx_n = arena[:, 6:8, :]
        den_inv = arena[0:P // 2, 8, 0:2 * P]
        neg_max = arena[:, 9, :].rearrange("p (g c) -> p g c", c=P)
        hidden = arena[:, 6:10, :]
        silu_out = [arena[:, 2 + i, :] for i in range(2)]
        pair_tmp = [arena[:, 6 + i, :] for i in range(2)]
        out_tiles = arena[:, 6:8, :]
        picks_t = [arena[:, i, :] for i in (0, 1, 8, 9)]
        qk_sb, q_cos, roped = tile_f[:, 0:2, :], tile_f[:, 2, :], tile_f[:, 4:6, :]
        prob = [tile_f[:, 8 + 2 * i:10 + 2 * i, :].rearrange("p a s -> p (a s)") for i in range(2)]
        x_res = tile_f[:, 12:14, :]
        wm = arena[:, 4:10, :].rearrange("p a s -> p (a s)")
        stages = [region.rearrange("p a s -> p (a s)") for region in (
            tile_f[:, 8:12, :], tile_f[:, 12:16, :], tile_f[:, 0:4, :], arena[:, 6:10, :], arena[:, 0:4, :],
            tile_f[:, 6:8, :])]
        k_ex = [arena_r[:, 4 * i:4 * i + 4, :].rearrange("p g (h s) -> p g h s", h=GH) for i in range(2)]
        rope_hl = [(arena_r[:, 8 + 2 * i, :], arena_r[:, 9 + 2 * i, :]) for i in range(4)]
        spread_t = [pair_tmp[0], pair_tmp[1], arena[:, 9, :], arena[:, 3, :]]
        lora_tmp = [tile_f[:, i, :] for i in (4, 6, 10, 11)]
        lora_hl = [(arena_r[:, 2 * i, :], arena_r[:, 2 * i + 1, :]) for i in range(4)]
        ff_hl = [(arena_r[:, 8 + 2 * i, :], arena_r[:, 9 + 2 * i, :]) for i in range(4)]

        x_loaded = signal("x_loaded", 16)
        small_loaded = signal("small_loaded", 0)
        wmod_loaded = signal("wmod_loaded", 0)
        const_loaded = signal("const_loaded", 0)
        mask_loaded = signal("mask_loaded", 0)
        plain_loaded = signal("plain_loaded", 0)
        chunk_loaded = [signal(f"chunk_loaded{i}", 0) for i in range(len(CHUNKS))]
        ones_set = signal("ones_set", 0)
        chunk_hi = signal("chunk_hi", 0)
        chunk_lo = signal("chunk_lo", 0)
        cond_ready = signal("cond_ready", 0)
        mod_ready = signal("mod_ready", 0)
        mod_steps = signal("mod_steps", 0)
        zeroed = signal("zeroed", 0)
        mod_row = signal("mod_row", 1)
        front, rest = [Norm(
            [signal(f"{name}_{what}", per_row) for what, per_row in (
                ("sum_ready", 1), ("mean_ready", 1), ("centred", 1), ("sq_ready", 2), ("square_mean", 2),
                ("std_ready", 2), ("rstd_ready", 2), ("rstd_spread", 2), ("scaled", 1), ("shifted", 1),
                ("rms_normed", 1), ("n_hi_ready", inputs), ("n_lo_ready", inputs))],
            sb(f"{name}_std", [P, S // P]), sb(f"{name}_rstd", [P, S // P]), where)
            for name, inputs, where in (("front", 1, 7), ("rest", 2, 2))]
        front_mod_ready = signal("front_mod_ready", 1)
        h_moved = signal("h_moved", 1)
        res_loaded = signal("res_loaded", 16)
        qk_proj = signal("qk_proj", 4)
        qk_copied = signal("qk_copied", 4)
        swapped = signal("swapped", 4)
        cos_done = signal("cos_done", 4)
        sin_done = signal("sin_done", 4)
        rope_done = signal("rope_done", 4)
        rope_hi = signal("rope_hi", 4)
        rope_lo = signal("rope_lo", 4)
        stacked = [signal(f"stacked{half}", STACK_DMAS * 16) for half in range(2)]
        v_proj = signal("v_proj", 2)
        v_copied = signal("v_copied", 2)
        k_spread = signal("k_spread", UNITS)
        v_spread = signal("v_spread", UNITS)
        s1_ready = signal("s1_ready", 2 * UNITS)
        max_done = signal("max_done", 2 * UNITS)
        max_t = signal("max_t", UNITS)
        max_rows = signal("max_rows", UNITS)
        s2_ready = signal("s2_ready", 2 * UNITS)
        exp_done = signal("exp_done", 2 * UNITS)
        den_done = signal("den_done", UNITS)
        pv_done = signal("pv_done", 2 * UNITS)
        ctx_done = signal("ctx_done", UNITS)
        o_proj = signal("o_proj", 1)
        x1_ready = signal("x1_ready", 1)
        up_ready = signal("up_ready", MT)
        up_silu = signal("up_silu", MT)
        hidden_done = signal("hidden_done", MT)
        down_ready = signal("down_ready", 1)
        d_added = signal("d_added", 1)
        x2_ready = signal("x2_ready", 1)
        route_ready = signal("route_ready", 1)
        l_copied = signal("l_copied", 1)
        l_steps = signal("l_steps", 10)
        l_exp_done = signal("l_exp_done", 1)
        l_picks = signal("l_picks", 2)
        spread = signal("spread", 4)
        pick_t = signal("pick_t", 4)
        pick_copied = signal("pick_copied", 4)
        lora_a = signal("lora_a", 1)
        lora_in = signal("lora_in", 4)
        lora_hi = signal("lora_hi", 4)
        lora_lo = signal("lora_lo", 4)
        gu_ready = signal("gu_ready", FT * VARIANTS)
        ff_silu = signal("ff_silu", FT * VARIANTS)
        ff_prod = signal("ff_prod", FT * VARIANTS)
        ff_hi = signal("ff_hi", FT * VARIANTS)
        ff_lo = signal("ff_lo", FT * VARIANTS)
        ff_used = signal("ff_used", FT * VARIANTS - 1)
        z_ready = signal("z_ready", 1)
        z_steps = signal("z_steps", 3)
        y_ready = signal("y_ready", 1)
        out_ready = signal("out_ready", 1, before=1)
        stored = signal("stored", 16, before=16)

        fills = [("s1", 0), ("s1", 1), ("t", 0)]
        for u in range(UNITS):
            for a in range(2):
                fills += [("s2", 2 * u + a)] + ([("s1", 2 * u + 2 + a)] if u + 1 < UNITS else [])
            if u + 1 < UNITS:
                fills += [("t", u + 1)]
        slot_of = {fill: n % 3 for n, fill in enumerate(fills)}
        freed_by = {"s1": max_done, "t": max_rows, "s2": exp_done}

        def slot(fill):
            return bank[:, 2 * slot_of[fill]:2 * slot_of[fill] + 2, :]

        def diagonal(flat, first):
            step = P + HD
            whole = flat[:, first:first + 7 * step + HD]
            return bass.AP(whole.tensor, whole.offset, [whole.ap[0], [step, 8], [1, HD]])

        block = ctx.enter_context(nc.Block())

        @block.sync
        def _(sp):
            def load_chunk(c):
                at, width = CHUNKS[c]
                sp.dma_start(stages[c][:, 0:width], wsplit[:, at:at + width]).then_inc(chunk_loaded[c].sem, 16)

            sp.dma_start(h_next[:], x[0]).then_inc(x_loaded.sem, 16)
            sp.dma_start(small[:], smalls).then_inc(small_loaded.sem, 16)
            sp.dma_start(const[:], consts).then_inc(const_loaded.sem, 16)
            sp.dma_start(wm, wmod).then_inc(wmod_loaded.sem, 16)
            for c in (0, 1, 2, 5):
                load_chunk(c)
            sp.dma_start(mask[:], masks).then_inc(mask_loaded.sem, 16)
            sp.wait_ge(mod_ready.sem, 1)
            load_chunk(3)
            sp.dma_start(w_plain[:], wplain).then_inc(plain_loaded.sem, 16)
            sp.wait_ge(front.n_lo_ready.sem, 1)
            load_chunk(4)

            def load(to, row, loaded):
                sp.dma_start(to, x[bass.ds(row, 1)].rearrange("b p t s -> p (b t) s")).then_inc(loaded.sem, 16)

            def stack(row, ahead):
                for i in range(4):
                    half, is_k = i // 2, i % 2
                    sp.wait_ge(rope_hi.sem, rope_hi.count(row, i + 1, ahead))
                    sp.wait_ge(rope_lo.sem, rope_lo.count(row, i + 1, ahead))
                    hi, lo = rope_hl[i]
                    dest = k_st if is_k else q_st
                    for part, src in enumerate((hi, lo, hi) if is_k else (hi, hi, lo)):
                        for gq in range(GQ):
                            sp.dma_start(dest[32 * part:32 * part + 32, half * GQ + gq, :].bitcast(F32),
                                         src[32 * gq:32 * gq + 32, :].bitcast(F32)).then_inc(stacked[half].sem, 16)

            def row_steps(row, last):
                if not last:
                    sp.wait_ge(h_moved.sem, h_moved.count(row, 1))
                    load(h_next[:], row + 1, x_loaded)
                sp.wait_ge(out_ready.sem, out_ready.count(row, 0))
                sp.wait_ge(stacked[1].sem, stacked[1].count(row, STACK_DMAS * 16))
                load(x_res, row, res_loaded)
                if not last:
                    stack(row, 1)
                sp.wait_ge(out_ready.sem, out_ready.count(row, 1))
                sp.dma_start(out[bass.ds(row, 1)].rearrange("b p t s -> p (b t) s"), out_tiles)\
                    .then_inc(stored.sem, 16)

            stack(0, 0)
            with sp.Fori(0, B - 1) as row:
                row_steps(row, False)
            row_steps(B - 1, True)
            sp.wait_ge(stored.sem, stored.count(B - 1, 16))

        @block.gpsimd
        def _(pool):
            def tile_sums(norm, src):
                nc.gpsimd.tensor_tensor(tile_sum, src[:, 0, :], src[:, 1, :], ALU.add).then_inc(norm.sum_ready.sem, 1)

            def rope_cos(row, i, ahead):
                pool.wait_ge(qk_copied.sem, qk_copied.count(row, i + 1, ahead))
                if i:
                    pool.wait_ge(rope_done.sem, rope_done.count(row, i, ahead))
                nc.gpsimd.tensor_tensor(q_cos, qk_sb[:, i % 2, :], con("cos"), ALU.mult).then_inc(cos_done.sem, 1)

            def spread_keys(row, u, ahead):
                blk, half = u % BLOCKS, u // BLOCKS
                if u in (0, BLOCKS):
                    pool.wait_ge(stacked[half].sem, stacked[half].count(row, STACK_DMAS * 16, ahead))
                if u == 0 and ahead:
                    pool.wait_ge(gu_ready.sem, gu_ready.count(row, FT * VARIANTS))
                if u >= 2:
                    pool.wait_ge(s2_ready.sem, s2_ready.count(row, 2 * (u - 1)))
                src = k_st[0:KS, half * GQ:(half + 1) * GQ, blk * P:(blk + 1) * P].bitcast(F32)
                nc.gpsimd.tensor_tensor(k_ex[u % 2][0:KS, :, 0, :], src,
                                        con("head")[0:KS, 0:1].unsqueeze(2).broadcast_to([KS, GQ, P]), ALU.mult)
                for hh in range(1, GH):
                    last = nc.gpsimd.tensor_scalar(k_ex[u % 2][0:KS, :, hh, :], src,
                                                   con("head")[0:KS, hh:hh + 1], 1.0, ALU.mult, ALU.mult)
                last.then_inc(k_spread.sem, 1)

            def spread_values(row, u, ahead):
                blk, half = u % BLOCKS, u // BLOCKS
                if u in (0, 2):
                    pool.wait_ge(v_copied.sem, v_copied.count(row, u // 2 + 1, ahead))
                if u:
                    pool.wait_ge(pv_done.sem, pv_done.count(row, 2 * u))
                elif ahead:
                    pool.wait_ge(pv_done.sem, pv_done.count(row, 2 * UNITS))
                values = v_sb[:, blk, half * P:(half + 1) * P].rearrange("p (a j d) -> p a j d", a=2, d=HD)
                for a in range(2):
                    flat = v_ex[:, 8 * a:8 * a + 8, :].rearrange("p j c -> p (j c)")
                    last = nc.gpsimd.tensor_tensor(diagonal(flat, 0), values[:, a],
                                                   con("one").unsqueeze(2).broadcast_to([P, 8, HD]), ALU.mult)
                last.then_inc(v_spread.sem, 1)

            def first_units(row, ahead):
                pool.wait_ge(rope_lo.sem, rope_lo.count(row, 4, ahead))
                for u in range(2):
                    spread_keys(row, u, ahead)
                spread_values(row, 0, ahead)

            def row_steps(row, last):
                for u in range(UNITS):
                    if 2 <= u + 1 < UNITS:
                        spread_keys(row, u + 1, 0)
                    if u:
                        spread_values(row, u, 0)
                    elif not last:
                        pool.wait_ge(x_loaded.sem, x_loaded.count(row, 16, 1))
                        pool.wait_ge(out_ready.sem, out_ready.count(row, 0))
                        tile_sums(front, h_next)
                if not last:
                    rope_cos(row, 0, 1)
                pool.wait_ge(x2_ready.sem, x2_ready.count(row, 1))
                tile_sums(rest, h)
                if not last:
                    for i in range(1, 4):
                        rope_cos(row, i, 1)
                    first_units(row, 1)

            pool.wait_ge(x_loaded.sem, 16)
            tile_sums(front, h_next)
            pool.wait_ge(front.sum_ready.sem, 1)
            nc.gpsimd.memset(k_st[MROW:P, :, :].bitcast(F32), 1.0).then_inc(ones_set.sem, 1)
            pool.wait_ge(ones_set.sem, 1)
            nc.gpsimd.memset(v_ex[:], 0.0).then_inc(ones_set.sem, 1)
            pool.wait_ge(ones_set.sem, 2)
            for a in range(2):
                flat = v_ex[:, 8 * a:8 * a + 8, :].rearrange("p j c -> p (j c)")
                nc.gpsimd.memset(diagonal(flat, P // 2), 1.0).then_inc(ones_set.sem, 1)
            pool.wait_ge(chunk_lo.sem, EARLY_CHUNKS)
            for i in range(4):
                rope_cos(0, i, 0)
            pool.wait_ge(ones_set.sem, 4)
            pool.wait_ge(chunk_lo.sem, len(CHUNKS))
            first_units(0, 0)
            with pool.Fori(0, B - 1) as row:
                row_steps(row, False)
            row_steps(B - 1, True)

        @block.scalar
        def _(act):
            act.wait_ge(small_loaded.sem, 16)
            nc.scalar.activation(act_c[:], small[:, 2 * KT:], ACT.Silu).then_inc(cond_ready.sem, 1)

            def chunk_highs(chunks):
                for c in chunks:
                    at, width = CHUNKS[c]
                    act.wait_ge(chunk_loaded[c].sem, 16)
                    nc.scalar.copy(w_hi[:, at:at + width], stages[c][:, 0:width]).then_inc(chunk_hi.sem, 1)

            def squares(norm, n, src):
                for t in range(KT):
                    last = nc.scalar.activation(sq[:, t, :], src[:, t, :], ACT.Square)
                last.then_inc(norm.sq_ready.sem, 1)

            def deviation(norm, row, n, ahead):
                act.wait_ge(norm.square_mean.sem, norm.square_mean.count(row, n + 1, ahead))
                nc.scalar.activation(norm.std[:], bank[:, norm.where, 0:S // P], ACT.Sqrt, bias=eps_col[:])\
                    .then_inc(norm.std_ready.sem, 1)

            def shift(norm, row, ahead, to, src, columns):
                act.wait_ge(norm.scaled.sem, norm.scaled.count(row, 1, ahead))
                for t in range(KT):
                    last = nc.scalar.activation(to[:, t, :], src[:, t, :], ACT.Identity, bias=columns[:, t:t + 1])
                last.then_inc(norm.shifted.sem, 1)
                act.wait_ge(norm.shifted.sem, norm.shifted.count(row, 1, ahead))

            def front_squares(row, n, ahead):
                if n == 0:
                    act.wait_ge(front.centred.sem, front.centred.count(row, 1, ahead))
                else:
                    shift(front, row, ahead, h_next, h_next, front_mod[:, 0:KT])
                squares(front, n, h_next)

            def copy_qk(row, i, ahead):
                act.wait_ge(qk_proj.sem, qk_proj.count(row, i + 1, ahead))
                if i >= 2:
                    act.wait_ge(swapped.sem, swapped.count(row, i - 1, ahead))
                    act.wait_ge(cos_done.sem, cos_done.count(row, i - 1, ahead))
                nc.scalar.copy(qk_sb[:, i % 2, :], bank[:, 3 + i % 2, :]).then_inc(qk_copied.sem, 1)

            def rope_high(row, i, ahead):
                act.wait_ge(rope_done.sem, rope_done.count(row, i + 1, ahead))
                nc.scalar.copy(rope_hl[i][0], roped[:, i % 2, :]).then_inc(rope_hi.sem, 1)

            def copy_v(row, i, ahead):
                act.wait_ge(v_proj.sem, v_proj.count(row, i + 1, ahead))
                nc.scalar.copy(arena[:, 4 + i, :], bank[:, 7 if i == 0 else 1, :]).then_inc(v_copied.sem, 1)

            def front_projections(row, ahead):
                act.wait_ge(front.rms_normed.sem, front.rms_normed.count(row, 1, ahead))
                nc.scalar.copy(n_hi[:], xc[:]).then_inc(front.n_hi_ready.sem, 1)
                copy_qk(row, 0, ahead)
                copy_qk(row, 1, ahead)
                rope_high(row, 0, ahead)
                copy_qk(row, 2, ahead)
                rope_high(row, 1, ahead)
                if ahead:
                    nc.scalar.preload_act_table(ACT.Sqrt)
                    act.wait_ge(rest.centred.sem, rest.centred.count(row, 1))
                    squares(rest, 1, xc)
                copy_qk(row, 3, ahead)
                rope_high(row, 2, ahead)
                if ahead:
                    deviation(rest, row, 1, 0)
                copy_v(row, 0, ahead)
                rope_high(row, 3, ahead)
                copy_v(row, 1, ahead)

            def max_to_rows(row, u):
                blk, half = u % BLOCKS, u // BLOCKS
                act.wait_ge(max_t.sem, max_t.count(row, u + 1))
                src = slot(("t", u))[MROW:KS, 0, :].rearrange("p (g s) -> p g s", s=P)
                nc.scalar.copy(q_st[MROW:KS, half * GQ:(half + 1) * GQ, blk * P:(blk + 1) * P], src)\
                    .then_inc(max_rows.sem, 1)

            def row_steps(row, last):
                act.wait_ge(out_ready.sem, out_ready.count(row, 0))
                act.wait_ge(front.shifted.sem, front.shifted.count(row, 1))
                nc.scalar.copy(h[:], h_next[:]).then_inc(h_moved.sem, 1)
                max_to_rows(row, 0)
                for u in range(UNITS):
                    if not last and u in (4, 7):
                        deviation(front, row, 0 if u == 4 else 1, 1)
                    for a in range(2):
                        n = 2 * u + a
                        act.wait_ge(s2_ready.sem, s2_ready.count(row, n + 1))
                        if n >= 2:
                            act.wait_ge(pv_done.sem, pv_done.count(row, n - 1))
                        nc.scalar.activation(prob[a], slot(("s2", n)).rearrange("p a s -> p (a s)"),
                                             ACT.Exp, scale=SCALE).then_inc(exp_done.sem, 1)
                    if u + 1 < UNITS:
                        max_to_rows(row, u + 1)
                    if not last and u in (2, 5):
                        front_squares(row, 0 if u == 2 else 1, 1)
                nc.scalar.preload_act_table(ACT.Sqrt)
                act.wait_ge(x1_ready.sem, x1_ready.count(row, 1))
                squares(rest, 0, h)
                deviation(rest, row, 0, 0)
                act.wait_ge(rest.rms_normed.sem, rest.rms_normed.count(row, 1))
                nc.scalar.copy(n_hi[:], xc[:]).then_inc(rest.n_hi_ready.sem, 1)
                for m in range(MT):
                    act.wait_ge(up_ready.sem, up_ready.count(row, m + 1))
                    if m >= 2:
                        act.wait_ge(hidden_done.sem, hidden_done.count(row, m - 1))
                    nc.scalar.activation(silu_out[m % 2], bank[:, 3 + 2 * (m % 2), :], ACT.Silu).then_inc(up_silu.sem, 1)
                if last:
                    nc.scalar.preload_act_table(ACT.Sqrt)
                    act.wait_ge(rest.centred.sem, rest.centred.count(row, 1))
                    squares(rest, 1, xc)
                    deviation(rest, row, 1, 0)
                else:
                    front_projections(row, 1)
                shift(rest, row, 0, xc, xc, mod[:, 3 * KT:4 * KT])
                nc.scalar.copy(n_hi[:], xc[:]).then_inc(rest.n_hi_ready.sem, 1)
                act.wait_ge(l_steps.sem, l_steps.count(row, 2))
                nc.scalar.activation(l_exp[:], l_exp[:], ACT.Exp).then_inc(l_exp_done.sem, 1)
                nc.scalar.preload_act_table(ACT.Silu)
                def gate_silu(n):
                    m, v = FF_STEPS[n]
                    width = FF_TILES[m][1]
                    act.wait_ge(gu_ready.sem, gu_ready.count(row, n + 1))
                    if n >= 2:
                        act.wait_ge(ff_prod.sem, ff_prod.count(row, n - 1))
                    nc.scalar.activation(silu_out[n % 2][0:width], bank[0:width, 2 + 2 * (m % 2), :], ACT.Silu)\
                        .then_inc(ff_silu.sem, 1)

                def product_high(j):
                    width = FF_TILES[FF_STEPS[j][0]][1]
                    act.wait_ge(ff_prod.sem, ff_prod.count(row, j + 1))
                    if j >= 4:
                        act.wait_ge(ff_used.sem, ff_used.count(row, FF_USED[j - 4]))
                    else:
                        if j == 1:
                            act.wait_ge(lora_lo.sem, lora_lo.count(row, 4))
                        if j % 2 == 0 and not last:
                            act.wait_ge(stacked[j // 2].sem, stacked[j // 2].count(row, STACK_DMAS * 16, 1))
                    nc.scalar.copy(ff_hl[j % 4][0][0:width], pair_tmp[j % 2][0:width]).then_inc(ff_hi.sem, 1)

                def copy_pick(kind):
                    act.wait_ge(pick_t.sem, pick_t.count(row, kind + 1))
                    nc.scalar.copy(picks_t[kind], bank[:, 6 + kind % 2, :]).then_inc(pick_copied.sem, 1)

                gate_silu(0)
                act.wait_ge(rest.n_lo_ready.sem, rest.n_lo_ready.count(row, 2))
                copy_pick(0)
                copy_pick(1)
                for i in range(4):
                    if i == 2:
                        act.wait_ge(lora_lo.sem, lora_lo.count(row, 2))
                        product_high(0)
                        copy_pick(2)
                        copy_pick(3)
                    act.wait_ge(lora_in.sem, lora_in.count(row, i + 1))
                    nc.scalar.copy(lora_hl[i][0], lora_tmp[i]).then_inc(lora_hi.sem, 1)
                gate_silu(1)
                for n in range(2, len(FF_STEPS)):
                    gate_silu(n)
                    product_high(n - 1)
                product_high(len(FF_STEPS) - 1)

            act.wait_ge(zeroed.sem, 1)
            front_squares(0, 0, 0)
            deviation(front, 0, 0, 0)
            chunk_highs(range(EARLY_CHUNKS))
            front_squares(0, 1, 0)
            deviation(front, 0, 1, 0)
            front_projections(0, 0)
            chunk_highs(range(EARLY_CHUNKS, len(CHUNKS)))
            with act.Fori(0, B - 1) as row:
                row_steps(row, False)
            row_steps(B - 1, True)

        @block.vector
        def _(dve):
            nc.vector.memset(eps_col[:], EPS).then_inc(zeroed.sem, 1)
            nc.vector.memset(l_max[:], 0.0).then_inc(stored.sem, 16)
            nc.vector.memset(mod[:], 0.0).then_inc(out_ready.sem, 1)
            def modulation():
                dve.wait_ge(mod_ready.sem, 1)
                mod_ps = bank[:, 0, 0:6 * KT * B].rearrange("p (c b) -> p c b", b=B)
                nc.vector.tensor_copy(mod_all[:], mod_ps).then_inc(mod_steps.sem, 1)
                dve.wait_ge(mod_steps.sem, 1)
                for n, c in enumerate((1, 4)):
                    part = mod_all[:, c * KT:(c + 1) * KT, :]
                    nc.vector.tensor_scalar(part, part, 1.0, None, ALU.add).then_inc(mod_steps.sem, 1)
                for n, c in enumerate((2, 5)):
                    part = mod_all[:, c * KT:(c + 1) * KT, :]
                    sign = gate_tmp[:, n * KT * B:(n + 1) * KT * B].rearrange("p (t b) -> p t b", b=B)
                    nc.vector.tensor_scalar(sign, part, 0.0, 2.0, ALU.is_ge, ALU.mult).then_inc(mod_steps.sem, 1)
                    dve.wait_ge(mod_steps.sem, 4 + 4 * n)
                    nc.vector.scalar_tensor_tensor(part, part, -1.0, part, ALU.mult, ALU.max).then_inc(mod_steps.sem, 1)
                    dve.wait_ge(mod_steps.sem, 5 + 4 * n)
                    nc.vector.tensor_scalar(part, part, 0.25, None, ALU.max).then_inc(mod_steps.sem, 1)
                    dve.wait_ge(mod_steps.sem, 6 + 4 * n)
                    nc.vector.scalar_tensor_tensor(part, sign, -1.0, part, ALU.add, ALU.mult).then_inc(mod_steps.sem, 1)
                dve.wait_ge(mod_steps.sem, 11)

            def chunk_lows(chunks):
                for c in chunks:
                    at, width = CHUNKS[c]
                    dve.wait_ge(chunk_hi.sem, c + 1)
                    nc.vector.tensor_tensor(w_lo[:, at:at + width], stages[c][:, 0:width],
                                            w_hi[:, at:at + width].bitcast(F32), ALU.subtract).then_inc(chunk_lo.sem, 1)

            def centre(norm, row, ahead, to, src):
                dve.wait_ge(norm.mean_ready.sem, norm.mean_ready.count(row, 1, ahead))
                for t in range(KT):
                    last = nc.vector.tensor_tensor(to[:, t, :], src[:, t, :], bank[:, norm.where, :], ALU.subtract)
                last.then_inc(norm.centred.sem, 1)

            def inverse(norm, row, n, ahead):
                dve.wait_ge(norm.std_ready.sem, norm.std_ready.count(row, n + 1, ahead))
                nc.vector.reciprocal(norm.rstd[:], norm.std[:]).then_inc(norm.rstd_ready.sem, 1)

            def scale(norm, row, n, ahead, to, src, columns, done):
                dve.wait_ge(norm.rstd_spread.sem, norm.rstd_spread.count(row, n + 1, ahead))
                for t in range(KT):
                    last = nc.vector.scalar_tensor_tensor(to[:, t, :], src[:, t, :], columns[:, t:t + 1],
                                                          bank[:, norm.where, :], ALU.mult, ALU.mult)
                last.then_inc(done.sem, 1)

            def n_lows(norm, row, n, ahead):
                dve.wait_ge(norm.n_hi_ready.sem, norm.n_hi_ready.count(row, n + 1, ahead))
                nc.vector.tensor_tensor(n_lo[:], xc[:], n_hi[:].bitcast(F32), ALU.subtract)\
                    .then_inc(norm.n_lo_ready.sem, 1)

            def front_modulation(row, ahead):
                nc.vector.tensor_copy(front_mod[:], mod_all[:, 0:2 * KT, bass.ds(row + ahead, 1)]
                                      .rearrange("p c b -> p (c b)")).then_inc(front_mod_ready.sem, 1)

            def front_scale(row, ahead):
                dve.wait_ge(front_mod_ready.sem, front_mod_ready.count(row, 1, ahead))
                scale(front, row, 0, ahead, h_next, h_next, front_mod[:, KT:2 * KT], front.scaled)

            def front_rms(row, ahead):
                dve.wait_ge(front.shifted.sem, front.shifted.count(row, 1, ahead))
                scale(front, row, 1, ahead, xc, h_next, small[:, 0:KT], front.rms_normed)
                dve.wait_ge(front.rms_normed.sem, front.rms_normed.count(row, 1, ahead))
                n_lows(front, row, 0, ahead)

            def rope_sin(row, i, ahead):
                dve.wait_ge(swapped.sem, swapped.count(row, i + 1, ahead))
                if i >= 2:
                    dve.wait_ge(rope_lo.sem, rope_lo.count(row, i - 1, ahead))
                nc.vector.tensor_tensor(roped[:, i % 2, :], bank[:, 5 + i % 2, :], con("sin"), ALU.mult)\
                    .then_inc(sin_done.sem, 1)

            def rope_add(row, i, ahead):
                dve.wait_ge(cos_done.sem, cos_done.count(row, i + 1, ahead))
                dve.wait_ge(sin_done.sem, sin_done.count(row, i + 1, ahead))
                nc.vector.tensor_tensor(roped[:, i % 2, :], roped[:, i % 2, :], q_cos, ALU.add)\
                    .then_inc(rope_done.sem, 1)

            def rope_low(row, i, ahead):
                dve.wait_ge(rope_hi.sem, rope_hi.count(row, i + 1, ahead))
                nc.vector.tensor_tensor(rope_hl[i][1], roped[:, i % 2, :], rope_hl[i][0].bitcast(F32),
                                        ALU.subtract).then_inc(rope_lo.sem, 1)

            def front_rope(row, ahead):
                rope_sin(row, 0, ahead)
                rope_add(row, 0, ahead)
                rope_sin(row, 1, ahead)
                rope_low(row, 0, ahead)
                rope_add(row, 1, ahead)
                if ahead:
                    centre(rest, row, 0, xc, h)
                rope_sin(row, 2, ahead)
                rope_low(row, 1, ahead)
                rope_add(row, 2, ahead)
                if ahead:
                    inverse(rest, row, 1, 0)
                rope_low(row, 2, ahead)
                rope_sin(row, 3, ahead)
                rope_add(row, 3, ahead)
                dve.wait_ge(rope_done.sem, rope_done.count(row, 4, ahead))
                rope_low(row, 3, ahead)

            def row_steps(row, is_last):
                dve.wait_ge(out_ready.sem, out_ready.count(row, 0))
                nc.vector.tensor_copy(mod[:], mod_all[:, :, bass.ds(row, 1)].rearrange("p c b -> p (c b)"))\
                    .then_inc(mod_row.sem, 1)

                def unit_max(u):
                    if u:
                        dve.wait_ge(max_t.sem, max_t.count(row, u))
                    for a in range(2):
                        n = 2 * u + a
                        dve.wait_ge(s1_ready.sem, s1_ready.count(row, n + 1))
                        nc.vector.tensor_reduce(neg_max[:, 2 * a:2 * a + 2, MROW:KS],
                                                slot(("s1", n)).rearrange("p a (h s) -> p a h s", s=P),
                                                AX_X, ALU.max, negate=True).then_inc(max_done.sem, 1)

                def normalise(u):
                    blk, half = u % BLOCKS, u // BLOCKS
                    acc = bank[:, 6, 0:2 * P]
                    dve.wait_ge(pv_done.sem, pv_done.count(row, 2 * u + 2))
                    if u == 0:
                        dve.wait_ge(stored.sem, stored.count(row, 0))
                    else:
                        dve.wait_ge(ctx_done.sem, ctx_done.count(row, u))
                    nc.vector.reciprocal(den_inv, acc[P // 2:P, :]).then_inc(den_done.sem, 1)
                    dve.wait_ge(den_done.sem, den_done.count(row, u + 1))
                    for a in range(2):
                        last = nc.vector.tensor_tensor(ctx_n[64 * a:64 * a + 64, half, blk * P:(blk + 1) * P],
                                                       acc[0:64, a * P:(a + 1) * P], den_inv[:, a * P:(a + 1) * P],
                                                       ALU.mult)
                    last.then_inc(ctx_done.sem, 1)

                unit_max(0)
                for u in range(UNITS):
                    if u + 1 < UNITS:
                        unit_max(u + 1)
                    if not is_last:
                        if u == 0:
                            dve.wait_ge(front.shifted.sem, front.shifted.count(row, 1))
                            front_modulation(row, 1)
                        elif u == 2:
                            centre(front, row, 1, h_next, h_next)
                        elif u == 4:
                            inverse(front, row, 0, 1)
                        elif u == 5:
                            front_scale(row, 1)
                        elif u == 7:
                            inverse(front, row, 1, 1)
                    normalise(u)
                dve.wait_ge(o_proj.sem, o_proj.count(row, 1))
                dve.wait_ge(h_moved.sem, h_moved.count(row, 1))
                nc.vector.tensor_tensor(h[:], h[:], bank[:, 0:2, :], ALU.add).then_inc(x1_ready.sem, 1)
                dve.wait_ge(x1_ready.sem, x1_ready.count(row, 1))
                inverse(rest, row, 0, 0)
                scale(rest, row, 0, 0, xc, h, small[:, KT:2 * KT], rest.rms_normed)
                dve.wait_ge(rest.rms_normed.sem, rest.rms_normed.count(row, 1))
                n_lows(rest, row, 0, 0)
                for m in range(MT):
                    dve.wait_ge(up_silu.sem, up_silu.count(row, m + 1))
                    nc.vector.tensor_tensor(hidden[:, m, :], silu_out[m % 2], bank[:, 4 + 2 * (m % 2), :], ALU.mult)\
                        .then_inc(hidden_done.sem, 1)
                if not is_last:
                    dve.wait_ge(rest.n_lo_ready.sem, rest.n_lo_ready.count(row, 1))
                    front_rms(row, 1)
                dve.wait_ge(down_ready.sem, down_ready.count(row, 1))
                nc.vector.tensor_tensor(h[:], h[:], bank[:, 0:2, :], ALU.add).then_inc(d_added.sem, 1)
                dve.wait_ge(d_added.sem, d_added.count(row, 1))
                dve.wait_ge(res_loaded.sem, res_loaded.count(row, 16))
                dve.wait_ge(mod_row.sem, mod_row.count(row, 1))
                for t in range(KT):
                    last = nc.vector.scalar_tensor_tensor(h[:, t, :], h[:, t, :], mod[:, 2 * KT + t:2 * KT + t + 1],
                                                          x_res[:, t, :], ALU.mult, ALU.add)
                last.then_inc(x2_ready.sem, 1)
                dve.wait_ge(x2_ready.sem, x2_ready.count(row, 1))
                if is_last:
                    centre(rest, row, 0, xc, h)
                    inverse(rest, row, 1, 0)
                else:
                    dve.wait_ge(front.n_lo_ready.sem, front.n_lo_ready.count(row, 1, 1))
                    front_rope(row, 1)
                scale(rest, row, 1, 0, xc, xc, mod[:, 4 * KT:5 * KT], rest.scaled)
                n_lows(rest, row, 1, 0)

                steps = [0]

                def step(ins):
                    steps[0] += 1
                    ins.then_inc(l_steps.sem, 1)
                    return steps[0]

                def after(n):
                    dve.wait_ge(l_steps.sem, l_steps.count(row, n))

                dve.wait_ge(route_ready.sem, route_ready.count(row, 1))
                nc.vector.tensor_copy(logits[:], bank[:, 3, 0:S // P * E].rearrange("p (j e) -> p j e", e=E))\
                    .then_inc(l_copied.sem, 1)
                dve.wait_ge(l_copied.sem, l_copied.count(row, 1))
                after(step(nc.vector.tensor_reduce(l_max[:], logits[:], AX_X, ALU.max)))
                step(nc.vector.tensor_tensor(l_exp[:], logits[:], l_max[:].unsqueeze(2).broadcast_to([P, S // P, E]),
                                             ALU.subtract))
                wide = [t.rearrange("p (j e f) -> p j e f", j=8, e=8)[:, 0:S // P] for t in pair_tmp]
                other = logits[:].unsqueeze(2).broadcast_to([P, S // P, E, E])
                own = logits[:].unsqueeze(3).broadcast_to([P, S // P, E, E])
                before = con("before").rearrange("p (e f) -> p e f", f=E).unsqueeze(1).broadcast_to([P, S // P, E, E])
                step(nc.vector.tensor_tensor(wide[0], other, own, ALU.is_gt))
                after(step(nc.vector.tensor_tensor(wide[1], other, own, ALU.is_equal)))
                after(step(nc.vector.tensor_tensor(wide[1], wide[1], before, ALU.mult)))
                after(step(nc.vector.tensor_tensor(wide[0], wide[0], wide[1], ALU.add)))
                after(step(nc.vector.tensor_reduce(rank[:], wide[0], AX_X, ALU.add)))
                dve.wait_ge(l_exp_done.sem, l_exp_done.count(row, 1))
                after(step(nc.vector.tensor_reduce(l_sum[:], l_exp[:], AX_X, ALU.add)))
                after(step(nc.vector.reciprocal(l_max[:], l_sum[:])))
                step(nc.vector.tensor_tensor(l_exp[:], l_exp[:], l_max[:].unsqueeze(2).broadcast_to([P, S // P, E]),
                                             ALU.mult))
                def spread_to(kind):
                    return spread_t[kind].rearrange("p (j e r) -> p j e r", j=S // P, r=R)

                def over_ranks(t):
                    return t.unsqueeze(3).broadcast_to([P, S // P, E, R])

                after(steps[0])
                nc.vector.tensor_scalar(pick[:, 0], rank[:], 0.0, LORA_SCALE, ALU.is_equal, ALU.mult)\
                    .then_inc(l_picks.sem, 1)
                nc.vector.tensor_scalar(pick[:, 1], rank[:], 1.0, LORA_SCALE, ALU.is_equal, ALU.mult)\
                    .then_inc(l_picks.sem, 1)
                dve.wait_ge(l_picks.sem, l_picks.count(row, 2))
                nc.vector.tensor_copy(spread_to(0), over_ranks(pick[:, 0])).then_inc(spread.sem, 1)
                nc.vector.tensor_tensor(spread_to(1), over_ranks(pick[:, 1]), over_ranks(pick[:, 0]), ALU.subtract)\
                    .then_inc(spread.sem, 1)
                for k in range(2):
                    nc.vector.tensor_tensor(spread_to(2 + k), over_ranks(pick[:, k]), over_ranks(l_exp[:]), ALU.mult)\
                        .then_inc(spread.sem, 1)

                def lora_input(i):
                    gate_up, kind = i % 2, i // 2
                    dve.wait_ge(pick_copied.sem, pick_copied.count(row, kind + 1))
                    nc.vector.tensor_tensor(lora_tmp[i], picks_t[kind], bank[:, gate_up, :], ALU.mult)\
                        .then_inc(lora_in.sem, 1)

                def lora_low(i):
                    dve.wait_ge(lora_hi.sem, lora_hi.count(row, i + 1))
                    nc.vector.tensor_tensor(lora_hl[i][1], lora_tmp[i], lora_hl[i][0].bitcast(F32), ALU.subtract)\
                        .then_inc(lora_lo.sem, 1)

                def ff_low(j):
                    width = FF_TILES[FF_STEPS[j][0]][1]
                    dve.wait_ge(ff_hi.sem, ff_hi.count(row, j + 1))
                    nc.vector.tensor_tensor(ff_hl[j % 4][1][0:width], pair_tmp[j % 2][0:width],
                                            ff_hl[j % 4][0][0:width].bitcast(F32), ALU.subtract)\
                        .then_inc(ff_lo.sem, 1)

                def ff_product(n):
                    m = FF_STEPS[n][0]
                    width = FF_TILES[m][1]
                    dve.wait_ge(ff_silu.sem, ff_silu.count(row, n + 1))
                    if n >= 2:
                        dve.wait_ge(ff_lo.sem, ff_lo.count(row, n - 1))
                    else:
                        dve.wait_ge(pick_t.sem, pick_t.count(row, n + 1))
                    nc.vector.tensor_tensor(pair_tmp[n % 2][0:width], silu_out[n % 2][0:width],
                                            bank[0:width, 3 + 2 * (m % 2), :], ALU.mult).then_inc(ff_prod.sem, 1)

                dve.wait_ge(lora_a.sem, lora_a.count(row, 1))
                if not is_last:
                    dve.wait_ge(stacked[0].sem, stacked[0].count(row, STACK_DMAS * 16, 1))
                ff_product(0)
                for kind in range(2):
                    lora_input(2 * kind)
                    lora_input(2 * kind + 1)
                    lora_low(2 * kind)
                    lora_low(2 * kind + 1)
                    if kind == 0:
                        ff_low(0)
                ff_product(1)
                for n in range(2, len(FF_STEPS)):
                    if n > 2:
                        ff_low(n - 2)
                    ff_product(n)
                ff_low(len(FF_STEPS) - 2)
                ff_low(len(FF_STEPS) - 1)
                dve.wait_ge(z_ready.sem, z_ready.count(row, 1))
                for k in range(2):
                    nc.vector.tensor_tensor(silu_out[k], picks_t[2 + k], bank[:, k, :], ALU.mult)\
                        .then_inc(z_steps.sem, 1)
                dve.wait_ge(z_steps.sem, z_steps.count(row, 2))
                nc.vector.tensor_tensor(silu_out[0], silu_out[0], silu_out[1], ALU.add).then_inc(z_steps.sem, 1)
                dve.wait_ge(y_ready.sem, y_ready.count(row, 1))
                for t in range(KT):
                    last = nc.vector.scalar_tensor_tensor(pair_tmp[t], bank[:, 6 + t, :],
                                                          mod[:, 5 * KT + t:5 * KT + t + 1], h[:, t, :],
                                                          ALU.mult, ALU.add)
                last.then_inc(out_ready.sem, 1)

            centre(front, 0, 0, h_next, h_next)
            inverse(front, 0, 0, 0)
            chunk_lows(range(EARLY_CHUNKS))
            modulation()
            front_modulation(0, 0)
            front_scale(0, 0)
            inverse(front, 0, 1, 0)
            front_rms(0, 0)
            front_rope(0, 0)
            chunk_lows(range(EARLY_CHUNKS, len(CHUNKS)))
            with dve.Fori(0, B - 1) as row:
                row_steps(row, False)
            row_steps(B - 1, True)

        @block.tensor
        def _(pe):
            def product(to, w, w_cols, acts, rows, start, stop):
                (wh, wl), (ah, al) = w, acts
                nc.tensor.matmul(to, wl[rows, w_cols], ah[rows], start=start, stop=False)
                nc.tensor.matmul(to, wh[rows, w_cols], al[rows], start=False, stop=False)
                return nc.tensor.matmul(to, wh[rows, w_cols], ah[rows], start=False, stop=stop)

            def normed(w, width, cols, to):
                for kt in range(KT):
                    last = product(to, w, slice(kt * width + cols.start, kt * width + cols.stop),
                                   (n_hi[:, kt, :], n_lo[:, kt, :]), slice(0, P), kt == 0, kt == KT - 1)
                return last

            def mean(norm, row, ahead):
                pe.wait_ge(norm.sum_ready.sem, norm.sum_ready.count(row, 1, ahead))
                nc.tensor.matmul(bank[:, norm.where, :], con("mean"), tile_sum, start=True, stop=True)\
                    .then_inc(norm.mean_ready.sem, 1)

            def mean_squares(norm, row, n, ahead):
                pe.wait_ge(norm.sq_ready.sem, norm.sq_ready.count(row, n + 1, ahead))
                for j in range(S // P):
                    for t in range(KT):
                        last = nc.tensor.matmul(bank[:, norm.where, j:j + 1], sq[:, t, j * P:(j + 1) * P],
                                                con("mean")[:, 0:1], start=t == 0, stop=t == KT - 1)
                last.then_inc(norm.square_mean.sem, 1)

            def spread_rstd(norm, row, n, ahead):
                pe.wait_ge(norm.rstd_ready.sem, norm.rstd_ready.count(row, n + 1, ahead))
                for j in range(S // P):
                    last = nc.tensor.matmul(bank[:, norm.where, j * P:(j + 1) * P],
                                            norm.rstd[:, j:j + 1].broadcast_to([P, P]), con("ident"),
                                            start=True, stop=True)
                last.then_inc(norm.rstd_spread.sem, 1)

            def swap(row, i, ahead):
                pe.wait_ge(qk_copied.sem, qk_copied.count(row, i + 1, ahead))
                if i >= 2:
                    pe.wait_ge(sin_done.sem, sin_done.count(row, i - 1, ahead))
                nc.tensor.matmul(bank[:, 5 + i % 2, :], con("swap"), qk_sb[:, i % 2, :], start=True, stop=True)\
                    .then_inc(swapped.sem, 1)

            def project_qk(row, i, ahead):
                first = (i // 2) * P + (i % 2) * D
                if i >= 2:
                    pe.wait_ge(qk_copied.sem, qk_copied.count(row, i - 1, ahead))
                normed(hi_lo("qk"), 2 * D, slice(first, first + P), bank[:, 3 + i % 2, :])\
                    .then_inc(qk_proj.sem, 1)

            def project_v(i):
                wv = hi_lo("v")
                for blk in (2 * i, 2 * i + 1):
                    to = bank[:, 7 if i == 0 else 1, (blk % 2) * D:(blk % 2 + 1) * D]
                    for kt in range(KT):
                        rows = slice(kt * S + blk * P, kt * S + (blk + 1) * P)
                        feats = slice(kt * D, (kt + 1) * D)
                        nh = n_hi[:].rearrange("p t s -> p (t s)")[:, rows]
                        nl = n_lo[:].rearrange("p t s -> p (t s)")[:, rows]
                        nc.tensor.matmul(to, nl, wv[0][:, feats], start=kt == 0, stop=False)
                        nc.tensor.matmul(to, nh, wv[1][:, feats], start=False, stop=False)
                        last = nc.tensor.matmul(to, nh, wv[0][:, feats], start=False, stop=kt == KT - 1)
                last.then_inc(v_proj.sem, 1)

            def front_projections(row, ahead):
                pe.wait_ge(front.n_lo_ready.sem, front.n_lo_ready.count(row, 1, ahead))
                project_qk(row, 0, ahead)
                project_qk(row, 1, ahead)
                swap(row, 0, ahead)
                project_qk(row, 2, ahead)
                swap(row, 1, ahead)
                if ahead:
                    mean(rest, row, 0)
                project_qk(row, 3, ahead)
                swap(row, 2, ahead)
                project_v(0)
                if ahead:
                    mean_squares(rest, row, 1, 0)
                swap(row, 3, ahead)
                if ahead:
                    pe.wait_ge(d_added.sem, d_added.count(row, 1))
                project_v(1)

            def row_steps(row, is_last):
                def fill(kind, n):
                    at = fills.index((kind, n))
                    if at >= 3:
                        what, k = fills[at - 3]
                        pe.wait_ge(freed_by[what].sem, freed_by[what].count(row, k + 1))
                    return slot((kind, n))

                def masked(to, which):
                    nc.tensor.matmul(to, mask[:, 0, :], mask[:, which:which + 1, :].broadcast_to([P, GH, P]),
                                     start=True, stop=which == 2)

                def scores_for_max(n):
                    u, a = n // 2, n % 2
                    blk, half = u % BLOCKS, u // BLOCKS
                    if a == 0:
                        pe.wait_ge(k_spread.sem, k_spread.count(row, u + 1))
                        if u == BLOCKS:
                            pe.wait_ge(stacked[1].sem, stacked[1].count(row, STACK_DMAS * 16))
                    to = fill("s1", n)
                    for g in range(2):
                        masked(to[:, g, :], 1)
                    for g in range(2):
                        gq = 2 * a + g
                        last = nc.tensor.matmul(to[:, g, :],
                                                q_st[0:MROW, half * GQ + gq, blk * P:(blk + 1) * P],
                                                k_ex[u % 2][0:MROW, gq, :, :], start=False, stop=True)
                    last.then_inc(s1_ready.sem, 1)

                def max_transposed(u):
                    pe.wait_ge(max_done.sem, max_done.count(row, 2 * u + 2))
                    to = fill("t", u)
                    for gq in range(GQ):
                        last = nc.tensor.transpose(to[0:KS, 0, gq * P:(gq + 1) * P], neg_max[:, gq, 0:KS], con("ident"))
                    last.then_inc(max_t.sem, 1)

                def shifted_scores(n):
                    u, a = n // 2, n % 2
                    blk, half = u % BLOCKS, u // BLOCKS
                    if a == 0:
                        pe.wait_ge(max_rows.sem, max_rows.count(row, u + 1))
                    to = fill("s2", n)
                    for g in range(2):
                        masked(to[:, g, :], 2)
                    for g in range(2):
                        gq = 2 * a + g
                        for hh in range(GH):
                            last = nc.tensor.matmul(to[:, g, hh * P:(hh + 1) * P], k_ex[u % 2][0:KS, gq, hh, :],
                                                    q_st[0:KS, half * GQ + gq, blk * P:(blk + 1) * P],
                                                    start=False, stop=True, skip_group_check=True)
                    last.then_inc(s2_ready.sem, 1)

                def contexts(n):
                    u, a = n // 2, n % 2
                    if a == 0:
                        pe.wait_ge(v_spread.sem, v_spread.count(row, u + 1))
                        if u:
                            pe.wait_ge(ctx_done.sem, ctx_done.count(row, u))
                    pe.wait_ge(exp_done.sem, exp_done.count(row, n + 1))
                    for j in range(8):
                        last = nc.tensor.matmul(bank[:, 6, a * P:(a + 1) * P], v_ex[:, 8 * a + j, :],
                                                prob[a][:, j * P:(j + 1) * P], start=j == 0, stop=j == 7)
                    last.then_inc(pv_done.sem, 1)

                pe.wait_ge(stacked[0].sem, stacked[0].count(row, STACK_DMAS * 16))
                pe.wait_ge(v_copied.sem, v_copied.count(row, 2))
                pe.wait_ge(sin_done.sem, sin_done.count(row, 4))
                pe.wait_ge(out_ready.sem, out_ready.count(row, 0))
                scores_for_max(0)
                scores_for_max(1)
                max_transposed(0)
                for u in range(UNITS):
                    for a in range(2):
                        shifted_scores(2 * u + a)
                        if u + 1 < UNITS:
                            scores_for_max(2 * u + 2 + a)
                    contexts(2 * u)
                    if u + 1 < UNITS:
                        max_transposed(u + 1)
                    contexts(2 * u + 1)
                    if not is_last:
                        if u == 1:
                            mean(front, row, 1)
                        elif u == 3:
                            mean_squares(front, row, 0, 1)
                        elif u == 4:
                            spread_rstd(front, row, 0, 1)
                        elif u == 6:
                            mean_squares(front, row, 1, 1)
                pe.wait_ge(ctx_done.sem, ctx_done.count(row, UNITS))
                for t in range(KT):
                    for kt in range(KT):
                        last = nc.tensor.matmul(bank[:, t, :], plain("o")[:, kt * D + t * P:kt * D + (t + 1) * P],
                                                ctx_n[:, kt, :], start=kt == 0, stop=kt == KT - 1)
                last.then_inc(o_proj.sem, 1)
                mean_squares(rest, row, 0, 0)
                spread_rstd(rest, row, 0, 0)
                pe.wait_ge(rest.n_lo_ready.sem, rest.n_lo_ready.count(row, 1))
                for m in range(MT):
                    if m >= 2:
                        pe.wait_ge(hidden_done.sem, hidden_done.count(row, m - 1))
                    for part in range(2):
                        last = normed(hi_lo("up"), 2 * INTER, slice(part * INTER + m * P, part * INTER + (m + 1) * P),
                                      bank[:, 3 + 2 * (m % 2) + part, :])
                    last.then_inc(up_ready.sem, 1)
                if not is_last:
                    spread_rstd(front, row, 1, 1)
                pe.wait_ge(x1_ready.sem, x1_ready.count(row, 1))
                for t in range(KT):
                    for m in range(MT):
                        if t == 0:
                            pe.wait_ge(hidden_done.sem, hidden_done.count(row, m + 1))
                        last = nc.tensor.matmul(bank[:, t, :], plain("down")[:, m * D + t * P:m * D + (t + 1) * P],
                                                hidden[:, m, :], start=m == 0, stop=m == MT - 1)
                last.then_inc(down_ready.sem, 1)
                if is_last:
                    mean(rest, row, 0)
                    mean_squares(rest, row, 1, 0)
                else:
                    front_projections(row, 1)
                spread_rstd(rest, row, 1, 0)
                pe.wait_ge(rest.shifted.sem, rest.shifted.count(row, 1))
                for j in range(S // P):
                    for kt in range(KT):
                        last = nc.tensor.matmul(bank[:, 3, j * E:(j + 1) * E], xc[:, kt, j * P:(j + 1) * P],
                                                plain("r")[:, kt * E:(kt + 1) * E], start=kt == 0, stop=kt == KT - 1)
                last.then_inc(route_ready.sem, 1)
                pe.wait_ge(rest.n_lo_ready.sem, rest.n_lo_ready.count(row, 2))
                if not is_last:
                    pe.wait_ge(v_copied.sem, v_copied.count(row, 2, 1))
                    pe.wait_ge(sin_done.sem, sin_done.count(row, 4, 1))
                normed(hi_lo("ag"), E * R, slice(0, E * R), bank[:, 0, :])
                normed(hi_lo("au"), E * R, slice(0, E * R), bank[:, 1, :]).then_inc(lora_a.sem, 1)

                gate_banks = [(2, 3), (4, 5)]

                def base(m):
                    at, width = FF_TILES[m]
                    if m >= 2:
                        pe.wait_ge(ff_prod.sem, ff_prod.count(row, FF_STEPS.index((m - 2, 2)) + 1))
                    for name, where in zip(("wg", "wu"), gate_banks[m % 2]):
                        last = normed(hi_lo(name), DFF, slice(at, at + width), bank[0:width, where, :])
                    last.then_inc(gu_ready.sem, 1)

                def transposed_picks(kinds):
                    for kind in kinds:
                        pe.wait_ge(spread.sem, spread.count(row, kind + 1))
                        if kind >= 2:
                            pe.wait_ge(pick_copied.sem, pick_copied.count(row, kind - 1))
                        for j in range(S // P):
                            last = nc.tensor.transpose(bank[:, 6 + kind % 2, j * P:(j + 1) * P],
                                                       spread_t[kind][:, j * P:(j + 1) * P], con("ident"))
                        last.then_inc(pick_t.sem, 1)

                pe.wait_ge(l_copied.sem, l_copied.count(row, 1))
                base(0)
                transposed_picks((0, 1))
                base(1)
                transposed_picks((2, 3))

                def lora(m, v):
                    at, width = FF_TILES[m]
                    before = FF_STEPS.index((m, v - 1)) + 1
                    pe.wait_ge(ff_prod.sem, ff_prod.count(row, before))
                    if m == 0:
                        pe.wait_ge(lora_lo.sem, lora_lo.count(row, 2 * v))
                    for i, (name, where) in enumerate(zip(("bg", "bu"), gate_banks[m % 2])):
                        wh, wl = hi_lo(name)
                        ah, al = lora_hl[2 * (v - 1) + i]
                        to = bank[0:width, where, :]
                        cols = slice(at, at + width)
                        nc.tensor.matmul(to, wl[:, cols], ah, start=False, stop=False, skip_group_check=True)
                        nc.tensor.matmul(to, wh[:, cols], al, start=False, stop=False, skip_group_check=True)
                        last = nc.tensor.matmul(to, wh[:, cols], ah, start=False, stop=True, skip_group_check=True)
                    last.then_inc(gu_ready.sem, 1)

                def down(m, v):
                    n = FF_STEPS.index((m, v))
                    rows = slice(0, FF_TILES[m][1])
                    pe.wait_ge(ff_lo.sem, ff_lo.count(row, n + 1))
                    if v == 0:
                        for t in range(KT):
                            last = product(bank[:, 6 + t, :], hi_lo("wd"), slice(m * D + t * P, m * D + (t + 1) * P),
                                           ff_hl[n % 4], rows, m == 0, m == FT - 1)
                    else:
                        last = product(bank[:, v - 1, :], hi_lo("ad"), slice(m * P, (m + 1) * P),
                                       ff_hl[n % 4], rows, m == 0, m == FT - 1)
                        if m == FT - 1 and v == 2:
                            last.then_inc(z_ready.sem, 1)
                            return
                    last.then_inc(ff_used.sem, 1)

                for m in range(FT):
                    lora(m, 1)
                    if m == 1:
                        down(0, 1)
                    if 0 < m < FT - 1:
                        base(m + 1)
                    if m:
                        down(m - 1, 2)
                    else:
                        pe.wait_ge(pick_copied.sem, pick_copied.count(row, 4))
                        pe.wait_ge(lora_in.sem, lora_in.count(row, 4))
                    if 0 < m < FT - 1:
                        lora(m, 2)
                        down(m, 0)
                    else:
                        down(m, 0)
                        lora(m, 2)
                    if m:
                        down(m, 1)
                down(FT - 1, 2)
                pe.wait_ge(z_steps.sem, z_steps.count(row, 3))
                for t in range(KT):
                    last = nc.tensor.matmul(bank[:, 6 + t, :], plain("bd")[:, t * P:(t + 1) * P], silu_out[0],
                                            start=False, stop=True, skip_group_check=True)
                last.then_inc(y_ready.sem, 1)

            pe.wait_ge(const_loaded.sem, 16)
            mean(front, 0, 0)
            mean_squares(front, 0, 0, 0)
            pe.wait_ge(cond_ready.sem, 1)
            pe.wait_ge(wmod_loaded.sem, 16)
            for c in range(6 * KT):
                for kt in range(KT):
                    last = nc.tensor.matmul(bank[:, 0, c * B:(c + 1) * B],
                                            wm[:, kt * 6 * D + c * P:kt * 6 * D + (c + 1) * P],
                                            act_c[:, kt * B:(kt + 1) * B], start=kt == 0, stop=kt == KT - 1)
            last.then_inc(mod_ready.sem, 1)
            spread_rstd(front, 0, 0, 0)
            mean_squares(front, 0, 1, 0)
            spread_rstd(front, 0, 1, 0)
            pe.wait_ge(chunk_lo.sem, 1)
            front_projections(0, 0)
            pe.wait_ge(mask_loaded.sem, 16)
            pe.wait_ge(plain_loaded.sem, 16)
            pe.wait_ge(chunk_lo.sem, len(CHUNKS))
            pe.wait_ge(ones_set.sem, 4)
            with pe.Fori(0, B - 1) as row:
                row_steps(row, False)
            row_steps(B - 1, True)


def _tiles(w):
    n_out, n_in = w.shape
    tiles = -(-n_in // P)
    t = np.zeros((tiles * P, n_out), w.dtype)
    t[:n_in] = w.T
    return t.reshape(tiles, P, n_out).transpose(1, 0, 2).reshape(P, tiles * n_out)


def _columns(v):
    v = v.reshape(-1, KT, P)
    return v.transpose(2, 1, 0).reshape(P, -1)


def _constants():
    inv_freq = (1.0 / np.float32(10000.0) ** (np.arange(0, HD, 2, dtype=np.float32) / np.float32(HD))).astype(np.float32)
    freqs = np.outer(np.arange(S, dtype=np.float32), inv_freq).astype(np.float32)
    angle = np.concatenate([freqs, freqs], -1).astype(np.float64).T
    sign = np.where(np.arange(HD) < HD // 2, -1.0, 1.0)[:, None]
    rows = np.arange(P)
    partner = rows // HD * HD + (rows % HD + HD // 2) % HD
    swap = np.zeros((P, P))
    swap[partner, rows] = 1
    head = np.zeros((P, GH))
    for part in range(PARTS):
        for r in range(32):
            head[32 * part + r, r // HD] = 1
    for i in range(GH):
        head[MROW + i, i] = 1
    before = np.tile((np.arange(E)[None, :] < np.arange(E)[:, None]).reshape(1, -1), (P, 1))
    parts = {"cos": np.tile(np.cos(angle), (P // HD, 1)), "sin": np.tile(np.sin(angle) * sign, (P // HD, 1)),
             "ident": np.eye(P), "mean": np.full((P, P), 1.0 / D), "swap": swap, "head": head, "before": before,
             "one": np.ones((P, 1))}
    return np.concatenate([parts[n] for n, _ in CONST_WIDTHS], 1).astype(np.float32)


def kernel(**inputs):
    import concourse.bacc as bacc
    from concourse.bass_utils import run_bass_kernel_spmd
    import ml_dtypes

    a = {k[3:]: np.asarray(v) for k, v in inputs.items()}
    x = a["attn_x"].transpose(0, 2, 1).reshape(B, KT, P, S).transpose(0, 2, 1, 3)
    qkv = a["attn_w_qkv"]
    split = {"qk": _tiles(qkv[:2 * D]), "v": _tiles(qkv[2 * D:]), "up": _tiles(a["attn_w_up"]),
             "ag": _tiles(a["ffn_Ag"].reshape(E * R, D)), "au": _tiles(a["ffn_Au"].reshape(E * R, D)),
             "wg": _tiles(a["ffn_Wg"]), "wu": _tiles(a["ffn_Wu"]),
             "bg": a["ffn_Bg"].transpose(0, 2, 1).reshape(E * R, DFF),
             "bu": a["ffn_Bu"].transpose(0, 2, 1).reshape(E * R, DFF),
             "wd": _tiles(a["ffn_Wd"]), "ad": _tiles(a["ffn_Ad"].reshape(E * R, DFF))}
    plain = {"o": _tiles(a["attn_w_o"]), "down": _tiles(a["attn_w_down"]),
             "bd": a["ffn_Bd"].transpose(0, 2, 1).reshape(E * R, D), "r": _tiles(a["ffn_Wr"])}
    query, key = np.arange(P)[:, None], np.arange(P)[None, :]
    masks = np.stack([np.eye(P), np.where(key > query, MASKED, 0), np.where(key > query, MASKED, 0).T], 1)
    arrays = {
        "x": x,
        "smalls": np.concatenate([_columns(a["attn_attn_norm_w"]), _columns(a["attn_ffn_norm_w"]),
                                  _columns(a["c"])], 1),
        "wmod": _tiles(a["wmod"].T),
        "wsplit": np.concatenate([split[n] for n, _ in SPLIT_WIDTHS], 1),
        "wplain": np.concatenate([plain[n] for n, _ in PLAIN_WIDTHS], 1),
        "consts": _constants(),
        "masks": masks.astype(ml_dtypes.bfloat16),
    }
    arrays = {k: np.ascontiguousarray(v) for k, v in arrays.items()}
    nc = bacc.Bacc("TRN2", target_bir_lowering=False, num_devices=1)
    args = [nc.dram_tensor(f"in_{k}", v.shape, mybir.dt.from_np(v.dtype), kind="ExternalInput").ap()
            for k, v in arrays.items()]
    out = nc.dram_tensor("out_0", (B, P, KT, S), F32, kind="ExternalOutput").ap()
    adaln_kernel(nc, *args, out)
    r = run_bass_kernel_spmd(nc, [{f"in_{k}": v for k, v in arrays.items()}], core_ids=[0])
    got = r.results[0]["out_0"]
    return got.transpose(0, 2, 1, 3).reshape(B, D, S).transpose(0, 2, 1)
```

```python
from contextlib import ExitStack

import numpy as np

import concourse.bass as bass
from concourse import mybir

ALU = mybir.AluOpType
ACT = mybir.ActivationFunctionType
F32 = mybir.dt.float32
F32R = mybir.dt.float32r
BF16 = mybir.dt.bfloat16
AX_X = mybir.AxisListType.X

P = 128
B, S, D = 4, 512, 256
KT = D // P
HEADS, HD = 32, 8
BLOCK = S // 4
INTER = 512
MT = INTER // P
DFF = 704
E, R = 8, 16
EPS = 1e-5
SCALE = float(HD) ** -0.5
LORA_SCALE = 2.0
MASKED = -1e30

GH = 4
HALF = HEADS // 2
GQ = HALF // GH
BLOCKS = S // BLOCK
UNITS = 2 * BLOCKS
PARTS = 3
MROW = PARTS * 32
KS = MROW + GH
FF_TILES = [(m * P, min(P, DFF - m * P)) for m in range(-(-DFF // P))]
FT = len(FF_TILES)
VARIANTS = 3

SPLIT_WIDTHS = [("qk", KT * 2 * D), ("v", KT * D), ("up", KT * 2 * INTER), ("ag", KT * E * R),
                ("au", KT * E * R), ("wg", KT * DFF), ("wu", KT * DFF), ("bg", DFF), ("bu", DFF),
                ("wd", FT * D), ("ad", FT * E * R)]
PLAIN_WIDTHS = [("o", KT * D), ("down", MT * D), ("bd", D), ("r", KT * E)]
CONST_WIDTHS = [("cos", S), ("sin", S), ("ident", P), ("mean", P), ("swap", P), ("head", GH), ("before", E * E), ("one", 1)]


def layout(widths):
    places, at = {}, 0
    for name, width in widths:
        places[name] = (at, width)
        at += width
    return places, at


SPLIT, SPLIT_COLS = layout(SPLIT_WIDTHS)
PLAIN, PLAIN_COLS = layout(PLAIN_WIDTHS)
CONST, CONST_COLS = layout(CONST_WIDTHS)
CHUNK_WIDTHS = [KT * 3 * D] + 4 * [4 * S]
CHUNK_WIDTHS += [SPLIT_COLS - sum(CHUNK_WIDTHS)]
CHUNKS = [(sum(CHUNK_WIDTHS[:c]), width) for c, width in enumerate(CHUNK_WIDTHS)]
EARLY_CHUNKS = 3


def ff_steps():
    steps = [(0, 0), (1, 0), (0, 1), (0, 2)]
    for m in range(1, FT):
        steps += [(m, 1)] + ([(m + 1, 0)] if m + 1 < FT else []) + [(m, 2)]
    return steps


FF_STEPS = ff_steps()
FF_USED = [VARIANTS * m + v + 1 for m, v in FF_STEPS]


class Signal:

    def __init__(self, sem, per_row, before=0):
        self.sem, self.per_row, self.before = sem, per_row, before

    def count(self, row, k, ahead=0):
        return row * self.per_row + (self.before + k + ahead * self.per_row)


class Norm:

    def __init__(self, signals, std, rstd, where):
        (self.sum_ready, self.mean_ready, self.centred, self.sq_ready, self.square_mean, self.std_ready,
         self.rstd_ready, self.rstd_spread, self.scaled, self.shifted, self.rms_normed, self.n_hi_ready,
         self.n_lo_ready) = signals
        self.std, self.rstd, self.where = std, rstd, where


def adaln_kernel(nc, x, smalls, wmod, wsplit, wplain, consts, masks, out):
    with ExitStack() as ctx:
        def sb(name, shape, dt=F32):
            return ctx.enter_context(nc.sbuf_tensor(name, shape, dt))

        def signal(name, per_row, before=0):
            return Signal(ctx.enter_context(nc.semaphore(name)), per_row, before)

        w_hi = sb("w_hi", [P, SPLIT_COLS], F32R)
        w_lo = sb("w_lo", [P, SPLIT_COLS], F32R)
        w_plain = sb("w_plain", [P, PLAIN_COLS])
        const = sb("const", [P, CONST_COLS])
        mask = sb("mask", [P, 3, P], BF16)
        small = sb("small", [P, 2 * KT + KT * B])
        act_c = sb("act_c", [P, KT * B])
        mod_all = sb("mod_all", [P, 6 * KT, B])
        mod = sb("mod", [P, 6 * KT])
        front_mod = sb("front_mod", [P, 2 * KT])
        gate_tmp = sb("gate_tmp", [P, 2 * KT * B])
        h_next = sb("h_next", [P, KT, S])
        h = sb("h", [P, KT, S])
        n_hi = sb("n_hi", [P, KT, S], F32R)
        n_lo = sb("n_lo", [P, KT, S], F32R)
        q_st = sb("q_st", [P, HEADS // GH, S], F32R)
        k_st = sb("k_st", [P, HEADS // GH, S], F32R)
        v_ex = sb("v_ex", [P, HALF, P])
        arena = sb("arena", [P, 10, S])
        with nc.sbuf_tensor("tile_f", [P, 16, S], F32) as tile_f:
            pass
        arena_r = sb("arena_r", [P, 16, S], F32R)
        logits = sb("logits", [P, S // P, E])
        l_max = sb("l_max", [P, S // P])
        l_sum = sb("l_sum", [P, S // P])
        l_exp = sb("l_exp", [P, S // P, E])
        rank = sb("rank", [P, S // P, E])
        pick = sb("pick", [P, 2, S // P, E])
        eps_col = sb("eps_col", [P, 1])
        pool_mark = sb("pool_mark", [P, 1])
        bank = ctx.enter_context(nc.psum_tensor("bank", [P, 8, S], F32))

        def hi_lo(name):
            at, width = SPLIT[name]
            return w_hi[:, at:at + width], w_lo[:, at:at + width]

        def plain(name):
            at, width = PLAIN[name]
            return w_plain[:, at:at + width]

        def con(name):
            at, width = CONST[name]
            return const[:, at:at + width]

        xc = arena[:, 0:2, :]
        sq = arena[:, 2:4, :]
        tile_sum = arena[:, 2, :]
        v_sb = arena[:, 4:6, :].rearrange("p a (b f) -> p (a b) f", b=2)
        ctx_n = arena[:, 6:8, :]
        den_inv = arena[0:P // 2, 8, 0:2 * P]
        neg_max = arena[:, 9, :].rearrange("p (g c) -> p g c", c=P)
        mlp_rstd = arena[:, 4, :]
        gate_scaled = [arena[:, i, :] for i in range(2)]
        hidden = arena[:, 6:10, :]
        silu_out = [arena[:, 2 + i, :] for i in range(2)]
        pair_tmp = [arena[:, 6 + i, :] for i in range(2)]
        out_tiles = arena[:, 6:8, :]
        picks_t = [arena[:, i, :] for i in (0, 1, 8, 9)]
        qk_sb, q_cos, roped = tile_f[:, 0:2, :], tile_f[:, 2, :], tile_f[:, 4:6, :]
        prob = [tile_f[:, 8 + 2 * i:10 + 2 * i, :].rearrange("p a s -> p (a s)") for i in range(2)]
        x_res = tile_f[:, 12:14, :]
        wm = arena[:, 4:10, :].rearrange("p a s -> p (a s)")
        stages = [region.rearrange("p a s -> p (a s)") for region in (
            tile_f[:, 8:12, :], tile_f[:, 12:16, :], tile_f[:, 0:4, :], arena[:, 6:10, :], arena[:, 0:4, :],
            tile_f[:, 6:8, :])]
        k_ex = [arena_r[:, 4 * i:4 * i + 4, :].rearrange("p g (h s) -> p g h s", h=GH) for i in range(2)]
        rope_hl = [(arena_r[:, 8 + 2 * i, :], arena_r[:, 9 + 2 * i, :]) for i in range(4)]
        spread_t = [pair_tmp[0], pair_tmp[1], arena[:, 9, :], arena[:, 3, :]]
        lora_tmp = [tile_f[:, i, :] for i in (4, 6, 10, 11)]
        lora_hl = [(arena_r[:, 2 * i, :], arena_r[:, 2 * i + 1, :]) for i in range(4)]
        ff_hl = [(arena_r[:, 8 + 2 * i, :], arena_r[:, 9 + 2 * i, :]) for i in range(4)]

        x_loaded = signal("x_loaded", 16)
        small_loaded = signal("small_loaded", 0)
        wmod_loaded = signal("wmod_loaded", 0)
        const_loaded = signal("const_loaded", 0)
        mask_loaded = signal("mask_loaded", 0)
        plain_loaded = signal("plain_loaded", 0)
        chunk_loaded = [signal(f"chunk_loaded{i}", 0) for i in range(len(CHUNKS))]
        ones_set = signal("ones_set", 0)
        chunk_hi = signal("chunk_hi", 0)
        chunk_lo = signal("chunk_lo", 0)
        cond_ready = signal("cond_ready", 0)
        mod_ready = signal("mod_ready", 0)
        mod_steps = signal("mod_steps", 0)
        zeroed = signal("zeroed", 0)
        mod_row = signal("mod_row", 1)
        front, rest = [Norm(
            [signal(f"{name}_{what}", per_row) for what, per_row in (
                ("sum_ready", 3), ("mean_ready", 1), ("centred", 1), ("sq_ready", 2), ("square_mean", 2),
                ("std_ready", 2), ("rstd_ready", 2), ("rstd_spread", 2), ("scaled", KT), ("shifted", 1),
                ("rms_normed", KT), ("n_hi_ready", inputs * KT), ("n_lo_ready", inputs * KT))],
            sb(f"{name}_std", [P, S // P]), sb(f"{name}_rstd", [P, S // P]), where)
            for name, inputs, where in (("front", 1, 7), ("rest", 2, 2))]
        front_mod_ready = signal("front_mod_ready", 1)
        h_moved = signal("h_moved", 1)
        res_loaded = signal("res_loaded", 16)
        qk_proj = signal("qk_proj", 4)
        qk_copied = signal("qk_copied", 4)
        swapped = signal("swapped", 4)
        cos_done = signal("cos_done", 4)
        sin_done = signal("sin_done", 4)
        rope_done = signal("rope_done", 4)
        rope_hi = signal("rope_hi", 4)
        rope_lo = signal("rope_lo", 4)
        stacked = [signal(f"stacked{i}", PARTS * GQ * 16) for i in range(4)]
        v_proj = signal("v_proj", 2)
        v_copied = signal("v_copied", 2)
        k_spread = signal("k_spread", UNITS)
        v_spread = signal("v_spread", UNITS)
        s1_ready = signal("s1_ready", 2 * UNITS)
        max_done = signal("max_done", 2 * UNITS)
        max_t = signal("max_t", UNITS)
        max_rows = signal("max_rows", UNITS)
        s2_ready = signal("s2_ready", 2 * UNITS)
        exp_done = signal("exp_done", 2 * UNITS)
        den_done = signal("den_done", UNITS)
        pv_done = signal("pv_done", 2 * UNITS)
        ctx_done = signal("ctx_done", UNITS)
        o_proj = signal("o_proj", KT)
        x1_ready = signal("x1_ready", KT)
        up_ready = signal("up_ready", MT)
        mlp_rstd_ready = signal("mlp_rstd_ready", 1)
        gate_ready = signal("gate_ready", MT)
        up_silu = signal("up_silu", MT)
        hidden_done = signal("hidden_done", MT)
        down_ready = signal("down_ready", KT)
        residual_ready = signal("residual_ready", KT)
        down_scaled = signal("down_scaled", KT)
        x2_ready = signal("x2_ready", KT)
        route_ready = signal("route_ready", 1)
        l_copied = signal("l_copied", 1)
        l_steps = signal("l_steps", 10)
        l_exp_done = signal("l_exp_done", 1)
        l_picks = signal("l_picks", 2)
        spread = signal("spread", 4)
        pick_t = signal("pick_t", 4)
        pick_copied = signal("pick_copied", 4)
        lora_a = signal("lora_a", 1)
        lora_in = signal("lora_in", 4)
        lora_hi = signal("lora_hi", 4)
        lora_lo = signal("lora_lo", 4)
        gu_ready = signal("gu_ready", FT * VARIANTS)
        ff_silu = signal("ff_silu", FT * VARIANTS)
        ff_prod = signal("ff_prod", FT * VARIANTS)
        ff_hi = signal("ff_hi", FT * VARIANTS)
        ff_lo = signal("ff_lo", FT * VARIANTS)
        ff_used = signal("ff_used", FT * VARIANTS - 2)
        z_ready = signal("z_ready", 2)
        z_steps = signal("z_steps", 3)
        y_ready = signal("y_ready", 1)
        out_ready = signal("out_ready", 1, before=1)
        stored = signal("stored", 16, before=16)

        fills = [("s1", 0), ("s1", 1), ("t", 0)]
        for u in range(UNITS):
            for a in range(2):
                fills += [("s2", 2 * u + a)] + ([("s1", 2 * u + 2 + a)] if u + 1 < UNITS else [])
            if u + 1 < UNITS:
                fills += [("t", u + 1)]
        slot_of = {fill: n % 3 for n, fill in enumerate(fills)}
        freed_by = {"s1": max_done, "t": max_rows, "s2": exp_done}

        def slot(fill):
            at = (2, 4, 0)[slot_of[fill]]
            return bank[:, at:at + 2, :]

        def up_bank(m, part):
            return (3, 5, 0, 3)[m] + part

        def mod_ps(where):
            return bank[:, where, 0:6 * KT * B].rearrange("p (c b) -> p c b", b=B)

        def diagonal(flat, first):
            step = P + HD
            whole = flat[:, first:first + 7 * step + HD]
            return bass.AP(whole.tensor, whole.offset, [whole.ap[0], [step, 8], [1, HD]])

        def half_stacked(engine, row, half, ahead):
            for i in (2 * half, 2 * half + 1):
                engine.wait_ge(stacked[i].sem, stacked[i].count(row, PARTS * GQ * 16, ahead))

        def stack_tile(engine, row, i, ahead):
            half, is_k = i // 2, i % 2
            engine.wait_ge(rope_hi.sem, rope_hi.count(row, i + 1, ahead))
            engine.wait_ge(rope_lo.sem, rope_lo.count(row, i + 1, ahead))
            if engine is nc.gpsimd:
                nc.gpsimd.tensor_tensor(pool_mark[:], con("one"), con("one"), ALU.mult)
            hi, lo = rope_hl[i]
            dest = k_st if is_k else q_st
            for part, src in enumerate((hi, lo, hi) if is_k else (hi, hi, lo)):
                for gq in range(GQ):
                    engine.dma_start(dest[32 * part:32 * part + 32, half * GQ + gq, :].bitcast(F32),
                                     src[32 * gq:32 * gq + 32, :].bitcast(F32)).then_inc(stacked[i].sem, 16)

        block = ctx.enter_context(nc.Block())

        @block.sync
        def _(sp):
            def load_chunk(c):
                at, width = CHUNKS[c]
                sp.dma_start(stages[c][:, 0:width], wsplit[:, at:at + width]).then_inc(chunk_loaded[c].sem, 16)

            sp.dma_start(h_next[:], x[0]).then_inc(x_loaded.sem, 16)
            sp.dma_start(small[:], smalls).then_inc(small_loaded.sem, 16)
            sp.dma_start(const[:], consts).then_inc(const_loaded.sem, 16)
            sp.dma_start(wm, wmod).then_inc(wmod_loaded.sem, 16)
            for c in (0, 1, 2, 5):
                load_chunk(c)
            sp.dma_start(mask[:], masks).then_inc(mask_loaded.sem, 16)
            sp.wait_ge(mod_ready.sem, 2)
            load_chunk(3)
            sp.dma_start(w_plain[:], wplain).then_inc(plain_loaded.sem, 16)
            sp.wait_ge(front.n_lo_ready.sem, KT)
            load_chunk(4)

            def load(to, row, loaded):
                sp.dma_start(to, x[bass.ds(row, 1)].rearrange("b p t s -> p (b t) s")).then_inc(loaded.sem, 16)

            def stack(row, ahead):
                for i in range(3):
                    stack_tile(sp, row, i, ahead)

            def row_steps(row, last):
                if not last:
                    sp.wait_ge(h_moved.sem, h_moved.count(row, 1))
                    load(h_next[:], row + 1, x_loaded)
                sp.wait_ge(out_ready.sem, out_ready.count(row, 0))
                half_stacked(sp, row, 1, 0)
                load(x_res, row, res_loaded)
                if not last:
                    stack(row, 1)
                sp.wait_ge(out_ready.sem, out_ready.count(row, 1))
                sp.dma_start(out[bass.ds(row, 1)].rearrange("b p t s -> p (b t) s"), out_tiles)\
                    .then_inc(stored.sem, 16)

            stack(0, 0)
            with sp.Fori(0, B - 1) as row:
                row_steps(row, False)
            row_steps(B - 1, True)
            sp.wait_ge(stored.sem, stored.count(B - 1, 16))

        @block.gpsimd
        def _(pool):
            def tile_sums(norm, src):
                nc.gpsimd.tensor_tensor(tile_sum, src[:, 0, :], src[:, 1, :], ALU.add).then_inc(norm.sum_ready.sem, 1)

            def square_sums(norm, row, n, ahead):
                pool.wait_ge(norm.sq_ready.sem, norm.sq_ready.count(row, n + 1, ahead))
                tile_sums(norm, sq)

            def rope_cos(row, i, ahead):
                pool.wait_ge(qk_copied.sem, qk_copied.count(row, i + 1, ahead))
                if i:
                    pool.wait_ge(rope_done.sem, rope_done.count(row, i, ahead))
                nc.gpsimd.tensor_tensor(q_cos, qk_sb[:, i % 2, :], con("cos"), ALU.mult).then_inc(cos_done.sem, 1)

            def spread_keys(row, u, ahead):
                blk, half = u % BLOCKS, u // BLOCKS
                if u in (0, BLOCKS):
                    half_stacked(pool, row, half, ahead)
                if u == 0 and ahead:
                    pool.wait_ge(gu_ready.sem, gu_ready.count(row, FT * VARIANTS))
                if u >= 2:
                    pool.wait_ge(s2_ready.sem, s2_ready.count(row, 2 * (u - 1)))
                src = k_st[0:KS, half * GQ:(half + 1) * GQ, blk * P:(blk + 1) * P].bitcast(F32)
                nc.gpsimd.tensor_tensor(k_ex[u % 2][0:KS, :, 0, :], src,
                                        con("head")[0:KS, 0:1].unsqueeze(2).broadcast_to([KS, GQ, P]), ALU.mult)
                for hh in range(1, GH):
                    last = nc.gpsimd.tensor_scalar(k_ex[u % 2][0:KS, :, hh, :], src,
                                                   con("head")[0:KS, hh:hh + 1], 1.0, ALU.mult, ALU.mult)
                last.then_inc(k_spread.sem, 1)

            def spread_values(row, u, ahead):
                blk, half = u % BLOCKS, u // BLOCKS
                if u in (0, 2):
                    pool.wait_ge(v_copied.sem, v_copied.count(row, u // 2 + 1, ahead))
                if u:
                    pool.wait_ge(pv_done.sem, pv_done.count(row, 2 * u))
                elif ahead:
                    pool.wait_ge(pv_done.sem, pv_done.count(row, 2 * UNITS))
                values = v_sb[:, blk, half * P:(half + 1) * P].rearrange("p (a j d) -> p a j d", a=2, d=HD)
                for a in range(2):
                    flat = v_ex[:, 8 * a:8 * a + 8, :].rearrange("p j c -> p (j c)")
                    last = nc.gpsimd.tensor_tensor(diagonal(flat, 0), values[:, a],
                                                   con("one").unsqueeze(2).broadcast_to([P, 8, HD]), ALU.mult)
                last.then_inc(v_spread.sem, 1)

            def first_units(row, ahead):
                pool.wait_ge(rope_lo.sem, rope_lo.count(row, 4, ahead))
                for u in range(2):
                    spread_keys(row, u, ahead)
                spread_values(row, 0, ahead)

            def row_steps(row, last):
                for u in range(UNITS):
                    if 2 <= u + 1 < UNITS:
                        spread_keys(row, u + 1, 0)
                    if u:
                        spread_values(row, u, 0)
                    if u == 1 and not last:
                        pool.wait_ge(x_loaded.sem, x_loaded.count(row, 16, 1))
                        pool.wait_ge(out_ready.sem, out_ready.count(row, 0))
                        tile_sums(front, h_next)
                    if u in (4, 7) and not last:
                        square_sums(front, row, 0 if u == 4 else 1, 1)
                square_sums(rest, row, 0, 0)
                pool.wait_ge(x2_ready.sem, x2_ready.count(row, KT))
                tile_sums(rest, h)
                if not last:
                    rope_cos(row, 0, 1)
                square_sums(rest, row, 1, 0)
                if not last:
                    for i in range(1, 4):
                        rope_cos(row, i, 1)
                    stack_tile(nc.gpsimd, row, 3, 1)
                    first_units(row, 1)

            pool.wait_ge(x_loaded.sem, 16)
            tile_sums(front, h_next)
            pool.wait_ge(front.sum_ready.sem, 1)
            nc.gpsimd.memset(k_st[MROW:P, :, :].bitcast(F32), 1.0).then_inc(ones_set.sem, 1)
            pool.wait_ge(ones_set.sem, 1)
            nc.gpsimd.memset(v_ex[:], 0.0).then_inc(ones_set.sem, 1)
            pool.wait_ge(ones_set.sem, 2)
            for a in range(2):
                flat = v_ex[:, 8 * a:8 * a + 8, :].rearrange("p j c -> p (j c)")
                nc.gpsimd.memset(diagonal(flat, P // 2), 1.0).then_inc(ones_set.sem, 1)
            for n in range(2):
                square_sums(front, 0, n, 0)
            pool.wait_ge(chunk_lo.sem, EARLY_CHUNKS)
            for i in range(4):
                rope_cos(0, i, 0)
            stack_tile(nc.gpsimd, 0, 3, 0)
            pool.wait_ge(ones_set.sem, 4)
            pool.wait_ge(chunk_lo.sem, len(CHUNKS))
            first_units(0, 0)
            with pool.Fori(0, B - 1) as row:
                row_steps(row, False)
            row_steps(B - 1, True)

        @block.scalar
        def _(act):
            act.wait_ge(small_loaded.sem, 16)
            nc.scalar.activation(act_c[:], small[:, 2 * KT:], ACT.Silu).then_inc(cond_ready.sem, 1)

            def chunk_highs(chunks):
                for c in chunks:
                    at, width = CHUNKS[c]
                    act.wait_ge(chunk_loaded[c].sem, 16)
                    nc.scalar.copy(w_hi[:, at:at + width], stages[c][:, 0:width]).then_inc(chunk_hi.sem, 1)

            def squares(norm, n, src):
                for t in range(KT):
                    last = nc.scalar.activation(sq[:, t, :], src[:, t, :], ACT.Square)
                last.then_inc(norm.sq_ready.sem, 1)

            def deviation(norm, row, n, ahead):
                act.wait_ge(norm.square_mean.sem, norm.square_mean.count(row, n + 1, ahead))
                nc.scalar.activation(norm.std[:], bank[:, norm.where, 0:S // P], ACT.Sqrt, bias=eps_col[:])\
                    .then_inc(norm.std_ready.sem, 1)

            def shift(norm, row, ahead, to, src, columns):
                for t in range(KT):
                    act.wait_ge(norm.scaled.sem, norm.scaled.count(row, t + 1, ahead))
                    last = nc.scalar.activation(to[:, t, :], src[:, t, :], ACT.Identity, bias=columns[:, t:t + 1])
                last.then_inc(norm.shifted.sem, 1)
                act.wait_ge(norm.shifted.sem, norm.shifted.count(row, 1, ahead))

            def front_squares(row, n, ahead):
                if n == 0:
                    act.wait_ge(front.centred.sem, front.centred.count(row, 1, ahead))
                else:
                    shift(front, row, ahead, h_next, h_next, front_mod[:, 0:KT])
                squares(front, n, h_next)

            def copy_qk(row, i, ahead):
                act.wait_ge(qk_proj.sem, qk_proj.count(row, i + 1, ahead))
                if i >= 2:
                    act.wait_ge(swapped.sem, swapped.count(row, i - 1, ahead))
                    act.wait_ge(cos_done.sem, cos_done.count(row, i - 1, ahead))
                nc.scalar.copy(qk_sb[:, i % 2, :], bank[:, 3 + i % 2, :]).then_inc(qk_copied.sem, 1)

            def rope_high(row, i, ahead):
                act.wait_ge(rope_done.sem, rope_done.count(row, i + 1, ahead))
                nc.scalar.copy(rope_hl[i][0], roped[:, i % 2, :]).then_inc(rope_hi.sem, 1)

            def copy_v(row, i, ahead):
                act.wait_ge(v_proj.sem, v_proj.count(row, i + 1, ahead))
                nc.scalar.copy(arena[:, 4 + i, :], bank[:, 7 if i == 0 else 1, :]).then_inc(v_copied.sem, 1)

            def rms_highs(norm, row, ahead):
                for t in range(KT):
                    act.wait_ge(norm.rms_normed.sem, norm.rms_normed.count(row, t + 1, ahead))
                    nc.scalar.copy(n_hi[:, t, :], xc[:, t, :]).then_inc(norm.n_hi_ready.sem, 1)

            def second_norm_highs():
                for t in range(KT):
                    nc.scalar.copy(n_hi[:, t, :], xc[:, t, :]).then_inc(rest.n_hi_ready.sem, 1)

            def front_projections(row, ahead):
                rms_highs(front, row, ahead)
                copy_qk(row, 0, ahead)
                if ahead:
                    nc.scalar.preload_act_table(ACT.Sqrt)
                    act.wait_ge(rest.centred.sem, rest.centred.count(row, 1))
                    squares(rest, 1, xc)
                copy_qk(row, 1, ahead)
                rope_high(row, 0, ahead)
                copy_qk(row, 2, ahead)
                rope_high(row, 1, ahead)
                if ahead:
                    deviation(rest, row, 1, 0)
                copy_qk(row, 3, ahead)
                rope_high(row, 2, ahead)
                if ahead:
                    act.wait_ge(x2_ready.sem, x2_ready.count(row, KT))
                copy_v(row, 0, ahead)
                if ahead:
                    shift(rest, row, 0, xc, xc, mod[:, 3 * KT:4 * KT])
                    act.wait_ge(v_proj.sem, v_proj.count(row, 2, ahead))
                    second_norm_highs()
                rope_high(row, 3, ahead)
                copy_v(row, 1, ahead)

            def max_to_rows(row, u):
                blk, half = u % BLOCKS, u // BLOCKS
                act.wait_ge(max_t.sem, max_t.count(row, u + 1))
                src = slot(("t", u))[MROW:KS, 0, :].rearrange("p (g s) -> p g s", s=P)
                nc.scalar.copy(q_st[MROW:KS, half * GQ:(half + 1) * GQ, blk * P:(blk + 1) * P], src)\
                    .then_inc(max_rows.sem, 1)

            def row_steps(row, last):
                max_to_rows(row, 0)
                for u in range(UNITS):
                    if not last and u == 5:
                        deviation(front, row, 0, 1)
                    for a in range(2):
                        n = 2 * u + a
                        act.wait_ge(s2_ready.sem, s2_ready.count(row, n + 1))
                        if n >= 2:
                            act.wait_ge(pv_done.sem, pv_done.count(row, n - 1))
                        nc.scalar.activation(prob[a], slot(("s2", n)).rearrange("p a s -> p (a s)"),
                                             ACT.Exp, scale=SCALE).then_inc(exp_done.sem, 1)
                    if u == 0:
                        act.wait_ge(out_ready.sem, out_ready.count(row, 0))
                        act.wait_ge(front.shifted.sem, front.shifted.count(row, 1))
                        nc.scalar.copy(h[:], h_next[:]).then_inc(h_moved.sem, 1)
                    if u + 1 < UNITS:
                        max_to_rows(row, u + 1)
                    if not last and u in (3, 6):
                        front_squares(row, 0 if u == 3 else 1, 1)
                if not last:
                    deviation(front, row, 1, 1)
                nc.scalar.preload_act_table(ACT.Sqrt)
                for t in range(KT):
                    act.wait_ge(x1_ready.sem, x1_ready.count(row, t + 1))
                    nc.scalar.activation(n_hi[:, t, :], h[:, t, :], ACT.Identity, scale=small[:, KT + t:KT + t + 1])\
                        .then_inc(rest.n_hi_ready.sem, 1)
                squares(rest, 0, h)
                deviation(rest, row, 0, 0)
                nc.scalar.preload_act_table(ACT.Silu)
                act.wait_ge(rest.rstd_spread.sem, rest.rstd_spread.count(row, 1))
                nc.scalar.copy(mlp_rstd, bank[:, rest.where, :]).then_inc(mlp_rstd_ready.sem, 1)
                for m in range(MT):
                    act.wait_ge(gate_ready.sem, gate_ready.count(row, m + 1))
                    if m >= 2:
                        act.wait_ge(hidden_done.sem, hidden_done.count(row, m - 1))
                    nc.scalar.activation(silu_out[m % 2], gate_scaled[m % 2], ACT.Silu).then_inc(up_silu.sem, 1)
                if last:
                    nc.scalar.preload_act_table(ACT.Sqrt)
                    act.wait_ge(rest.centred.sem, rest.centred.count(row, 1))
                    squares(rest, 1, xc)
                    deviation(rest, row, 1, 0)
                    shift(rest, row, 0, xc, xc, mod[:, 3 * KT:4 * KT])
                    second_norm_highs()
                else:
                    front_projections(row, 1)
                act.wait_ge(l_steps.sem, l_steps.count(row, 2))
                nc.scalar.activation(l_exp[:], l_exp[:], ACT.Exp).then_inc(l_exp_done.sem, 1)
                nc.scalar.preload_act_table(ACT.Silu)
                def gate_silu(n):
                    m, v = FF_STEPS[n]
                    width = FF_TILES[m][1]
                    act.wait_ge(gu_ready.sem, gu_ready.count(row, n + 1))
                    if n >= 2:
                        act.wait_ge(ff_prod.sem, ff_prod.count(row, n - 1))
                    nc.scalar.activation(silu_out[n % 2][0:width], bank[0:width, 2 + 2 * (m % 2), :], ACT.Silu)\
                        .then_inc(ff_silu.sem, 1)

                def product_high(j):
                    width = FF_TILES[FF_STEPS[j][0]][1]
                    act.wait_ge(ff_prod.sem, ff_prod.count(row, j + 1))
                    if j >= 4:
                        act.wait_ge(ff_used.sem, ff_used.count(row, FF_USED[j - 4]))
                    else:
                        if j == 1:
                            act.wait_ge(lora_lo.sem, lora_lo.count(row, 4))
                        if j % 2 == 0 and not last:
                            half_stacked(act, row, j // 2, 1)
                    nc.scalar.copy(ff_hl[j % 4][0][0:width], pair_tmp[j % 2][0:width]).then_inc(ff_hi.sem, 1)

                def copy_pick(kind):
                    act.wait_ge(pick_t.sem, pick_t.count(row, kind + 1))
                    nc.scalar.copy(picks_t[kind], bank[:, 6 + kind % 2, :]).then_inc(pick_copied.sem, 1)

                gate_silu(0)
                act.wait_ge(rest.n_lo_ready.sem, rest.n_lo_ready.count(row, 2 * KT))
                copy_pick(0)
                copy_pick(1)
                for i in range(4):
                    if i == 2:
                        product_high(0)
                        copy_pick(2)
                        copy_pick(3)
                        act.wait_ge(lora_lo.sem, lora_lo.count(row, 2))
                    act.wait_ge(lora_in.sem, lora_in.count(row, i + 1))
                    nc.scalar.copy(lora_hl[i][0], lora_tmp[i]).then_inc(lora_hi.sem, 1)
                gate_silu(1)
                for n in range(2, len(FF_STEPS)):
                    if n == len(FF_STEPS) - 2:
                        product_high(n - 1)
                        gate_silu(n)
                    else:
                        gate_silu(n)
                        product_high(n - 1)
                product_high(len(FF_STEPS) - 1)

            act.wait_ge(zeroed.sem, 1)
            front_squares(0, 0, 0)
            deviation(front, 0, 0, 0)
            chunk_highs(range(EARLY_CHUNKS))
            front_squares(0, 1, 0)
            deviation(front, 0, 1, 0)
            front_projections(0, 0)
            chunk_highs(range(EARLY_CHUNKS, len(CHUNKS)))
            with act.Fori(0, B - 1) as row:
                row_steps(row, False)
            row_steps(B - 1, True)

        @block.vector
        def _(dve):
            nc.vector.memset(eps_col[:], EPS).then_inc(zeroed.sem, 1)
            nc.vector.memset(l_max[:], 0.0).then_inc(stored.sem, 16)
            nc.vector.memset(mod[:], 0.0).then_inc(out_ready.sem, 1)
            def front_columns():
                dve.wait_ge(mod_ready.sem, 1)
                cols = slice(0, 2 * KT)
                nc.vector.tensor_copy(mod_all[:, cols, :], mod_ps(0)[:, cols, :]).then_inc(mod_steps.sem, 1)
                dve.wait_ge(mod_steps.sem, 1)
                part = mod_all[:, KT:2 * KT, :]
                nc.vector.tensor_scalar(part, part, 1.0, None, ALU.add).then_inc(mod_steps.sem, 1)
                dve.wait_ge(mod_steps.sem, 2)

            def other_columns():
                dve.wait_ge(mod_ready.sem, 2)
                cols = slice(2 * KT, 6 * KT)
                nc.vector.tensor_copy(mod_all[:, cols, :], mod_ps(2)[:, cols, :]).then_inc(mod_steps.sem, 1)
                dve.wait_ge(mod_steps.sem, 3)
                part = mod_all[:, 4 * KT:5 * KT, :]
                nc.vector.tensor_scalar(part, part, 1.0, None, ALU.add).then_inc(mod_steps.sem, 1)
                for n, c in enumerate((2, 5)):
                    part = mod_all[:, c * KT:(c + 1) * KT, :]
                    sign = gate_tmp[:, n * KT * B:(n + 1) * KT * B].rearrange("p (t b) -> p t b", b=B)
                    nc.vector.tensor_scalar(sign, part, 0.0, 2.0, ALU.is_ge, ALU.mult).then_inc(mod_steps.sem, 1)
                    dve.wait_ge(mod_steps.sem, 5 + 4 * n)
                    nc.vector.scalar_tensor_tensor(part, part, -1.0, part, ALU.mult, ALU.max).then_inc(mod_steps.sem, 1)
                    dve.wait_ge(mod_steps.sem, 6 + 4 * n)
                    nc.vector.tensor_scalar(part, part, 0.25, None, ALU.max).then_inc(mod_steps.sem, 1)
                    dve.wait_ge(mod_steps.sem, 7 + 4 * n)
                    nc.vector.scalar_tensor_tensor(part, sign, -1.0, part, ALU.add, ALU.mult).then_inc(mod_steps.sem, 1)
                dve.wait_ge(mod_steps.sem, 12)

            def chunk_lows(chunks):
                for c in chunks:
                    at, width = CHUNKS[c]
                    dve.wait_ge(chunk_hi.sem, c + 1)
                    nc.vector.tensor_tensor(w_lo[:, at:at + width], stages[c][:, 0:width],
                                            w_hi[:, at:at + width].bitcast(F32), ALU.subtract).then_inc(chunk_lo.sem, 1)

            def centre(norm, row, ahead, to, src):
                dve.wait_ge(norm.mean_ready.sem, norm.mean_ready.count(row, 1, ahead))
                for t in range(KT):
                    last = nc.vector.tensor_tensor(to[:, t, :], src[:, t, :], bank[:, norm.where, :], ALU.subtract)
                last.then_inc(norm.centred.sem, 1)

            def inverse(norm, row, n, ahead):
                dve.wait_ge(norm.std_ready.sem, norm.std_ready.count(row, n + 1, ahead))
                nc.vector.reciprocal(norm.rstd[:], norm.std[:]).then_inc(norm.rstd_ready.sem, 1)

            def scale(norm, row, n, ahead, to, src, columns, done):
                dve.wait_ge(norm.rstd_spread.sem, norm.rstd_spread.count(row, n + 1, ahead))
                for t in range(KT):
                    nc.vector.scalar_tensor_tensor(to[:, t, :], src[:, t, :], columns[:, t:t + 1],
                                                   bank[:, norm.where, :], ALU.mult, ALU.mult).then_inc(done.sem, 1)

            def n_lows(norm, row, n, ahead):
                for t in range(KT):
                    dve.wait_ge(norm.n_hi_ready.sem, norm.n_hi_ready.count(row, n * KT + t + 1, ahead))
                    nc.vector.tensor_tensor(n_lo[:, t, :], xc[:, t, :], n_hi[:, t, :].bitcast(F32), ALU.subtract)\
                        .then_inc(norm.n_lo_ready.sem, 1)

            def front_modulation(row, ahead):
                nc.vector.tensor_copy(front_mod[:], mod_all[:, 0:2 * KT, bass.ds(row + ahead, 1)]
                                      .rearrange("p c b -> p (c b)")).then_inc(front_mod_ready.sem, 1)

            def front_scale(row, ahead):
                dve.wait_ge(front_mod_ready.sem, front_mod_ready.count(row, 1, ahead))
                scale(front, row, 0, ahead, h_next, h_next, front_mod[:, KT:2 * KT], front.scaled)

            def front_rms(row, ahead):
                dve.wait_ge(front.shifted.sem, front.shifted.count(row, 1, ahead))
                scale(front, row, 1, ahead, xc, h_next, small[:, 0:KT], front.rms_normed)
                n_lows(front, row, 0, ahead)

            def rope_sin(row, i, ahead):
                dve.wait_ge(swapped.sem, swapped.count(row, i + 1, ahead))
                if i >= 2:
                    dve.wait_ge(rope_lo.sem, rope_lo.count(row, i - 1, ahead))
                nc.vector.tensor_tensor(roped[:, i % 2, :], bank[:, 5 + i % 2, :], con("sin"), ALU.mult)\
                    .then_inc(sin_done.sem, 1)

            def rope_add(row, i, ahead):
                dve.wait_ge(cos_done.sem, cos_done.count(row, i + 1, ahead))
                dve.wait_ge(sin_done.sem, sin_done.count(row, i + 1, ahead))
                nc.vector.tensor_tensor(roped[:, i % 2, :], roped[:, i % 2, :], q_cos, ALU.add)\
                    .then_inc(rope_done.sem, 1)

            def rope_low(row, i, ahead):
                dve.wait_ge(rope_hi.sem, rope_hi.count(row, i + 1, ahead))
                nc.vector.tensor_tensor(rope_hl[i][1], roped[:, i % 2, :], rope_hl[i][0].bitcast(F32),
                                        ALU.subtract).then_inc(rope_lo.sem, 1)

            def front_rope(row, ahead):
                if ahead:
                    centre(rest, row, 0, xc, h)
                rope_sin(row, 0, ahead)
                rope_add(row, 0, ahead)
                rope_low(row, 0, ahead)
                rope_sin(row, 1, ahead)
                rope_add(row, 1, ahead)
                if ahead:
                    inverse(rest, row, 1, 0)
                rope_low(row, 1, ahead)
                rope_sin(row, 2, ahead)
                rope_add(row, 2, ahead)
                if ahead:
                    scale(rest, row, 1, 0, xc, xc, mod[:, 4 * KT:5 * KT], rest.scaled)
                rope_low(row, 2, ahead)
                rope_sin(row, 3, ahead)
                rope_add(row, 3, ahead)
                if ahead:
                    n_lows(rest, row, 1, 0)
                rope_low(row, 3, ahead)

            def unit_max(row, u, ahead):
                if u:
                    dve.wait_ge(max_t.sem, max_t.count(row, u))
                for a in range(2):
                    n = 2 * u + a
                    dve.wait_ge(s1_ready.sem, s1_ready.count(row, n + 1, ahead))
                    nc.vector.tensor_reduce(neg_max[:, 2 * a:2 * a + 2, MROW:KS],
                                            slot(("s1", n)).rearrange("p a (h s) -> p a h s", s=P),
                                            AX_X, ALU.max, negate=True).then_inc(max_done.sem, 1)

            def row_steps(row, is_last):
                dve.wait_ge(out_ready.sem, out_ready.count(row, 0))
                nc.vector.tensor_copy(mod[:], mod_all[:, :, bass.ds(row, 1)].rearrange("p c b -> p (c b)"))\
                    .then_inc(mod_row.sem, 1)

                def normalise(u):
                    blk, half = u % BLOCKS, u // BLOCKS
                    acc = bank[:, 6, 0:2 * P]
                    dve.wait_ge(pv_done.sem, pv_done.count(row, 2 * u + 2))
                    if u == 0:
                        dve.wait_ge(stored.sem, stored.count(row, 0))
                    else:
                        dve.wait_ge(ctx_done.sem, ctx_done.count(row, u))
                    nc.vector.reciprocal(den_inv, acc[P // 2:P, :]).then_inc(den_done.sem, 1)
                    dve.wait_ge(den_done.sem, den_done.count(row, u + 1))
                    for a in range(2):
                        last = nc.vector.tensor_tensor(ctx_n[64 * a:64 * a + 64, half, blk * P:(blk + 1) * P],
                                                       acc[0:64, a * P:(a + 1) * P], den_inv[:, a * P:(a + 1) * P],
                                                       ALU.mult)
                    last.then_inc(ctx_done.sem, 1)

                for u in range(UNITS):
                    if u + 1 < UNITS:
                        unit_max(row, u + 1, 0)
                    if not is_last:
                        if u == 0:
                            dve.wait_ge(front.shifted.sem, front.shifted.count(row, 1))
                            front_modulation(row, 1)
                        elif u == 3:
                            centre(front, row, 1, h_next, h_next)
                        elif u == 5:
                            inverse(front, row, 0, 1)
                        elif u == 6:
                            front_scale(row, 1)
                    normalise(u)
                if not is_last:
                    inverse(front, row, 1, 1)
                dve.wait_ge(h_moved.sem, h_moved.count(row, 1))
                for t in range(KT):
                    dve.wait_ge(o_proj.sem, o_proj.count(row, t + 1))
                    nc.vector.tensor_tensor(h[:, t, :], h[:, t, :], bank[:, t, :], ALU.add).then_inc(x1_ready.sem, 1)
                for t in range(KT):
                    dve.wait_ge(x1_ready.sem, x1_ready.count(row, t + 1))
                    dve.wait_ge(rest.n_hi_ready.sem, rest.n_hi_ready.count(row, t + 1))
                    nc.vector.scalar_tensor_tensor(n_lo[:, t, :], h[:, t, :], small[:, KT + t:KT + t + 1],
                                                   n_hi[:, t, :].bitcast(F32), ALU.mult, ALU.subtract)\
                        .then_inc(rest.n_lo_ready.sem, 1)
                inverse(rest, row, 0, 0)
                dve.wait_ge(mlp_rstd_ready.sem, mlp_rstd_ready.count(row, 1))

                def scale_gate(m):
                    dve.wait_ge(up_ready.sem, up_ready.count(row, m + 1))
                    if m >= 2:
                        dve.wait_ge(up_silu.sem, up_silu.count(row, m - 1))
                    nc.vector.tensor_tensor(gate_scaled[m % 2], mlp_rstd, bank[:, up_bank(m, 0), :], ALU.mult)\
                        .then_inc(gate_ready.sem, 1)

                def hidden_tile(m):
                    dve.wait_ge(up_silu.sem, up_silu.count(row, m + 1))
                    nc.vector.tensor_tensor(hidden[:, m, :], silu_out[m % 2], bank[:, up_bank(m, 1), :], ALU.mult)\
                        .then_inc(hidden_done.sem, 1)

                scale_gate(0)
                for m in range(1, MT):
                    scale_gate(m)
                    hidden_tile(m - 1)
                hidden_tile(MT - 1)
                if not is_last:
                    dve.wait_ge(rest.n_lo_ready.sem, rest.n_lo_ready.count(row, KT))
                    front_rms(row, 1)
                dve.wait_ge(res_loaded.sem, res_loaded.count(row, 16))
                dve.wait_ge(mod_row.sem, mod_row.count(row, 1))
                for t in range(KT):
                    nc.vector.scalar_tensor_tensor(x_res[:, t, :], h[:, t, :], mod[:, 2 * KT + t:2 * KT + t + 1],
                                                   x_res[:, t, :], ALU.mult, ALU.add).then_inc(residual_ready.sem, 1)
                for t in range(KT):
                    dve.wait_ge(residual_ready.sem, residual_ready.count(row, t + 1))
                    dve.wait_ge(down_ready.sem, down_ready.count(row, t + 1))
                    nc.vector.scalar_tensor_tensor(h[:, t, :], bank[:, t, :], mod[:, 2 * KT + t:2 * KT + t + 1],
                                                   mlp_rstd, ALU.mult, ALU.mult).then_inc(down_scaled.sem, 1)
                    dve.wait_ge(down_scaled.sem, down_scaled.count(row, t + 1))
                    nc.vector.tensor_tensor(h[:, t, :], h[:, t, :], x_res[:, t, :], ALU.add).then_inc(x2_ready.sem, 1)
                if is_last:
                    centre(rest, row, 0, xc, h)
                    inverse(rest, row, 1, 0)
                    scale(rest, row, 1, 0, xc, xc, mod[:, 4 * KT:5 * KT], rest.scaled)
                    n_lows(rest, row, 1, 0)
                else:
                    dve.wait_ge(front.n_lo_ready.sem, front.n_lo_ready.count(row, KT, 1))
                    front_rope(row, 1)

                steps = [0]

                def step(ins):
                    steps[0] += 1
                    ins.then_inc(l_steps.sem, 1)
                    return steps[0]

                def after(n):
                    dve.wait_ge(l_steps.sem, l_steps.count(row, n))

                dve.wait_ge(route_ready.sem, route_ready.count(row, 1))
                nc.vector.tensor_copy(logits[:], bank[:, 3, 0:S // P * E].rearrange("p (j e) -> p j e", e=E))\
                    .then_inc(l_copied.sem, 1)
                dve.wait_ge(l_copied.sem, l_copied.count(row, 1))
                after(step(nc.vector.tensor_reduce(l_max[:], logits[:], AX_X, ALU.max)))
                step(nc.vector.tensor_tensor(l_exp[:], logits[:], l_max[:].unsqueeze(2).broadcast_to([P, S // P, E]),
                                             ALU.subtract))
                wide = [t.rearrange("p (j e f) -> p j e f", j=8, e=8)[:, 0:S // P] for t in pair_tmp]
                other = logits[:].unsqueeze(2).broadcast_to([P, S // P, E, E])
                own = logits[:].unsqueeze(3).broadcast_to([P, S // P, E, E])
                before = con("before").rearrange("p (e f) -> p e f", f=E).unsqueeze(1).broadcast_to([P, S // P, E, E])
                step(nc.vector.tensor_tensor(wide[0], other, own, ALU.is_gt))
                after(step(nc.vector.tensor_tensor(wide[1], other, own, ALU.is_equal)))
                after(step(nc.vector.tensor_tensor(wide[1], wide[1], before, ALU.mult)))
                after(step(nc.vector.tensor_tensor(wide[0], wide[0], wide[1], ALU.add)))
                after(step(nc.vector.tensor_reduce(rank[:], wide[0], AX_X, ALU.add)))
                dve.wait_ge(l_exp_done.sem, l_exp_done.count(row, 1))
                after(step(nc.vector.tensor_reduce(l_sum[:], l_exp[:], AX_X, ALU.add)))
                after(step(nc.vector.reciprocal(l_max[:], l_sum[:])))
                step(nc.vector.tensor_tensor(l_exp[:], l_exp[:], l_max[:].unsqueeze(2).broadcast_to([P, S // P, E]),
                                             ALU.mult))
                def spread_to(kind):
                    return spread_t[kind].rearrange("p (j e r) -> p j e r", j=S // P, r=R)

                def over_ranks(t):
                    return t.unsqueeze(3).broadcast_to([P, S // P, E, R])

                after(steps[0])
                nc.vector.tensor_scalar(pick[:, 0], rank[:], 0.0, LORA_SCALE, ALU.is_equal, ALU.mult)\
                    .then_inc(l_picks.sem, 1)
                nc.vector.tensor_scalar(pick[:, 1], rank[:], 1.0, LORA_SCALE, ALU.is_equal, ALU.mult)\
                    .then_inc(l_picks.sem, 1)
                dve.wait_ge(l_picks.sem, l_picks.count(row, 2))
                nc.vector.tensor_copy(spread_to(0), over_ranks(pick[:, 0])).then_inc(spread.sem, 1)
                nc.vector.tensor_tensor(spread_to(1), over_ranks(pick[:, 1]), over_ranks(pick[:, 0]), ALU.subtract)\
                    .then_inc(spread.sem, 1)
                for k in range(2):
                    nc.vector.tensor_tensor(spread_to(2 + k), over_ranks(pick[:, k]), over_ranks(l_exp[:]), ALU.mult)\
                        .then_inc(spread.sem, 1)

                def lora_input(i):
                    gate_up, kind = i % 2, i // 2
                    dve.wait_ge(pick_copied.sem, pick_copied.count(row, kind + 1))
                    nc.vector.tensor_tensor(lora_tmp[i], picks_t[kind], bank[:, gate_up, :], ALU.mult)\
                        .then_inc(lora_in.sem, 1)

                def lora_low(i):
                    dve.wait_ge(lora_hi.sem, lora_hi.count(row, i + 1))
                    nc.vector.tensor_tensor(lora_hl[i][1], lora_tmp[i], lora_hl[i][0].bitcast(F32), ALU.subtract)\
                        .then_inc(lora_lo.sem, 1)

                def ff_low(j):
                    width = FF_TILES[FF_STEPS[j][0]][1]
                    dve.wait_ge(ff_hi.sem, ff_hi.count(row, j + 1))
                    nc.vector.tensor_tensor(ff_hl[j % 4][1][0:width], pair_tmp[j % 2][0:width],
                                            ff_hl[j % 4][0][0:width].bitcast(F32), ALU.subtract)\
                        .then_inc(ff_lo.sem, 1)

                def ff_product(n):
                    m = FF_STEPS[n][0]
                    width = FF_TILES[m][1]
                    dve.wait_ge(ff_silu.sem, ff_silu.count(row, n + 1))
                    if n >= 2:
                        dve.wait_ge(ff_lo.sem, ff_lo.count(row, n - 1))
                    else:
                        dve.wait_ge(pick_t.sem, pick_t.count(row, n + 1))
                    nc.vector.tensor_tensor(pair_tmp[n % 2][0:width], silu_out[n % 2][0:width],
                                            bank[0:width, 3 + 2 * (m % 2), :], ALU.mult).then_inc(ff_prod.sem, 1)

                dve.wait_ge(lora_a.sem, lora_a.count(row, 1))
                ff_product(0)
                for kind in range(2):
                    if kind and not is_last:
                        half_stacked(dve, row, 0, 1)
                    lora_input(2 * kind)
                    lora_input(2 * kind + 1)
                    lora_low(2 * kind)
                    lora_low(2 * kind + 1)
                    if kind == 0:
                        ff_low(0)
                ff_product(1)
                for n in range(2, len(FF_STEPS)):
                    if 2 < n < len(FF_STEPS) - 1:
                        ff_low(n - 2)
                    if n == len(FF_STEPS) - 2:
                        ff_low(n - 1)
                    ff_product(n)
                ff_low(len(FF_STEPS) - 2)
                ff_low(len(FF_STEPS) - 1)
                for k in range(2):
                    dve.wait_ge(z_ready.sem, z_ready.count(row, k + 1))
                    nc.vector.tensor_tensor(silu_out[k], picks_t[2 + k], bank[:, k, :], ALU.mult)\
                        .then_inc(z_steps.sem, 1)
                dve.wait_ge(z_steps.sem, z_steps.count(row, 2))
                nc.vector.tensor_tensor(silu_out[0], silu_out[0], silu_out[1], ALU.add).then_inc(z_steps.sem, 1)
                if not is_last:
                    dve.wait_ge(z_steps.sem, z_steps.count(row, 2))
                    unit_max(row, 0, 1)
                dve.wait_ge(y_ready.sem, y_ready.count(row, 1))
                for t in range(KT):
                    last = nc.vector.scalar_tensor_tensor(pair_tmp[t], bank[:, 6 + t, :],
                                                          mod[:, 5 * KT + t:5 * KT + t + 1], h[:, t, :],
                                                          ALU.mult, ALU.add)
                last.then_inc(out_ready.sem, 1)

            centre(front, 0, 0, h_next, h_next)
            inverse(front, 0, 0, 0)
            chunk_lows(range(EARLY_CHUNKS))
            front_columns()
            front_modulation(0, 0)
            front_scale(0, 0)
            inverse(front, 0, 1, 0)
            front_rms(0, 0)
            front_rope(0, 0)
            other_columns()
            chunk_lows(range(EARLY_CHUNKS, len(CHUNKS)))
            dve.wait_ge(chunk_lo.sem, len(CHUNKS))
            unit_max(0, 0, 0)
            with dve.Fori(0, B - 1) as row:
                row_steps(row, False)
            row_steps(B - 1, True)

        @block.tensor
        def _(pe):
            def product(to, w, w_cols, acts, rows, start, stop):
                (wh, wl), (ah, al) = w, acts
                nc.tensor.matmul(to, wl[rows, w_cols], ah[rows], start=start, stop=False)
                nc.tensor.matmul(to, wh[rows, w_cols], al[rows], start=False, stop=False)
                return nc.tensor.matmul(to, wh[rows, w_cols], ah[rows], start=False, stop=stop)

            def normed(w, width, cols, to, tile_ready=None):
                for kt in range(KT):
                    if tile_ready is not None:
                        tile_ready(kt)
                    last = product(to, w, slice(kt * width + cols.start, kt * width + cols.stop),
                                   (n_hi[:, kt, :], n_lo[:, kt, :]), slice(0, P), kt == 0, kt == KT - 1)
                return last

            def mean(norm, row, ahead):
                pe.wait_ge(norm.sum_ready.sem, norm.sum_ready.count(row, 1 if norm is front else 2, ahead))
                nc.tensor.matmul(bank[:, norm.where, :], con("mean"), tile_sum, start=True, stop=True)\
                    .then_inc(norm.mean_ready.sem, 1)

            def mean_squares(norm, row, n, ahead):
                sums = n + 2 if norm is front or n == 1 else 1
                pe.wait_ge(norm.sum_ready.sem, norm.sum_ready.count(row, sums, ahead))
                for j in range(S // P):
                    last = nc.tensor.matmul(bank[:, norm.where, j:j + 1], tile_sum[:, j * P:(j + 1) * P],
                                            con("mean")[:, 0:1], start=True, stop=True)
                last.then_inc(norm.square_mean.sem, 1)

            def spread_rstd(norm, row, n, ahead):
                pe.wait_ge(norm.rstd_ready.sem, norm.rstd_ready.count(row, n + 1, ahead))
                for j in range(S // P):
                    last = nc.tensor.matmul(bank[:, norm.where, j * P:(j + 1) * P],
                                            norm.rstd[:, j:j + 1].broadcast_to([P, P]), con("ident"),
                                            start=True, stop=True)
                last.then_inc(norm.rstd_spread.sem, 1)

            def swap(row, i, ahead):
                pe.wait_ge(qk_copied.sem, qk_copied.count(row, i + 1, ahead))
                if i >= 2:
                    pe.wait_ge(sin_done.sem, sin_done.count(row, i - 1, ahead))
                nc.tensor.matmul(bank[:, 5 + i % 2, :], con("swap"), qk_sb[:, i % 2, :], start=True, stop=True)\
                    .then_inc(swapped.sem, 1)

            def project_qk(row, i, ahead, tile_ready=None):
                first = (i // 2) * P + (i % 2) * D
                if i >= 2:
                    pe.wait_ge(qk_copied.sem, qk_copied.count(row, i - 1, ahead))
                normed(hi_lo("qk"), 2 * D, slice(first, first + P), bank[:, 3 + i % 2, :], tile_ready)\
                    .then_inc(qk_proj.sem, 1)

            def project_v(i):
                wv = hi_lo("v")
                for blk in (2 * i, 2 * i + 1):
                    to = bank[:, 7 if i == 0 else 1, (blk % 2) * D:(blk % 2 + 1) * D]
                    for kt in range(KT):
                        rows = slice(kt * S + blk * P, kt * S + (blk + 1) * P)
                        feats = slice(kt * D, (kt + 1) * D)
                        nh = n_hi[:].rearrange("p t s -> p (t s)")[:, rows]
                        nl = n_lo[:].rearrange("p t s -> p (t s)")[:, rows]
                        nc.tensor.matmul(to, nl, wv[0][:, feats], start=kt == 0, stop=False)
                        nc.tensor.matmul(to, nh, wv[1][:, feats], start=False, stop=False)
                        last = nc.tensor.matmul(to, nh, wv[0][:, feats], start=False, stop=kt == KT - 1)
                last.then_inc(v_proj.sem, 1)

            def front_projections(row, ahead):
                def tile_ready(kt):
                    pe.wait_ge(front.n_lo_ready.sem, front.n_lo_ready.count(row, kt + 1, ahead))

                project_qk(row, 0, ahead, tile_ready)
                project_qk(row, 1, ahead)
                if ahead:
                    mean(rest, row, 0)
                swap(row, 0, ahead)
                project_qk(row, 2, ahead)
                swap(row, 1, ahead)
                if ahead:
                    mean_squares(rest, row, 1, 0)
                project_qk(row, 3, ahead)
                swap(row, 2, ahead)
                if ahead:
                    spread_rstd(rest, row, 1, 0)
                project_v(0)
                swap(row, 3, ahead)
                project_v(1)

            def fill(row, kind, n):
                at = fills.index((kind, n))
                if at >= 3:
                    what, k = fills[at - 3]
                    pe.wait_ge(freed_by[what].sem, freed_by[what].count(row, k + 1))
                return slot((kind, n))

            def masked(to, which):
                nc.tensor.matmul(to, mask[:, 0, :], mask[:, which:which + 1, :].broadcast_to([P, GH, P]),
                                 start=True, stop=which == 2)

            def scores_for_max(row, n, ahead):
                u, a = n // 2, n % 2
                blk, half = u % BLOCKS, u // BLOCKS
                if a == 0:
                    pe.wait_ge(k_spread.sem, k_spread.count(row, u + 1, ahead))
                    if u in (0, BLOCKS):
                        half_stacked(pe, row, half, ahead)
                to = fill(row, "s1", n)
                for g in range(2):
                    masked(to[:, g, :], 1)
                for g in range(2):
                    gq = 2 * a + g
                    last = nc.tensor.matmul(to[:, g, :],
                                            q_st[0:MROW, half * GQ + gq, blk * P:(blk + 1) * P],
                                            k_ex[u % 2][0:MROW, gq, :, :], start=False, stop=True)
                last.then_inc(s1_ready.sem, 1)

            def row_steps(row, is_last):
                def max_transposed(u):
                    pe.wait_ge(max_done.sem, max_done.count(row, 2 * u + 2))
                    to = fill(row, "t", u)
                    for gq in range(GQ):
                        last = nc.tensor.transpose(to[0:KS, 0, gq * P:(gq + 1) * P], neg_max[:, gq, 0:KS], con("ident"))
                    last.then_inc(max_t.sem, 1)

                def shifted_scores(n):
                    u, a = n // 2, n % 2
                    blk, half = u % BLOCKS, u // BLOCKS
                    if a == 0:
                        pe.wait_ge(max_rows.sem, max_rows.count(row, u + 1))
                    to = fill(row, "s2", n)
                    for g in range(2):
                        masked(to[:, g, :], 2)
                    for g in range(2):
                        gq = 2 * a + g
                        for hh in range(GH):
                            last = nc.tensor.matmul(to[:, g, hh * P:(hh + 1) * P], k_ex[u % 2][0:KS, gq, hh, :],
                                                    q_st[0:KS, half * GQ + gq, blk * P:(blk + 1) * P],
                                                    start=False, stop=True, skip_group_check=True)
                    last.then_inc(s2_ready.sem, 1)

                def contexts(n):
                    u, a = n // 2, n % 2
                    if a == 0:
                        pe.wait_ge(v_spread.sem, v_spread.count(row, u + 1))
                        if u:
                            pe.wait_ge(ctx_done.sem, ctx_done.count(row, u))
                        else:
                            pe.wait_ge(out_ready.sem, out_ready.count(row, 0))
                    pe.wait_ge(exp_done.sem, exp_done.count(row, n + 1))
                    for j in range(8):
                        last = nc.tensor.matmul(bank[:, 6, a * P:(a + 1) * P], v_ex[:, 8 * a + j, :],
                                                prob[a][:, j * P:(j + 1) * P], start=j == 0, stop=j == 7)
                    last.then_inc(pv_done.sem, 1)

                max_transposed(0)
                for u in range(UNITS):
                    for a in range(2):
                        shifted_scores(2 * u + a)
                        if u + 1 < UNITS:
                            scores_for_max(row, 2 * u + 2 + a, 0)
                    contexts(2 * u)
                    if u + 1 < UNITS:
                        max_transposed(u + 1)
                    contexts(2 * u + 1)
                    if not is_last:
                        if u == 2:
                            mean(front, row, 1)
                        elif u == 4:
                            mean_squares(front, row, 0, 1)
                        elif u == 5:
                            spread_rstd(front, row, 0, 1)
                        elif u == 7:
                            mean_squares(front, row, 1, 1)
                for kt in range(KT):
                    pe.wait_ge(ctx_done.sem, ctx_done.count(row, (kt + 1) * BLOCKS))
                    for t in range(KT):
                        last = nc.tensor.matmul(bank[:, t, :], plain("o")[:, kt * D + t * P:kt * D + (t + 1) * P],
                                                ctx_n[:, kt, :], start=kt == 0, stop=kt == KT - 1)
                        if kt == KT - 1:
                            last.then_inc(o_proj.sem, 1)
                def mlp_input(kt):
                    pe.wait_ge(rest.n_lo_ready.sem, rest.n_lo_ready.count(row, kt + 1))

                for m in range(MT):
                    if m == 2:
                        pe.wait_ge(x1_ready.sem, x1_ready.count(row, KT))
                    if m == 3:
                        pe.wait_ge(hidden_done.sem, hidden_done.count(row, 1))
                    for part in range(2):
                        last = normed(hi_lo("up"), 2 * INTER, slice(part * INTER + m * P, part * INTER + (m + 1) * P),
                                      bank[:, up_bank(m, part), :], mlp_input if m == part == 0 else None)
                        if m == 1 and part == 0:
                            spread_rstd(rest, row, 0, 0)
                    last.then_inc(up_ready.sem, 1)
                    if m == 0:
                        mean_squares(rest, row, 0, 0)
                if not is_last:
                    spread_rstd(front, row, 1, 1)
                pe.wait_ge(hidden_done.sem, hidden_done.count(row, 3))
                pe.wait_ge(x1_ready.sem, x1_ready.count(row, KT))
                for t in range(KT):
                    for m in range(MT):
                        if t == 0:
                            pe.wait_ge(hidden_done.sem, hidden_done.count(row, m + 1))
                        last = nc.tensor.matmul(bank[:, t, :], plain("down")[:, m * D + t * P:m * D + (t + 1) * P],
                                                hidden[:, m, :], start=m == 0, stop=m == MT - 1)
                    last.then_inc(down_ready.sem, 1)
                if is_last:
                    mean(rest, row, 0)
                    mean_squares(rest, row, 1, 0)
                    spread_rstd(rest, row, 1, 0)
                else:
                    front_projections(row, 1)
                pe.wait_ge(rest.shifted.sem, rest.shifted.count(row, 1))
                for j in range(S // P):
                    for kt in range(KT):
                        last = nc.tensor.matmul(bank[:, 3, j * E:(j + 1) * E], xc[:, kt, j * P:(j + 1) * P],
                                                plain("r")[:, kt * E:(kt + 1) * E], start=kt == 0, stop=kt == KT - 1)
                last.then_inc(route_ready.sem, 1)
                def ffn_input(kt):
                    pe.wait_ge(rest.n_lo_ready.sem, rest.n_lo_ready.count(row, KT + kt + 1))

                normed(hi_lo("ag"), E * R, slice(0, E * R), bank[:, 0, :], ffn_input)
                if not is_last:
                    pe.wait_ge(v_copied.sem, v_copied.count(row, 2, 1))
                    pe.wait_ge(sin_done.sem, sin_done.count(row, 4, 1))
                normed(hi_lo("au"), E * R, slice(0, E * R), bank[:, 1, :]).then_inc(lora_a.sem, 1)

                gate_banks = [(2, 3), (4, 5)]

                def base(m):
                    at, width = FF_TILES[m]
                    if m >= 2:
                        pe.wait_ge(ff_prod.sem, ff_prod.count(row, FF_STEPS.index((m - 2, 2)) + 1))
                    for name, where in zip(("wg", "wu"), gate_banks[m % 2]):
                        last = normed(hi_lo(name), DFF, slice(at, at + width), bank[0:width, where, :])
                    last.then_inc(gu_ready.sem, 1)

                def transposed_picks(kinds):
                    for kind in kinds:
                        pe.wait_ge(spread.sem, spread.count(row, kind + 1))
                        if kind >= 2:
                            pe.wait_ge(pick_copied.sem, pick_copied.count(row, kind - 1))
                        for j in range(S // P):
                            last = nc.tensor.transpose(bank[:, 6 + kind % 2, j * P:(j + 1) * P],
                                                       spread_t[kind][:, j * P:(j + 1) * P], con("ident"))
                        last.then_inc(pick_t.sem, 1)

                pe.wait_ge(l_copied.sem, l_copied.count(row, 1))
                base(0)
                transposed_picks((0, 1))
                base(1)
                transposed_picks((2, 3))

                def lora(m, v):
                    at, width = FF_TILES[m]
                    before = FF_STEPS.index((m, v - 1)) + 1
                    pe.wait_ge(ff_prod.sem, ff_prod.count(row, before))
                    if m == 0:
                        pe.wait_ge(lora_lo.sem, lora_lo.count(row, 2 * v))
                    for i, (name, where) in enumerate(zip(("bg", "bu"), gate_banks[m % 2])):
                        wh, wl = hi_lo(name)
                        ah, al = lora_hl[2 * (v - 1) + i]
                        to = bank[0:width, where, :]
                        cols = slice(at, at + width)
                        nc.tensor.matmul(to, wl[:, cols], ah, start=False, stop=False, skip_group_check=True)
                        nc.tensor.matmul(to, wh[:, cols], al, start=False, stop=False, skip_group_check=True)
                        last = nc.tensor.matmul(to, wh[:, cols], ah, start=False, stop=True, skip_group_check=True)
                    last.then_inc(gu_ready.sem, 1)

                def down(m, v):
                    n = FF_STEPS.index((m, v))
                    rows = slice(0, FF_TILES[m][1])
                    pe.wait_ge(ff_lo.sem, ff_lo.count(row, n + 1))
                    if v == 0:
                        for t in range(KT):
                            last = product(bank[:, 6 + t, :], hi_lo("wd"), slice(m * D + t * P, m * D + (t + 1) * P),
                                           ff_hl[n % 4], rows, m == 0, m == FT - 1)
                    else:
                        last = product(bank[:, v - 1, :], hi_lo("ad"), slice(m * P, (m + 1) * P),
                                       ff_hl[n % 4], rows, m == 0, m == FT - 1)
                        if m == FT - 1:
                            last.then_inc(z_ready.sem, 1)
                            return
                    last.then_inc(ff_used.sem, 1)

                lora(0, 1)
                pe.wait_ge(pick_copied.sem, pick_copied.count(row, 4))
                pe.wait_ge(lora_in.sem, lora_in.count(row, 4))
                down(0, 0)
                lora(0, 2)
                for m in range(1, FT - 1):
                    lora(m, 1)
                    down(m - 1, 1)
                    base(m + 1)
                    down(m - 1, 2)
                    lora(m, 2)
                    down(m, 0)
                lora(FT - 1, 1)
                down(FT - 2, 1)
                down(FT - 2, 2)
                lora(FT - 1, 2)
                down(FT - 1, 0)
                down(FT - 1, 1)
                down(FT - 1, 2)
                if not is_last:
                    scores_for_max(row, 0, 1)
                    scores_for_max(row, 1, 1)
                pe.wait_ge(z_steps.sem, z_steps.count(row, 3))
                for t in range(KT):
                    last = nc.tensor.matmul(bank[:, 6 + t, :], plain("bd")[:, t * P:(t + 1) * P], silu_out[0],
                                            start=False, stop=True, skip_group_check=True)
                last.then_inc(y_ready.sem, 1)

            def modulate(columns, where):
                for c in columns:
                    for kt in range(KT):
                        last = nc.tensor.matmul(mod_ps(where)[:, c, :],
                                                wm[:, kt * 6 * D + c * P:kt * 6 * D + (c + 1) * P],
                                                act_c[:, kt * B:(kt + 1) * B], start=kt == 0, stop=kt == KT - 1)
                last.then_inc(mod_ready.sem, 1)

            pe.wait_ge(const_loaded.sem, 16)
            mean(front, 0, 0)
            mean_squares(front, 0, 0, 0)
            pe.wait_ge(cond_ready.sem, 1)
            pe.wait_ge(wmod_loaded.sem, 16)
            modulate(range(2 * KT), 0)
            spread_rstd(front, 0, 0, 0)
            modulate(range(2 * KT, 6 * KT), 2)
            mean_squares(front, 0, 1, 0)
            spread_rstd(front, 0, 1, 0)
            pe.wait_ge(chunk_lo.sem, 1)
            front_projections(0, 0)
            pe.wait_ge(mask_loaded.sem, 16)
            pe.wait_ge(ones_set.sem, 4)
            pe.wait_ge(v_copied.sem, v_copied.count(0, 2))
            pe.wait_ge(sin_done.sem, sin_done.count(0, 4))
            scores_for_max(0, 0, 0)
            scores_for_max(0, 1, 0)
            pe.wait_ge(plain_loaded.sem, 16)
            pe.wait_ge(chunk_lo.sem, len(CHUNKS))
            with pe.Fori(0, B - 1) as row:
                row_steps(row, False)
            row_steps(B - 1, True)


def _tiles(w):
    n_out, n_in = w.shape
    tiles = -(-n_in // P)
    t = np.zeros((tiles * P, n_out), w.dtype)
    t[:n_in] = w.T
    return t.reshape(tiles, P, n_out).transpose(1, 0, 2).reshape(P, tiles * n_out)


def _columns(v):
    v = v.reshape(-1, KT, P)
    return v.transpose(2, 1, 0).reshape(P, -1)


def _constants():
    inv_freq = (1.0 / np.float32(10000.0) ** (np.arange(0, HD, 2, dtype=np.float32) / np.float32(HD))).astype(np.float32)
    freqs = np.outer(np.arange(S, dtype=np.float32), inv_freq).astype(np.float32)
    angle = np.concatenate([freqs, freqs], -1).astype(np.float64).T
    sign = np.where(np.arange(HD) < HD // 2, -1.0, 1.0)[:, None]
    rows = np.arange(P)
    partner = rows // HD * HD + (rows % HD + HD // 2) % HD
    swap = np.zeros((P, P))
    swap[partner, rows] = 1
    head = np.zeros((P, GH))
    for part in range(PARTS):
        for r in range(32):
            head[32 * part + r, r // HD] = 1
    for i in range(GH):
        head[MROW + i, i] = 1
    before = np.tile((np.arange(E)[None, :] < np.arange(E)[:, None]).reshape(1, -1), (P, 1))
    parts = {"cos": np.tile(np.cos(angle), (P // HD, 1)), "sin": np.tile(np.sin(angle) * sign, (P // HD, 1)),
             "ident": np.eye(P), "mean": np.full((P, P), 1.0 / D), "swap": swap, "head": head, "before": before,
             "one": np.ones((P, 1))}
    return np.concatenate([parts[n] for n, _ in CONST_WIDTHS], 1).astype(np.float32)


def kernel(**inputs):
    import concourse.bacc as bacc
    from concourse.bass_utils import run_bass_kernel_spmd
    import ml_dtypes

    a = {k[3:]: np.asarray(v) for k, v in inputs.items()}
    x = a["attn_x"].transpose(0, 2, 1).reshape(B, KT, P, S).transpose(0, 2, 1, 3)
    qkv = a["attn_w_qkv"]
    split = {"qk": _tiles(qkv[:2 * D]), "v": _tiles(qkv[2 * D:]), "up": _tiles(a["attn_w_up"]),
             "ag": _tiles(a["ffn_Ag"].reshape(E * R, D)), "au": _tiles(a["ffn_Au"].reshape(E * R, D)),
             "wg": _tiles(a["ffn_Wg"]), "wu": _tiles(a["ffn_Wu"]),
             "bg": a["ffn_Bg"].transpose(0, 2, 1).reshape(E * R, DFF),
             "bu": a["ffn_Bu"].transpose(0, 2, 1).reshape(E * R, DFF),
             "wd": _tiles(a["ffn_Wd"]), "ad": _tiles(a["ffn_Ad"].reshape(E * R, DFF))}
    plain = {"o": _tiles(a["attn_w_o"]), "down": _tiles(a["attn_w_down"]),
             "bd": a["ffn_Bd"].transpose(0, 2, 1).reshape(E * R, D), "r": _tiles(a["ffn_Wr"])}
    query, key = np.arange(P)[:, None], np.arange(P)[None, :]
    masks = np.stack([np.eye(P), np.where(key > query, MASKED, 0), np.where(key > query, MASKED, 0).T], 1)
    arrays = {
        "x": x,
        "smalls": np.concatenate([_columns(a["attn_attn_norm_w"]), _columns(a["attn_ffn_norm_w"]),
                                  _columns(a["c"])], 1),
        "wmod": _tiles(a["wmod"].T),
        "wsplit": np.concatenate([split[n] for n, _ in SPLIT_WIDTHS], 1),
        "wplain": np.concatenate([plain[n] for n, _ in PLAIN_WIDTHS], 1),
        "consts": _constants(),
        "masks": masks.astype(ml_dtypes.bfloat16),
    }
    arrays = {k: np.ascontiguousarray(v) for k, v in arrays.items()}
    nc = bacc.Bacc("TRN2", target_bir_lowering=False, num_devices=1)
    args = [nc.dram_tensor(f"in_{k}", v.shape, mybir.dt.from_np(v.dtype), kind="ExternalInput").ap()
            for k, v in arrays.items()]
    out = nc.dram_tensor("out_0", (B, P, KT, S), F32, kind="ExternalOutput").ap()
    adaln_kernel(nc, *args, out)
    r = run_bass_kernel_spmd(nc, [{f"in_{k}": v for k, v in arrays.items()}], core_ids=[0])
    got = r.results[0]["out_0"]
    return got.transpose(0, 2, 1, 3).reshape(B, D, S).transpose(0, 2, 1)
```
